# Optimizing a Trainium2 kernel written in Bass

```python
import numpy as np
import jax
import jax.numpy as jnp

def _softmax(x, axis=-1):
    return jax.nn.softmax(x, axis=axis)

def _gelu(x):
    return jax.nn.gelu(x, approximate=True)

def _silu(x):
    return jax.nn.silu(x)

def _sigmoid(x):
    return jax.nn.sigmoid(x)

def _layernorm(x, axis=-1, eps=1e-05):
    m = jnp.mean(x, axis=axis, keepdims=True)
    v = jnp.var(x, axis=axis, keepdims=True)
    return (x - m) / jnp.sqrt(v + eps)

def _scatter_add(tgt, idx, src, axis=0):
    return tgt.at[idx].add(src)

def _segment_sum(src, seg, n):
    return jax.ops.segment_sum(src, seg, n)
kernel_name = 'mk_macaron_d2_jaxref_r4_c97f71'

def setup_inputs(seed: int=0):
    np.random.seed(seed)
    _w = jnp.asarray

    def _L0_attn_setup():
        import jax, jax.numpy as jnp
        import numpy as np
        N_EMBD = 256
        N_HEAD = 16
        HEAD_DIM = N_EMBD // N_HEAD
        KV_RANK = 64
        Q_RANK = 128
        ROPE_DIM = 32
        B, T = (2, 512)
        EPS = 1e-06

        def _rope_tables(T, dim):
            inv_freq = 1.0 / 10000.0 ** (np.arange(0, dim, 2, dtype=np.float32) / dim)
            t = np.arange(T, dtype=np.float32)
            freqs = np.outer(t, inv_freq)
            emb = np.concatenate([freqs, freqs], -1)
            return (jnp.asarray(np.cos(emb)), jnp.asarray(np.sin(emb)))

        def _apply_rope(x, cos, sin):
            d2 = x.shape[-1] // 2
            x1, x2 = (x[..., :d2], x[..., d2:])
            rot = jnp.concatenate([-x2, x1], axis=-1)
            return x * cos[None, None, :, :] + rot * sin[None, None, :, :]
        key = jax.random.key(seed)
        ks = jax.random.split(key, 10)

        def w(k, fan_in, fan_out):
            return jax.random.normal(k, (fan_in, fan_out), dtype=jnp.float32) * fan_in ** (-0.5)
        return {'x': jax.random.normal(ks[0], (B, T, N_EMBD), dtype=jnp.float32), 'W_kv': w(ks[1], N_EMBD, KV_RANK), 'g_kv': jnp.ones((KV_RANK,), dtype=jnp.float32), 'W_kdec': w(ks[2], KV_RANK, N_HEAD * HEAD_DIM), 'W_vdec': w(ks[3], KV_RANK, N_HEAD * HEAD_DIM), 'W_q': w(ks[4], N_EMBD, Q_RANK), 'W_qdec': w(ks[5], Q_RANK, N_HEAD * HEAD_DIM), 'W_krope': w(ks[6], N_EMBD, N_HEAD * ROPE_DIM), 'W_qrope': w(ks[7], Q_RANK, N_HEAD * ROPE_DIM), 'W_o': w(ks[8], N_HEAD * HEAD_DIM, N_EMBD)}
    _L0_attn_in = _L0_attn_setup()

    def _L0_ffn_setup():
        import jax, jax.numpy as jnp
        import numpy as np
        B, S, DIM = (4, 1024, 256)
        BASE_COUPLING = 0.1
        NUM_CYCLES = 3

        def _gelu(x):
            return jax.nn.gelu(x, approximate=False)

        def _coupling_net(h, w1, b1, w2, b2, w3, b3, w4, b4):
            h = _gelu(h @ w1 + b1)
            h = _gelu(h @ w2 + b2)
            h = _gelu(h @ w3 + b3)
            return jax.nn.sigmoid(h @ w4 + b4)

        def _global_net(h, w1, b1, w2, b2, w3, b3):
            h = _gelu(h @ w1 + b1)
            h = _gelu(h @ w2 + b2)
            return jax.nn.sigmoid(h @ w3 + b3)

        def _twist(x):
            o_r, o_i, p_r, p_i = jnp.split(x, 4, axis=-1)
            return jnp.concatenate([p_r, -p_i, -o_r, o_i], axis=-1)
        key = jax.random.key(seed)
        ks = jax.random.split(key, 9)
        d = DIM

        def w(k, fan_in, fan_out):
            return jax.random.normal(k, (fan_in, fan_out), dtype=jnp.float32) / np.sqrt(fan_in).astype(np.float32)
        inp = {'x': jax.random.normal(ks[0], (B, S, d), dtype=jnp.float32)}
        cn_dims = [(d, d), (d, d // 2), (d // 2, d // 4), (d // 4, 1)]
        for i, (a, b) in enumerate(cn_dims):
            inp[f'cn_w{i + 1}'] = w(ks[1 + i], a, b)
            inp[f'cn_b{i + 1}'] = jnp.zeros((b,), dtype=jnp.float32)
        gc_dims = [(d, d // 2), (d // 2, d // 4), (d // 4, 1)]
        for i, (a, b) in enumerate(gc_dims):
            inp[f'gc_w{i + 1}'] = w(ks[5 + i], a, b)
            inp[f'gc_b{i + 1}'] = jnp.zeros((b,), dtype=jnp.float32)
        inp['adaptive_range'] = jnp.full((1,), 0.2, dtype=jnp.float32)
        return inp
    _L0_ffn_in = _L0_ffn_setup()

    def _L1_attn_setup():
        import jax, jax.numpy as jnp
        import numpy as np
        D_MODEL = 256
        NUM_HEADS = 16
        HEAD_DIM = D_MODEL // NUM_HEADS
        STRIDES = [1, 1, 2, 2, 2, 2, 4, 4, 4, 4, 8, 8, 8, 8, 16, 16]
        LN_EPS = 1e-05

        def layer_norm(x, gamma, beta):
            mu = jnp.mean(x, axis=-1, keepdims=True)
            var = jnp.mean(jnp.square(x - mu), axis=-1, keepdims=True)
            return (x - mu) * jax.lax.rsqrt(var + LN_EPS) * gamma + beta

        def hepos_attention(x, Wqkv, bqkv, Wout, bout):
            B, L, D = x.shape
            qkv = x @ Wqkv + bqkv
            q, k, v = jnp.split(qkv, 3, axis=-1)
            q = q.reshape(B, L, NUM_HEADS, HEAD_DIM).transpose(0, 2, 1, 3)
            k = k.reshape(B, L, NUM_HEADS, HEAD_DIM).transpose(0, 2, 1, 3)
            v = v.reshape(B, L, NUM_HEADS, HEAD_DIM).transpose(0, 2, 1, 3)
            scale = 1.0 / np.sqrt(HEAD_DIM)
            outs = []
            for h, stride in enumerate(STRIDES):
                k_s = k[:, h, ::stride, :]
                v_s = v[:, h, ::stride, :]
                scores = jnp.einsum('bqd,bkd->bqk', q[:, h], k_s) * scale
                attn = jax.nn.softmax(scores, axis=-1)
                outs.append(jnp.einsum('bqk,bkd->bqd', attn, v_s))
            out = jnp.stack(outs, axis=1)
            out = out.transpose(0, 2, 1, 3).reshape(B, L, D)
            return out @ Wout + bout
        key = jax.random.key(seed)
        ks = jax.random.split(key, 12)
        B, L, D = (2, 1024, D_MODEL)
        s = 1.0 / np.sqrt(D)
        inp = {'x': jax.random.normal(ks[0], (B, L, D), dtype=jnp.float32), 'Wqkv': jax.random.normal(ks[1], (D, 3 * D), dtype=jnp.float32) * s, 'bqkv': jnp.zeros((3 * D,), dtype=jnp.float32), 'Wout': jax.random.normal(ks[2], (D, D), dtype=jnp.float32) * s, 'bout': jnp.zeros((D,), dtype=jnp.float32), 'gamma': jnp.ones((D,), dtype=jnp.float32), 'beta': jnp.zeros((D,), dtype=jnp.float32), 'W1': jax.random.normal(ks[3], (D, 4 * D), dtype=jnp.float32) * s, 'b1': jnp.zeros((4 * D,), dtype=jnp.float32), 'W2': jax.random.normal(ks[4], (4 * D, D), dtype=jnp.float32) * (0.5 * s), 'b2': jnp.zeros((D,), dtype=jnp.float32)}
        return inp
    _L1_attn_in = _L1_attn_setup()

    def _L1_ffn_setup():
        import jax, jax.numpy as jnp
        import numpy as np
        D_MODEL = 256
        M = 64
        INNER = 16
        key = jax.random.key(seed)
        ks = jax.random.split(key, 9)

        def init(k, shape, fan_in):
            bound = 1.0 / np.sqrt(fan_in)
            return jax.random.uniform(k, shape, jnp.float32, -bound, bound)
        x = jax.random.normal(ks[0], (16, 1024, D_MODEL), dtype=jnp.float32)
        Win = init(ks[1], (D_MODEL, M), D_MODEL)
        bin_ = init(ks[2], (M,), D_MODEL)
        W1 = init(ks[3], (M, INNER), 1)
        b1 = init(ks[4], (M, INNER), 1)
        W2 = init(ks[5], (M, INNER), INNER)
        b2 = init(ks[6], (M,), INNER)
        Wout = init(ks[7], (M, D_MODEL), M)
        bout = init(ks[8], (D_MODEL,), M)
        return {'x': x, 'Win': Win, 'bin_': bin_, 'W1': W1, 'b1': b1, 'W2': W2, 'b2': b2, 'Wout': Wout, 'bout': bout}
    _L1_ffn_in = _L1_ffn_setup()
    _d = {'L0_attn_x': _L0_attn_in['x'], 'L0_attn_W_kv': _L0_attn_in['W_kv'], 'L0_attn_g_kv': _L0_attn_in['g_kv'], 'L0_attn_W_kdec': _L0_attn_in['W_kdec'], 'L0_attn_W_vdec': _L0_attn_in['W_vdec'], 'L0_attn_W_q': _L0_attn_in['W_q'], 'L0_attn_W_qdec': _L0_attn_in['W_qdec'], 'L0_attn_W_krope': _L0_attn_in['W_krope'], 'L0_attn_W_qrope': _L0_attn_in['W_qrope'], 'L0_attn_W_o': _L0_attn_in['W_o'], 'L0_ffn_cn_w1': _L0_ffn_in['cn_w1'], 'L0_ffn_cn_b1': _L0_ffn_in['cn_b1'], 'L0_ffn_cn_w2': _L0_ffn_in['cn_w2'], 'L0_ffn_cn_b2': _L0_ffn_in['cn_b2'], 'L0_ffn_cn_w3': _L0_ffn_in['cn_w3'], 'L0_ffn_cn_b3': _L0_ffn_in['cn_b3'], 'L0_ffn_cn_w4': _L0_ffn_in['cn_w4'], 'L0_ffn_cn_b4': _L0_ffn_in['cn_b4'], 'L0_ffn_gc_w1': _L0_ffn_in['gc_w1'], 'L0_ffn_gc_b1': _L0_ffn_in['gc_b1'], 'L0_ffn_gc_w2': _L0_ffn_in['gc_w2'], 'L0_ffn_gc_b2': _L0_ffn_in['gc_b2'], 'L0_ffn_gc_w3': _L0_ffn_in['gc_w3'], 'L0_ffn_gc_b3': _L0_ffn_in['gc_b3'], 'L0_ffn_adaptive_range': _L0_ffn_in['adaptive_range'], 'L1_attn_Wqkv': _L1_attn_in['Wqkv'], 'L1_attn_bqkv': _L1_attn_in['bqkv'], 'L1_attn_Wout': _L1_attn_in['Wout'], 'L1_attn_bout': _L1_attn_in['bout'], 'L1_attn_gamma': _L1_attn_in['gamma'], 'L1_attn_beta': _L1_attn_in['beta'], 'L1_attn_W1': _L1_attn_in['W1'], 'L1_attn_b1': _L1_attn_in['b1'], 'L1_attn_W2': _L1_attn_in['W2'], 'L1_attn_b2': _L1_attn_in['b2'], 'L1_ffn_Win': _L1_ffn_in['Win'], 'L1_ffn_bin_': _L1_ffn_in['bin_'], 'L1_ffn_W1': _L1_ffn_in['W1'], 'L1_ffn_b1': _L1_ffn_in['b1'], 'L1_ffn_W2': _L1_ffn_in['W2'], 'L1_ffn_b2': _L1_ffn_in['b2'], 'L1_ffn_Wout': _L1_ffn_in['Wout'], 'L1_ffn_bout': _L1_ffn_in['bout']}
    _x0 = _d['L0_attn_x']
    _d['L0_attn_x'] = jax.random.normal(jax.random.fold_in(jax.random.key(seed), 1), (16, 512, 256), dtype=_x0.dtype)
    del _x0
    return _d

def reference(L0_attn_x, L0_attn_W_kv, L0_attn_g_kv, L0_attn_W_kdec, L0_attn_W_vdec, L0_attn_W_q, L0_attn_W_qdec, L0_attn_W_krope, L0_attn_W_qrope, L0_attn_W_o, L0_ffn_cn_w1, L0_ffn_cn_b1, L0_ffn_cn_w2, L0_ffn_cn_b2, L0_ffn_cn_w3, L0_ffn_cn_b3, L0_ffn_cn_w4, L0_ffn_cn_b4, L0_ffn_gc_w1, L0_ffn_gc_b1, L0_ffn_gc_w2, L0_ffn_gc_b2, L0_ffn_gc_w3, L0_ffn_gc_b3, L0_ffn_adaptive_range, L1_attn_Wqkv, L1_attn_bqkv, L1_attn_Wout, L1_attn_bout, L1_attn_gamma, L1_attn_beta, L1_attn_W1, L1_attn_b1, L1_attn_W2, L1_attn_b2, L1_ffn_Win, L1_ffn_bin_, L1_ffn_W1, L1_ffn_b1, L1_ffn_W2, L1_ffn_b2, L1_ffn_Wout, L1_ffn_bout):

    def _L0_attn_ref(x, W_kv, g_kv, W_kdec, W_vdec, W_q, W_qdec, W_krope, W_qrope, W_o):
        import jax, jax.numpy as jnp
        import numpy as np
        N_EMBD = 256
        N_HEAD = 16
        HEAD_DIM = N_EMBD // N_HEAD
        KV_RANK = 64
        Q_RANK = 128
        ROPE_DIM = 32
        B, T = (2, 512)
        EPS = 1e-06

        def _rope_tables(T, dim):
            inv_freq = 1.0 / 10000.0 ** (np.arange(0, dim, 2, dtype=np.float32) / dim)
            t = np.arange(T, dtype=np.float32)
            freqs = np.outer(t, inv_freq)
            emb = np.concatenate([freqs, freqs], -1)
            return (jnp.asarray(np.cos(emb)), jnp.asarray(np.sin(emb)))

        def _apply_rope(x, cos, sin):
            d2 = x.shape[-1] // 2
            x1, x2 = (x[..., :d2], x[..., d2:])
            rot = jnp.concatenate([-x2, x1], axis=-1)
            return x * cos[None, None, :, :] + rot * sin[None, None, :, :]
        Bx, Tx, C = x.shape
        kv_c = x @ W_kv
        kv_c = kv_c * jax.lax.rsqrt(jnp.mean(kv_c * kv_c, axis=-1, keepdims=True) + EPS) * g_kv
        q_c = x @ W_q

        def heads(y, d):
            return y.reshape(Bx, Tx, N_HEAD, d).transpose(0, 2, 1, 3)
        k_content = heads(kv_c @ W_kdec, HEAD_DIM)
        v = heads(kv_c @ W_vdec, HEAD_DIM)
        q_content = heads(q_c @ W_qdec, HEAD_DIM)
        k_rope = heads(x @ W_krope, ROPE_DIM)
        q_rope = heads(q_c @ W_qrope, ROPE_DIM)
        cos, sin = _rope_tables(Tx, ROPE_DIM)
        q_rope = _apply_rope(q_rope, cos, sin)
        k_rope = _apply_rope(k_rope, cos, sin)
        q = jnp.concatenate([q_content, q_rope], axis=-1)
        k = jnp.concatenate([k_content, k_rope], axis=-1)
        scale = 1.0 / jnp.sqrt(jnp.float32(q.shape[-1]))
        scores = jnp.einsum('bhqd,bhkd->bhqk', q, k) * scale
        causal = jnp.tril(jnp.ones((Tx, Tx), dtype=bool))
        scores = jnp.where(causal[None, None], scores, jnp.float32(-jnp.inf))
        attn = jax.nn.softmax(scores, axis=-1)
        out = jnp.einsum('bhqk,bhkd->bhqd', attn, v)
        out = out.transpose(0, 2, 1, 3).reshape(Bx, Tx, N_HEAD * HEAD_DIM)
        return out @ W_o

    def _L0_ffn_ref(x, cn_w1, cn_b1, cn_w2, cn_b2, cn_w3, cn_b3, cn_w4, cn_b4, gc_w1, gc_b1, gc_w2, gc_b2, gc_w3, gc_b3, adaptive_range):
        import jax, jax.numpy as jnp
        import numpy as np
        B, S, DIM = (4, 1024, 256)
        BASE_COUPLING = 0.1
        NUM_CYCLES = 3

        def _gelu(x):
            return jax.nn.gelu(x, approximate=False)

        def _coupling_net(h, w1, b1, w2, b2, w3, b3, w4, b4):
            h = _gelu(h @ w1 + b1)
            h = _gelu(h @ w2 + b2)
            h = _gelu(h @ w3 + b3)
            return jax.nn.sigmoid(h @ w4 + b4)

        def _global_net(h, w1, b1, w2, b2, w3, b3):
            h = _gelu(h @ w1 + b1)
            h = _gelu(h @ w2 + b2)
            return jax.nn.sigmoid(h @ w3 + b3)

        def _twist(x):
            o_r, o_i, p_r, p_i = jnp.split(x, 4, axis=-1)
            return jnp.concatenate([p_r, -p_i, -o_r, o_i], axis=-1)
        global_context = x.mean(axis=1, keepdims=True)
        gf = _global_net(global_context, gc_w1, gc_b1, gc_w2, gc_b2, gc_w3, gc_b3)
        out = x
        for _ in range(NUM_CYCLES):
            tf = _coupling_net(out, cn_w1, cn_b1, cn_w2, cn_b2, cn_w3, cn_b3, cn_w4, cn_b4)
            combined = 0.7 * gf + 0.3 * tf
            coupling = BASE_COUPLING + adaptive_range * (combined - 0.5) * 2.0
            out = out + coupling * _twist(out)
        return out

    def _L1_attn_ref(x, Wqkv, bqkv, Wout, bout, gamma, beta, W1, b1, W2, b2):
        import jax, jax.numpy as jnp
        import numpy as np
        D_MODEL = 256
        NUM_HEADS = 16
        HEAD_DIM = D_MODEL // NUM_HEADS
        STRIDES = [1, 1, 2, 2, 2, 2, 4, 4, 4, 4, 8, 8, 8, 8, 16, 16]
        LN_EPS = 1e-05

        def layer_norm(x, gamma, beta):
            mu = jnp.mean(x, axis=-1, keepdims=True)
            var = jnp.mean(jnp.square(x - mu), axis=-1, keepdims=True)
            return (x - mu) * jax.lax.rsqrt(var + LN_EPS) * gamma + beta

        def hepos_attention(x, Wqkv, bqkv, Wout, bout):
            B, L, D = x.shape
            qkv = x @ Wqkv + bqkv
            q, k, v = jnp.split(qkv, 3, axis=-1)
            q = q.reshape(B, L, NUM_HEADS, HEAD_DIM).transpose(0, 2, 1, 3)
            k = k.reshape(B, L, NUM_HEADS, HEAD_DIM).transpose(0, 2, 1, 3)
            v = v.reshape(B, L, NUM_HEADS, HEAD_DIM).transpose(0, 2, 1, 3)
            scale = 1.0 / np.sqrt(HEAD_DIM)
            outs = []
            for h, stride in enumerate(STRIDES):
                k_s = k[:, h, ::stride, :]
                v_s = v[:, h, ::stride, :]
                scores = jnp.einsum('bqd,bkd->bqk', q[:, h], k_s) * scale
                attn = jax.nn.softmax(scores, axis=-1)
                outs.append(jnp.einsum('bqk,bkd->bqd', attn, v_s))
            out = jnp.stack(outs, axis=1)
            out = out.transpose(0, 2, 1, 3).reshape(B, L, D)
            return out @ Wout + bout
        attn_out = hepos_attention(x, Wqkv, bqkv, Wout, bout)
        h = layer_norm(x + attn_out, gamma, beta)
        ffn = jax.nn.relu(h @ W1 + b1) @ W2 + b2
        return layer_norm(h + ffn, gamma, beta)

    def _L1_ffn_ref(x, Win, bin_, W1, b1, W2, b2, Wout, bout):
        import jax, jax.numpy as jnp
        import numpy as np
        D_MODEL = 256
        M = 64
        INNER = 16
        s = jnp.einsum('btd,dm->btm', x, Win) + bin_
        h = jax.nn.relu(s[..., None] * W1 + b1)
        g = jnp.einsum('btmh,mh->btm', h, W2) + b2
        out = jnp.einsum('btm,md->btd', g, Wout) + bout
        return out
    x = L0_attn_x
    x = x + 0.5 * _L0_ffn_ref(_layernorm(x, axis=-1), L0_ffn_cn_w1, L0_ffn_cn_b1, L0_ffn_cn_w2, L0_ffn_cn_b2, L0_ffn_cn_w3, L0_ffn_cn_b3, L0_ffn_cn_w4, L0_ffn_cn_b4, L0_ffn_gc_w1, L0_ffn_gc_b1, L0_ffn_gc_w2, L0_ffn_gc_b2, L0_ffn_gc_w3, L0_ffn_gc_b3, L0_ffn_adaptive_range)
    x = x + _L0_attn_ref(_layernorm(x, axis=-1), L0_attn_W_kv, L0_attn_g_kv, L0_attn_W_kdec, L0_attn_W_vdec, L0_attn_W_q, L0_attn_W_qdec, L0_attn_W_krope, L0_attn_W_qrope, L0_attn_W_o)
    x = x + 0.5 * _L0_ffn_ref(_layernorm(x, axis=-1), L0_ffn_cn_w1, L0_ffn_cn_b1, L0_ffn_cn_w2, L0_ffn_cn_b2, L0_ffn_cn_w3, L0_ffn_cn_b3, L0_ffn_cn_w4, L0_ffn_cn_b4, L0_ffn_gc_w1, L0_ffn_gc_b1, L0_ffn_gc_w2, L0_ffn_gc_b2, L0_ffn_gc_w3, L0_ffn_gc_b3, L0_ffn_adaptive_range)
    x = x + 0.5 * _L1_ffn_ref(_layernorm(x, axis=-1), L1_ffn_Win, L1_ffn_bin_, L1_ffn_W1, L1_ffn_b1, L1_ffn_W2, L1_ffn_b2, L1_ffn_Wout, L1_ffn_bout)
    x = x + _L1_attn_ref(_layernorm(x, axis=-1), L1_attn_Wqkv, L1_attn_bqkv, L1_attn_Wout, L1_attn_bout, L1_attn_gamma, L1_attn_beta, L1_attn_W1, L1_attn_b1, L1_attn_W2, L1_attn_b2)
    x = x + 0.5 * _L1_ffn_ref(_layernorm(x, axis=-1), L1_ffn_Win, L1_ffn_bin_, L1_ffn_W1, L1_ffn_b1, L1_ffn_W2, L1_ffn_b2, L1_ffn_Wout, L1_ffn_bout)
    return x

_drawn_inputs = setup_inputs


def setup_inputs(seed=0):
    import zlib

    import numpy as np

    out = dict(_drawn_inputs(seed))
    spreads = {'L0_attn_g_kv': (1.0, 0.2),
     'L0_ffn_cn_b1': (0.0, 2.0),
     'L0_ffn_cn_b2': (0.0, 2.0),
     'L0_ffn_cn_b3': (0.0, 2.0),
     'L0_ffn_gc_b1': (0.0, 0.8),
     'L0_ffn_gc_b2': (0.0, 0.8),
     'L1_attn_bqkv': (0.0, 0.1),
     'L1_attn_bout': (0.0, 0.1),
     'L1_attn_gamma': (1.0, 0.2),
     'L1_attn_beta': (0.0, 0.1),
     'L1_attn_b1': (0.0, 0.401),
     'L1_attn_b2': (0.0, 0.291)}
    factors = {'L0_ffn_cn_w1': 6.361,
     'L0_ffn_cn_w2': 6.635,
     'L0_ffn_cn_w3': 5.309,
     'L0_ffn_cn_w4': 6.03,
     'L0_ffn_gc_w1': 8.0,
     'L0_ffn_gc_w2': 8.0,
     'L0_ffn_gc_w3': 5.124,
     'L1_ffn_bin_': 33.045}
    for name, (base, spread) in spreads.items():
        noise = np.random.default_rng([zlib.crc32(name.encode()), seed]).standard_normal(out[name].shape)
        drawn = base * np.exp(spread * noise) if base else spread * noise
        out[name] = jnp.asarray(drawn.astype(out[name].dtype))
    for name, factor in factors.items():
        out[name] = (out[name] * factor).astype(out[name].dtype)
    return out
```

```python
from contextlib import ExitStack

import numpy as np

import concourse.bass as bass
from concourse import mybir

F32 = mybir.dt.float32
F32R = mybir.dt.float32r
BF16 = mybir.dt.bfloat16
ALU = mybir.AluOpType
ACT = mybir.ActivationFunctionType
AX_X = mybir.AxisListType.X

P = 128
CH = 2
CYCLES = 3
HEADS, HD, RD = 16, 16, 32
GROUPS = HEADS // 4
STRIDES = [1, 1, 2, 2, 2, 2, 4, 4, 4, 4, 8, 8, 8, 8, 16, 16]
LN_EPS = 1e-5
RMS_EPS = 1e-6
MASKED = -1.0e30
STAGES = "ABCDEF"


def attention_shapes(stage, T):
    keys = [T] * HEADS if stage == "B" else [T // s for s in STRIDES]
    tiles = [-(-k // P) for k in keys]
    first = [sum(tiles[:h]) for h in range(HEADS)]
    return keys, tiles, first


def max_jobs(stage, g, T):
    keys, _, _ = attention_shapes(stage, T)
    jobs = []
    if stage == "B":
        for t in range(T // P):
            n = P * (t + 1)
            m = min(4, 512 // n)
            m = 1 if m == 3 else m
            jobs += [([t], list(range(j, j + m)), n) for j in range(0, 4, m)]
        return jobs
    for pair in (0, 2):
        n = keys[4 * g + pair]
        if n == 512:
            jobs += [([t], [j], n) for t in range(T // P) for j in (pair, pair + 1)]
        else:
            m = min(T // P, 512 // (2 * n))
            jobs += [(list(range(t, t + m)), [pair, pair + 1], n) for t in range(0, T // P, m)]
    return jobs


def attention_steps(stage, T):
    _, tiles, _ = attention_shapes(stage, T)
    steps = []
    if stage == "B":
        steps += [("rope", 0), ("rope", 1)]
    steps += [("stack", 0), ("stack", 1)]
    steps += [("max", 0, n) for n in range(len(max_jobs(stage, 0, T)))] + [("shift", 0)]
    for g in range(GROUPS):
        exps = [(kt, pair) for kt in range(4) for pair in (0, 1) if kt < tiles[4 * g + 2 * pair]]
        depth = max(kt for kt, _ in exps) + 1
        ahead = [("max", g + 1, n) for n in range(len(max_jobs(stage, g + 1, T)))] if g + 1 < GROUPS else []
        per = -(-len(ahead) // len(exps)) if ahead else 0
        if g:
            steps.append(("divide", g - 1))
        for n, (kt, pair) in enumerate(exps):
            steps.append(("exp", g, kt, pair))
            steps += ahead[per * n:per * (n + 1)]
            if n and exps[n - 1][0] != kt:
                steps.append(("sum", g, kt - 1))
        if g + 1 < GROUPS:
            steps.append(("shift", g + 1))
        if stage == "B" and g + 2 < GROUPS:
            steps.append(("rope", g + 2))
        steps.append(("sum", g, depth - 1))
        if g + 2 < GROUPS:
            steps.append(("stack", g + 2))
    steps.append(("divide", GROUPS - 1))
    return steps


def build(nc, ins, out):
    x_in = ins["L0_attn_x"]
    B, T, C = x_in.shape
    TT, KT = T // P, C // P
    assert T == 512 and C == 256 and B % CH == 0
    TURNS = B // CH
    x_v = x_in.rearrange("(i c) (t p) d -> i c p t d", c=CH, p=P)
    o_v = out.rearrange("(i c) (t p) d -> i c p t d", c=CH, p=P)
    _, e_tiles, e_first = attention_shapes("E", T)
    E_SLOTS = sum(e_tiles)
    SCALE = {"B": float(1.0 / np.sqrt(np.float32(HD + RD))), "E": 1.0 / np.sqrt(HD)}
    STEPS = {s: attention_steps(s, T) for s in "BE"}
    KCOPY, width = {}, 0
    for x in range(2):
        for s in sorted({STRIDES[h] for h in range(8 * x, 8 * x + 8)}):
            KCOPY[x, s] = width
            width += T // s
    KWIDE = width

    ctx = ExitStack()
    with ctx:
        def sb(name, shape, dt=F32):
            return ctx.enter_context(nc.sbuf_tensor(name, shape, dt))

        def sem(name):
            return ctx.enter_context(nc.semaphore(name))

        cn_w1 = sb("cn_w1", [P, 2, 256])
        cn_w2 = sb("cn_w2", [P, 2, 128])
        cn_w3 = sb("cn_w3", [P, 128])
        cn_w4 = sb("cn_w4", [P, 128])
        gc_w1 = sb("gc_w1", [P, 2, 128])
        gc_w2 = sb("gc_w2", [P, 128])
        gc_w3 = sb("gc_w3", [P, 128])
        cols = sb("cols", [P, 96])
        w_kv = sb("w_kv", [P, 2, 64])
        w_kdec = sb("w_kdec", [P, 256])
        w_vdec = sb("w_vdec", [P, 256])
        w_q = sb("w_q", [P, 2, 128])
        w_qdec = sb("w_qdec", [P, 256])
        w_qrope = sb("w_qrope", [P, 512])
        w_qturn = sb("w_qturn", [P, 512])
        w_krope = sb("w_krope", [P, 2, 512])
        w_kturn = sb("w_kturn", [P, 2, 512])
        w_o = sb("w_o", [P, 2, 256])
        rope_cos = sb("rope_cos", [P, T])
        rope_sin = sb("rope_sin", [P, T])
        ident = sb("ident", [P, P])
        ident_b = sb("ident_b", [P, P], BF16)
        mask_q = sb("mask_q", [P, P], BF16)
        mask_k = sb("mask_k", [P, P], BF16)
        w_qkv = sb("w_qkv", [P, 2, 768])
        w_out = sb("w_out", [P, 2, 256])
        w_up = sb("w_up", [P, 2, 1024])
        w_down = sb("w_down", [P, 8, 256])
        rows = sb("rows", [P, 5, 256])
        bout_e, gamma_r, beta_r, betab2_r, bout_d = (rows[:, n, :] for n in range(5))
        m_in = sb("m_in", [P, 2, 128])
        m_out = sb("m_out", [P, 256])

        used = [0]

        def col(n=1):
            a = used[0]
            used[0] += n
            return cols[:, a:a + n]

        c_b1, c_b2, c_b3, c_b4 = col(2), col(), col(), col()
        c_g1, c_g2, c_g3 = col(), col(), col()
        c_half4, c_half3 = col(), col()
        c_w4, c_gw3, c_range, c_sign = col(), col(), col(), col()
        c_tf, c_gf, c_base = col(), col(), col()
        c_gkv = col()
        c_qkvb = col(6)
        c_gamma, c_beta, c_ub = col(2), col(2), col(8)
        c_bin = col()
        c_mw1, c_mb1, c_mw2, c_mprod = col(8), col(8), col(8), col(8)
        c_mb2, c_mbias = col(), col()
        neg_half = sb("neg_half", [P, 4])

        X = sb("X", [P, CH, TT, C])
        XN = sb("XN", [P, CH, TT, C])
        XT = sb("XT", [P, CH, KT, T])
        stats = sb("stats", [P, CH, TT, 6])
        mv = sb("mv", [P, CH, TT, 2])
        var = sb("var", [P, CH, TT])
        rstd = sb("rstd", [P, CH, TT])
        scratch = sb("scratch", [P, 8192])
        H1 = scratch[:, 0:2048].rearrange("p (c m n) -> p c m n", c=CH, m=2)
        H2 = scratch[:, 2048:3072].rearrange("p (c n) -> p c n", c=CH)
        H3 = scratch[:, 3072:4096].rearrange("p (c n) -> p c n", c=CH)
        TF = scratch[:, 4096:5120].rearrange("p (c n) -> p c n", c=CH)
        MV = scratch[:, 5120:7168].rearrange("p (c m n) -> p c m n", c=CH, m=2)
        S = scratch[:, 0:1024].rearrange("p (c n) -> p c n", c=CH)
        R = scratch[:, 1024:5120].rearrange("p (j n) -> p j n", j=8)
        G = scratch[:, 5120:6144].rearrange("p (c n) -> p c n", c=CH)
        split = scratch
        QR = split[:, 0:2048].rearrange("p (r s n) -> p r s n", r=2, s=2)
        KR = split[:, 2048:4096].rearrange("p (r s n) -> p r s n", r=2, s=2)
        QC = split[:, 4096:5120].rearrange("p (s n) -> p s n", s=2)
        KC = split[:, 5120:6144].rearrange("p (s n) -> p s n", s=2)
        AO = scratch[:, 6144:6656]
        NM = scratch[:, 6656:7168]
        ATN = scratch[:, 7168:8192].rearrange("p (t d) -> p t d", t=TT)
        QE = split[:, 0:2048].rearrange("p (x s n) -> p x s n", x=2, s=2)
        KE = split[:, 2048:2048 + 2 * KWIDE].rearrange("p (s n) -> p s n", s=2)
        SQ = sb("SQ", [P, 2, 4, T], F32R)
        SK1 = sb("SK1", [P, 2, 4, T], F32R)
        SK2 = sb("SK2", [P, 2, 4, T], F32R)
        SKE = sb("SKE", [P, E_SLOTS * P], F32R)
        SHIFT = 96
        VB = sb("VB", [P, TT, HEADS, HD + 1])
        VE = sb("VE", [P, E_SLOTS, HD + 1])
        PR = sb("PR", [P, 2, 4, T])
        U = PR[:, :, :, :].rearrange("p a j n -> p (a j) n")
        MX = sb("MX", [P, TT, P])
        rden = sb("rden", [P, 4, 4])
        ATT = sb("ATT", [P, KT, T])
        QL = ATT[:, 0, :]
        KVT = ATT[:, 1, :]
        HB = scratch[:, 6144:8192].rearrange("p (c t d) -> p c t d", c=CH, t=TT)
        means = sb("means", [P, CH, KT])
        gc_h = sb("gc_h", [P, CH, 4])

        ps = ctx.enter_context(nc.psum_tensor("ps", [P, 8, 512], F32))

        loaded, const_pool, const_dve, const_act = sem("loaded"), sem("const_pool"), sem("const_dve"), sem("const_act")
        cleared = sem("x_loaded")
        x_loaded = cleared
        full = [sem(f"bank_full{b}") for b in range(8)]
        free = [sem(f"bank_free{b}") for b in range(8)]

        class Signal:

            def __init__(self, name, events):
                self.sem, self.events = sem(name), list(events)

            def at(self, *event):
                return self.events.index(event if len(event) > 1 else event[0]) + 1

        seqs = range(CH)
        norms = [(s, c) for s in ("A", "B") for c in seqs] + [("KV", c) for c in seqs] + \
                [(s, c) for s in ("C", "D", "E", "E2", "E3", "F") for c in seqs]
        var_ready = Signal("var_ready", norms)
        rstd_ready = Signal("rstd_ready", norms)
        xn_ready = Signal("xn_ready", norms)
        cycles = [(s, k, c) for s in "AC" for k in range(CYCLES) for c in seqs]
        coupling_ready = Signal("coupling_ready", cycles)
        moved_pool = Signal("moved_pool", cycles)
        first_moved = Signal("first_moved", cycles)
        second_moved = Signal("second_moved", cycles)
        hi_ready = Signal("hi_ready", [(s, c, w, x) for s in "BE" for c in seqs for x in range(2) for w in "kq"])
        ropes = [(c, st[1], w) for c in seqs for st in STEPS["B"] if st[0] == "rope" for w in "kq"]
        rope_sum, rope_hi, rope_lo = (Signal(n, ropes) for n in ("rope_sum", "rope_hi", "rope_lo"))
        groups = [(s, c, g) for s in "BE" for c in seqs for g in range(GROUPS)]
        stacked = [sem(f"stacked{r}") for r in range(2)]
        stack_count, total = {}, [0, 0]
        for s, c, g in groups:
            total[g % 2] += 16 * 4 * (10 if s == "B" else 6)
            stack_count[s, c, g] = total[g % 2]
        shift_in = sem("shift_in")
        sums = [(s, c, *st[1:]) for s in "BE" for c in seqs for st in STEPS[s] if st[0] == "sum"]

        def depth(s, g):
            return max(attention_shapes(s, T)[1][4 * g:4 * g + 4])

        def last_exp(s, g):
            return [st[2:] for st in STEPS[s] if st[0] == "exp" and st[1] == g][-1]

        def rounded(ap):
            return ap.bitcast(F32R)

        sum_done = Signal("sum_done", [e for e in sums if e[3] < depth(e[0], e[2]) - 1])
        biased = Signal("biased", [(s, c) for s in ("D", "E", "HB", "E3", "F") for c in seqs])
        g_ready = Signal("g_ready", [(s, c) for s in "DF" for c in seqs])
        dve_step, pool_step = sem("dve_step"), sem("pool_step")
        x_stored = sem("x_stored")
        last_sem = x_stored
        V_PARTS = [(st, [h for h in range(HEADS) if STRIDES[h] == st], min(P, T // st)) for st in (1, 2, 4, 8, 16)]

        def over_partitions(vec, n):
            return vec.partition_broadcast(P) if n is None else vec.partition_broadcast(n)

        setup = ExitStack()
        with nc.Block() as block:
            loads = []

            def two_tiles(name, dst):
                loads.append((dst, ins[name].rearrange("(k p) n -> p k n", p=P)))

            def column(name, dst, m=None):
                v = ins[name]
                loads.append((dst, v.rearrange("(m p) -> p m", m=m)))

            two_tiles("L0_ffn_cn_w1", cn_w1[:])
            two_tiles("L0_ffn_cn_w2", cn_w2[:])
            two_tiles("L0_ffn_gc_w1", gc_w1[:])
            for h in range(2):
                loads.append((cn_w3[:, 64 * h:64 * h + 64], ins["L0_ffn_cn_w3"]))
                loads.append((gc_w2[:, 64 * h:64 * h + 64], ins["L0_ffn_gc_w2"]))
                loads.append((c_b3[64 * h:64 * h + 64, :], ins["L0_ffn_cn_b3"].rearrange("(p m) -> p m", m=1)))
                loads.append((c_g2[64 * h:64 * h + 64, :], ins["L0_ffn_gc_b2"].rearrange("(p m) -> p m", m=1)))
                loads.append((c_bin[64 * h:64 * h + 64, :], ins["L1_ffn_bin_"].rearrange("(p m) -> p m", m=1)))
                loads.append((c_mw1[64 * h:64 * h + 64, :], ins["L1_ffn_W1"][:, 8 * h:8 * h + 8]))
                loads.append((c_mb1[64 * h:64 * h + 64, :], ins["L1_ffn_b1"][:, 8 * h:8 * h + 8]))
                loads.append((c_mw2[64 * h:64 * h + 64, :], ins["L1_ffn_W2"][:, 8 * h:8 * h + 8]))
                loads.append((m_in[:, :, 64 * h:64 * h + 64], ins["L1_ffn_Win"].rearrange("(k p) n -> p k n", p=P)))
                loads.append((m_out[64 * h:64 * h + 64, :], ins["L1_ffn_Wout"]))
            loads.append((c_mb2[0:64, :], ins["L1_ffn_b2"].rearrange("(p m) -> p m", m=1)))
            loads.append((c_w4[0:64, :], ins["L0_ffn_cn_w4"]))
            loads.append((c_gw3[0:64, :], ins["L0_ffn_gc_w3"]))
            loads.append((c_gkv[0:64, :], ins["L0_attn_g_kv"].rearrange("(p m) -> p m", m=1)))
            column("L0_ffn_cn_b1", c_b1, 2)
            column("L0_ffn_cn_b2", c_b2, 1)
            column("L0_ffn_gc_b1", c_g1, 1)
            column("L1_attn_bqkv", c_qkvb, 6)
            column("L1_attn_gamma", c_gamma, 2)
            column("L1_attn_beta", c_beta, 2)
            column("L1_attn_b1", c_ub, 8)
            loads.append((c_b4, ins["L0_ffn_cn_b4"].partition_broadcast(P)))
            loads.append((c_g3, ins["L0_ffn_gc_b3"].partition_broadcast(P)))
            loads.append((c_range, ins["L0_ffn_adaptive_range"].partition_broadcast(P)))
            two_tiles("L0_attn_W_kv", w_kv[:])
            loads.append((w_kdec[0:64, :], ins["L0_attn_W_kdec"]))
            loads.append((w_vdec[0:64, :], ins["L0_attn_W_vdec"]))
            two_tiles("L0_attn_W_q", w_q[:])
            loads.append((w_qdec[:], ins["L0_attn_W_qdec"]))
            loads.append((w_qrope[:], ins["L0_attn_W_qrope"]))
            two_tiles("L0_attn_W_krope", w_krope[:])
            two_tiles("L0_attn_W_o", w_o[:])
            loads.append((rope_cos[:], ins["rope_cos"]))
            loads.append((rope_sin[:], ins["rope_sin"]))
            two_tiles("L1_attn_Wqkv", w_qkv[:])
            two_tiles("L1_attn_Wout", w_out[:])
            two_tiles("L1_attn_W1", w_up[:])
            loads.append((w_down[:], ins["L1_attn_W2"].rearrange("(k p) n -> p k n", p=P)))
            loads.append((bout_e, ins["L1_attn_bout"].partition_broadcast(P)))
            loads.append((gamma_r, ins["L1_attn_gamma"].partition_broadcast(P)))
            loads.append((beta_r, ins["L1_attn_beta"].partition_broadcast(P)))
            loads.append((betab2_r, ins["L1_attn_b2"].partition_broadcast(P)))
            loads.append((bout_d, ins["L1_ffn_bout"].partition_broadcast(P)))
            ALL_LOADS = 16 * len(loads)

            @block.sync
            def _(sp):
                for dst, src in loads:
                    sp.dma_start(dst, src, allow_slow_non_contiguous=True).then_inc(loaded, 16)
                sp.wait_ge(loaded, ALL_LOADS)

            @block.gpsimd
            def _(pool):
                for m in (ident, ident_b, mask_q, mask_k):
                    pool.memset(m[:], 0.0).then_inc(const_pool, 1)
                pool.memset(neg_half[:], -0.5).then_inc(const_pool, 1)
                pool.wait_ge(const_pool, 5)
                for m in (ident, ident_b):
                    pool.affine_select(out=m[:], in_=m[:], compare_op=ALU.not_equal, fill=1.0, base=0,
                                       pattern=[[-1, P]], channel_multiplier=1).then_inc(const_pool, 1)
                pool.affine_select(out=mask_q[:], in_=mask_q[:], compare_op=ALU.is_ge, fill=MASKED, base=0,
                                   pattern=[[-1, P]], channel_multiplier=1).then_inc(const_pool, 1)
                pool.affine_select(out=mask_k[:], in_=mask_k[:], compare_op=ALU.is_ge, fill=MASKED, base=0,
                                   pattern=[[1, P]], channel_multiplier=-1).then_inc(const_pool, 1)
                pool.memset(VB[:], 1.0).then_inc(const_pool, 1)
                pool.memset(VE[:], 1.0).then_inc(const_pool, 1)
                pool.memset(MX[:], 0.0).then_inc(const_pool, 1)
                pool.memset(ATT[:], 0.0).then_inc(const_pool, 1)
                pool.wait_ge(const_pool, 13)
                for h in range(HEADS):
                    n = T // STRIDES[h]
                    if n < P and STRIDES[h] != STRIDES[h - 1]:
                        heads = STRIDES.count(STRIDES[h])
                        for q in range(n, P, 32):
                            pool.memset(VE[q:q + 32, e_first[h]:e_first[h] + heads, :], 0.0).then_inc(const_pool, 1)

            @block.vector
            def _(dve):
                n = 0

                def then(ins_):
                    ins_.then_inc(const_dve, 1)
                    nonlocal n
                    n += 1

                for m in (SQ, SK1, SK2):
                    then(dve.memset(m[:].bitcast(F32), 0.0))
                then(dve.memset(SKE[:].bitcast(F32), 0.0))
                then(dve.memset(cn_w4[64:P, :], 0.0))
                then(dve.memset(gc_w3[64:P, :], 0.0))
                then(dve.memset(w_kdec[64:P, :], 0.0))
                then(dve.memset(w_vdec[64:P, :], 0.0))
                then(dve.memset(c_sign[0:64, :], 1.0))
                then(dve.memset(c_sign[64:P, :], -1.0))
                then(dve.memset(c_mb2[64:P, :], 0.0))
                then(dve.memset(cn_w4[0:64, :], 1.0))
                then(dve.memset(gc_w3[0:64, :], 1.0))
                then(dve.memset(ps[:, 6:8, :], 0.0))
                dve.wait_ge(const_dve, n)
                then(dve.memset(SK1[SHIFT:SHIFT + 1, :, :, :].bitcast(F32), 1.0))
                for h in range(HEADS):
                    a = e_first[h] * P
                    then(dve.memset(SKE[SHIFT:SHIFT + 1, a:a + T // STRIDES[h]].bitcast(F32), 1.0))
                dve.wait_ge(loaded, ALL_LOADS)
                then(dve.tensor_scalar(cn_w4[0:64, :], cn_w4[0:64, :], c_w4[0:64, :], None, ALU.mult))
                then(dve.tensor_scalar(gc_w3[0:64, :], gc_w3[0:64, :], c_gw3[0:64, :], None, ALU.mult))
                then(dve.tensor_scalar(c_half4, c_b4, 0.5, None, ALU.mult))
                then(dve.tensor_scalar(c_half3, c_g3, 0.5, None, ALU.mult))
                then(dve.tensor_scalar(c_tf, c_sign, c_range, 0.3, ALU.mult, ALU.mult))
                then(dve.tensor_scalar(c_gf, c_sign, c_range, 0.7, ALU.mult, ALU.mult))
                then(dve.tensor_scalar(c_base, c_sign, 0.1, None, ALU.mult))
                then(dve.tensor_scalar(w_kdec[0:64, :], w_kdec[0:64, :], c_gkv[0:64, :], None, ALU.mult))
                then(dve.tensor_scalar(w_vdec[0:64, :], w_vdec[0:64, :], c_gkv[0:64, :], None, ALU.mult))
                for w, turn in ((w_qrope[:], w_qturn[:]), (w_krope[:, 0, :], w_kturn[:, 0, :]),
                                (w_krope[:, 1, :], w_kturn[:, 1, :])):
                    a = w.rearrange("p (h s d) -> p h s d", s=2, d=RD // 2)
                    b = turn.rearrange("p (h s d) -> p h s d", s=2, d=RD // 2)
                    for s in range(2):
                        then(dve.tensor_copy(b[:, :, s, :], a[:, :, 1 - s, :]))
                then(dve.tensor_tensor(betab2_r, betab2_r, beta_r, ALU.add))
                then(dve.tensor_scalar(bout_d, bout_d, 0.5, None, ALU.mult))
                then(dve.tensor_scalar(m_out[:], m_out[:], 0.5, None, ALU.mult))
                then(dve.tensor_tensor(c_mprod, c_mw2, c_mb1, ALU.mult))
                dve.wait_ge(const_dve, n)
                then(dve.tensor_reduce(c_mbias, c_mprod, AX_X, ALU.add))
                then(dve.tensor_scalar(c_mb1, c_mb1, -1.0, None, ALU.mult))
                dve.wait_ge(const_dve, n)
                then(dve.tensor_tensor(c_mbias, c_mbias, c_mb2, ALU.add))

        J = {}

        def when_full(eng, *key):
            b, n = J[key]
            eng.wait_ge(full[b], n)
            return ps[:, b, :]

        def read_out(eng, *key):
            b, n = J[key]
            eng.wait_ge(free[b], n)

        def freed(ins_, *key):
            ins_.then_inc(free[J[key][0]], 1)

        with nc.Fori(0, TURNS) as turn:
          with nc.Block() as block:

            @block.tensor
            def _(pe):
                count, last_job = [0] * 8, [None] * 8

                def take(bank, *key, width=1):
                    for b in range(bank, bank + width):
                        if last_job[b] is not None and last_job[b] not in [last_job[x] for x in range(bank, b)]:
                            pe.wait_ge(free[last_job[b][0]], last_job[b][1])
                    count[bank] += 1
                    J[key] = (bank, count[bank])
                    for b in range(bank, bank + width):
                        last_job[b] = J[key]
                    return ps[:, bank, :] if width == 1 else ps[:, bank:bank + width, :]

                def mm(dst, lhsT, rhs, start=True, stop=True):
                    return pe.matmul(dst, lhsT, rhs, start=start, stop=stop, skip_group_check=True)

                def transposed(s, c, banks):
                    pe.wait_ge(xn_ready.sem, xn_ready.at(s, c))
                    for f in range(KT):
                        dst = take(banks[f], "xt", s, c, f)
                        for t in range(TT):
                            last = pe.transpose(dst[:, t * P:(t + 1) * P], XN[:, c, t, f * P:(f + 1) * P], ident[:])
                        last.then_inc(full[banks[f]], 1)

                def in_xt(s, c):
                    for f in range(KT):
                        read_out(pe, "xt", s, c, f)

                def product(bank, key, pairs, rows=P, cols_=T):
                    dst = take(bank, *key)
                    for n, (lhsT, rhs) in enumerate(pairs):
                        last = mm(dst[0:rows, 0:cols_], lhsT, rhs, n == 0, n == len(pairs) - 1)
                    last.then_inc(full[bank], 1)

                def coupled(s):
                    for c in seqs:
                        transposed(s, c, (4 * c + 2, 4 * c + 3))
                    for k in range(CYCLES):
                        for c in seqs:
                            if k == 0:
                                in_xt(s, c)
                            else:
                                pe.wait_ge(first_moved.sem, first_moved.at(s, k - 1, c))
                                pe.wait_ge(second_moved.sem, second_moved.at(s, k - 1, c))
                            for m in range(2):
                                product(4 * c + m, ("h1", s, k, c, m),
                                        [(cn_w1[:, f, m * P:(m + 1) * P], XT[:, c, f, :]) for f in range(KT)])
                            if k == 0:
                                product(4 * c + 3, ("gc", s, 0, c),
                                        [(gc_w1[:, f, :], means[:, c, f:f + 1]) for f in range(KT)], cols_=1)
                        for c in seqs:
                            if k == 0:
                                read_out(pe, "gc", s, 0, c)
                                product(4 * c + 3, ("gc", s, 1, c), [(gc_w2[:], gc_h[:, c, 0:1])], cols_=1)
                            for m in range(2):
                                read_out(pe, "h1", s, k, c, m)
                            product(4 * c + 2, ("h2", s, k, c), [(cn_w2[:, f, :], H1[:, c, f, :]) for f in range(KT)])
                        for c in seqs:
                            if k == 0:
                                read_out(pe, "gc", s, 1, c)
                                product(4 * c + 3, ("gc", s, 2, c), [(gc_w3[:], gc_h[:, c, 1:2])], cols_=1)
                            read_out(pe, "h2", s, k, c)
                            product(4 * c, ("h3", s, k, c), [(cn_w3[:], H2[:, c, :])])
                        for c in seqs:
                            read_out(pe, "h3", s, k, c)
                            product(4 * c + 1, ("tf", s, k, c), [(cn_w4[:], H3[:, c, :])])
                    for c in seqs:
                        pe.wait_ge(first_moved.sem, first_moved.at(s, CYCLES - 1, c))
                        pe.wait_ge(second_moved.sem, second_moved.at(s, CYCLES - 1, c))
                        for b in range(2):
                            dst = take(4 * c + 2 + b, "back", s, c, b)
                            for n in range(4):
                                t, f = 2 * b + n // 2, n % 2
                                last = pe.transpose(dst[:, n * P:(n + 1) * P], XT[:, c, f, t * P:(t + 1) * P], ident[:])
                            last.then_inc(full[4 * c + 2 + b], 1)

                def attention(s, c):
                    keys, tiles, first = attention_shapes(s, T)
                    ring = [0]

                    def side():
                        ring[0] ^= 1
                        return ring[0]

                    def causal(dst, mask, stop=True):
                        return mm(dst, ident_b[:], mask[:], False, stop)

                    for st in STEPS[s]:
                        g = st[1]
                        r = g % 2
                        if st[0] == "rope":
                            if r == 0:
                                a = slice(g // 2 * P, (g // 2 + 1) * P)
                                product(side(), ("hi", s, c, "k", g // 2), [(w_kdec[:, a], KVT)])
                                product(side(), ("hi", s, c, "q", g // 2), [(w_qdec[:, a], QL)])
                            for w, (w_r, w_t) in (("k", (w_krope, w_kturn)), ("q", (w_qrope, w_qturn))):
                                for part, wt in (("straight", w_r), ("turned", w_t)):
                                    a = slice(g * P, (g + 1) * P)
                                    pairs = [(wt[:, a], QL)] if w == "q" else \
                                            [(wt[:, f, a], XT[:, c, f, :]) for f in range(KT)]
                                    product(side(), ("rope", c, g, w, part), pairs)
                        elif st[0] == "max":
                            ts, hs, nk = max_jobs(s, g, T)[st[2]]
                            if st[2] == 0:
                                pe.wait_ge(stacked[r], stack_count[s, c, g])
                            b = side()
                            dst = take(b, *((s, c) + st))
                            at = 0
                            for t in ts:
                                for j in hs:
                                    h = 4 * g + j
                                    k1 = SK1[0:SHIFT, r, j, 0:nk] if s == "B" else \
                                        SKE[0:SHIFT, first[h] * P:first[h] * P + nk]
                                    last = mm(dst[:, at:at + nk], SQ[0:SHIFT, r, j, t * P:(t + 1) * P], k1,
                                              True, s == "E")
                                    if s == "B":
                                        last = causal(dst[:, at + t * P:at + nk], mask_q)
                                    at += nk
                            last.then_inc(full[b], 1)
                        elif st[0] == "shift":
                            read_out(pe, s, c, "max", g, len(max_jobs(s, g, T)) - 1)
                            b = side()
                            dst = take(b, s, c, "shift", g)
                            for t in range(TT):
                                last = pe.transpose(dst[:, t * P:(t + 1) * P], MX[:, t, :], ident[:])
                            last.then_inc(full[b], 1)
                        elif st[0] == "exp":
                            _, _, kt, pair = st
                            if (kt, pair) == (0, 0):
                                pe.wait_ge(shift_in, 16 * (groups.index((s, c, g)) + 1))
                            q0 = kt * P if s == "B" else 0
                            b = 2 + 2 * pair
                            both = take(b, s, c, "exp", g, kt, pair, width=2)
                            for n in range(2):
                                j = 2 * pair + n
                                h = 4 * g + j
                                dst = both[:, n, 0:T - q0]
                                q = SQ[0:SHIFT + 1, r, j, q0:T]
                                if s == "B":
                                    mm(dst, SK1[0:SHIFT + 1, r, j, kt * P:(kt + 1) * P], q, True, False)
                                    mm(dst, SK2[0:SHIFT + 1, r, j, kt * P:(kt + 1) * P], q, False, False)
                                    last = causal(dst[:, 0:P], mask_k)
                                else:
                                    a = (first[h] + kt) * P
                                    last = mm(dst, SKE[0:SHIFT + 1, a:a + P], q)
                            last.then_inc(full[b], 1)
                        elif st[0] == "sum":
                            _, _, kt = st
                            for pair in (0, 1):
                                if kt < tiles[4 * g + 2 * pair]:
                                    read_out(pe, s, c, "exp", g, kt, pair)
                            if (g, kt) == (0, 0):
                                for b in range(2 if s == "B" else 1):
                                    read_out(pe, "v", s, c, b)
                            b = 6 + r
                            dst = take(b, s, c, "sum", g) if kt == 0 else ps[:, b, :]
                            q0 = kt * P if s == "B" else 0
                            for j in range(4):
                                h = 4 * g + j
                                if kt < tiles[h]:
                                    v = VB[:, kt, h, :] if s == "B" else VE[:, first[h] + kt, :]
                                    last = mm(dst[32 * j:32 * j + HD + 1, q0:T], v, PR[:, kt % 2, j, q0:T],
                                              kt == 0, kt == tiles[h] - 1)
                            if kt == max(tiles[4 * g:4 * g + 4]) - 1:
                                last.then_inc(full[b], 1)
                            else:
                                last.then_inc(sum_done.sem, 1)
                        elif st[0] == "divide":
                            read_out(pe, s, c, "sum", g)
                            b = side()
                            dst = take(b, s, c, "divide", g)
                            for t in range(TT):
                                last = pe.transpose(dst[:, t * P:(t + 1) * P], AO[:, t * P:(t + 1) * P], ident[:])
                            last.then_inc(full[b], 1)
                    read_out(pe, s, c, "divide", GROUPS - 1)
                    for f in range(KT):
                        dst = take(2 + f, s, c, "att", f)
                        for t in range(TT):
                            last = pe.transpose(dst[:, t * P:(t + 1) * P], ATN[:, t, f * P:(f + 1) * P], ident[:])
                        last.then_inc(full[2 + f], 1)
                    for f in range(KT):
                        read_out(pe, s, c, "att", f)
                    w = w_o if s == "B" else w_out
                    for b in range(2):
                        dst = take(4 + b, s, c, "proj", b)
                        for n in range(2):
                            t = 2 * b + n
                            for f in range(KT):
                                last = mm(dst[:, n * C:(n + 1) * C], ATT[:, f, t * P:(t + 1) * P], w[:, f, :],
                                          f == 0, f == KT - 1)
                        last.then_inc(full[4 + b], 1)

                def latent(c):
                    in_xt("B", c)
                    dst = take(0, "kv", c)
                    for t in range(TT):
                        for f in range(KT):
                            last = mm(dst[:, 64 * t:64 * t + 64], XT[:, c, f, t * P:(t + 1) * P], w_kv[:, f, :],
                                      f == 0, f == KT - 1)
                    last.then_inc(full[0], 1)
                    product(1, ("ql", c), [(w_q[:, f, :], XT[:, c, f, :]) for f in range(KT)])
                    pe.wait_ge(xn_ready.sem, xn_ready.at("KV", c))
                    dst = take(2, "kvt", c)
                    for t in range(TT):
                        last = pe.transpose(dst[0:64, t * P:(t + 1) * P], XN[:, c, 2, 64 * t:64 * t + 64], ident[:])
                    last.then_inc(full[2], 1)
                    read_out(pe, "kvt", c)
                    read_out(pe, "ql", c)
                    for b in range(2):
                        dst = take(2 + b, "v", "B", c, b)
                        for n in range(2):
                            t = 2 * b + n
                            last = mm(dst[:, n * C:(n + 1) * C], KVT[:, t * P:(t + 1) * P], w_vdec[:])
                        last.then_inc(full[2 + b], 1)

                def qkv(c):
                    in_xt("E", c)
                    for x in range(2):
                        for n, w in enumerate("kq"):
                            a = (256 if w == "k" else 0) + x * P
                            product(4 + 2 * n + x, ("hi", "E", c, w, x),
                                    [(w_qkv[:, f, a:a + P], XT[:, c, f, :]) for f in range(KT)])
                    dst = take(2, "v", "E", c, 0)
                    at = 0
                    for st, heads, m in V_PARTS:
                        for t in range(e_tiles[heads[0]]):
                            for f in range(KT):
                                tok = XT[:, c, f, t * P * st:t * P * st + m * st:st]
                                last = mm(dst[0:m, at:at + HD * len(heads)], tok,
                                          w_qkv[:, f, 512 + HD * heads[0]:512 + HD * (heads[-1] + 1)],
                                          f == 0, f == KT - 1)
                            at += HD * len(heads)
                    last.then_inc(full[2], 1)

                def per_feature(s):
                    for c in seqs:
                        transposed(s, c, (0, 1))
                        in_xt(s, c)
                        product(2 + c, ("s", s, c), [(m_in[:, f, :], XT[:, c, f, :]) for f in range(KT)])
                    for c in seqs:
                        pe.wait_ge(g_ready.sem, g_ready.at(s, c))
                        for b in range(2):
                            dst = take(4 + 2 * c + b, "mout", s, c, b)
                            for n in range(2):
                                t = 2 * b + n
                                last = mm(dst[:, n * C:(n + 1) * C], G[:, c, t * P:(t + 1) * P], m_out[:])
                            last.then_inc(full[4 + 2 * c + b], 1)

                def feed_forward(c):
                    transposed("E2", c, (0, 1))
                    in_xt("E2", c)
                    for m in range(8):
                        product(2 + m % 4, ("up", c, m), [(w_up[:, f, m * P:(m + 1) * P], XT[:, c, f, :]) for f in range(KT)])
                    for b in range(2):
                        dst = take(6 + b, "down", c, b)
                        for n in range(2):
                            t = 2 * b + n
                            for m in range(8):
                                read_out(pe, "up", c, m)
                                last = mm(dst[:, n * C:(n + 1) * C], U[:, m, t * P:(t + 1) * P], w_down[:, m, :],
                                          m == 0, m == 7)
                        last.then_inc(full[6 + b], 1)

                coupled("A")
                for c in seqs:
                    transposed("B", c, (0, 1))
                for c in seqs:
                    latent(c)
                    attention("B", c)
                coupled("C")
                per_feature("D")
                for c in seqs:
                    transposed("E", c, (0, 1))
                for c in seqs:
                    qkv(c)
                    attention("E", c)
                for c in seqs:
                    feed_forward(c)
                per_feature("F")

            @block.vector
            def _(dve):
                steps = [0]

                def link(ins_):
                    ins_.then_inc(dve_step, 1)
                    steps[0] += 1
                    dve.wait_ge(dve_step, steps[0])

                def statistics(s, c, src, *after):
                    for key in after:
                        read_out(dve, *key)
                    for t in range(TT):
                        last = dve.bn_stats(stats[:, c, t, :], src[:, t, :])
                    link(last)
                    for t in range(TT):
                        last = dve.bn_aggr(mv[:, c, t, :], stats[:, c, t, :])
                    link(last)
                    dve.tensor_scalar(var[:, c, :], mv[:, c, :, 1], LN_EPS, None, ALU.add).then_inc(var_ready.sem, 1)

                def normalize(s, c, src, dst):
                    dve.wait_ge(rstd_ready.sem, rstd_ready.at(s, c))
                    for t in range(TT):
                        last = dve.tensor_scalar(dst[:, t, :], src[:, t, :], mv[:, c, t, 0:1], rstd[:, c, t:t + 1],
                                                 ALU.subtract, ALU.mult)
                    last.then_inc(xn_ready.sem, 1)

                def both_norms(s, after):
                    for c in seqs:
                        statistics(s, c, X[:, c], *after(c))
                    for c in seqs:
                        normalize(s, c, X[:, c], XN[:, c])

                def coupled(s, after):
                    both_norms(s, after)
                    for k in range(CYCLES):
                        for c in seqs:
                            if k == 0:
                                read_out(dve, "gc", s, 2, c)
                                link(dve.tensor_scalar(gc_h[:, c, 3:4], gc_h[:, c, 2:3], c_gf, c_base, ALU.mult, ALU.add))
                            read_out(dve, "tf", s, k, c)
                            dve.tensor_scalar(TF[:, c, :], TF[:, c, :], c_tf, gc_h[:, c, 3:4],
                                              ALU.mult, ALU.add).then_inc(coupling_ready.sem, 1)
                            dve.wait_ge(coupling_ready.sem, coupling_ready.at(s, k, c))
                            link(dve.tensor_tensor(MV[:, c, 0, :], TF[:, c, :], XT[:, c, 1, :], ALU.mult))
                            dve.wait_ge(moved_pool.sem, moved_pool.at(s, k, c))
                            dve.tensor_tensor(XT[:, c, 0, :], XT[:, c, 0, :], MV[:, c, 0, :],
                                              ALU.add).then_inc(first_moved.sem, 1)
                    for c in seqs:
                        for b in range(2):
                            src = when_full(dve, "back", s, c, b)
                            x = X[:, c, 2 * b:2 * b + 2, :]
                            last = dve.scalar_tensor_tensor(x, src.rearrange("p (t d) -> p t d", t=2), 0.5, x,
                                                            ALU.mult, ALU.add)
                            freed(last, "back", s, c, b)

                def latent(c):
                    read_out(dve, "kv", c)
                    kv = XN[:, c, 0, :]
                    sq = XN[:, c, 1, :]
                    link(dve.tensor_tensor(sq, kv, kv, ALU.mult))
                    link(dve.tensor_reduce(var[:, c, :], sq.rearrange("p (t d) -> p t d", t=TT), AX_X, ALU.add))
                    dve.tensor_scalar(var[:, c, :], var[:, c, :], 1.0 / 64, RMS_EPS, ALU.mult,
                                      ALU.add).then_inc(var_ready.sem, 1)
                    dve.wait_ge(rstd_ready.sem, rstd_ready.at("KV", c))
                    for t in range(TT):
                        last = dve.tensor_scalar(XN[:, c, 2, 64 * t:64 * t + 64], kv[:, 64 * t:64 * t + 64], rstd[:, c, t:t + 1], None,
                                                 ALU.mult)
                    last.then_inc(xn_ready.sem, 1)
                    dve.wait_ge(xn_ready.sem, xn_ready.at("KV", c))

                def qkv(c):
                    for x in range(2):
                        for w, n in (("k", 2), ("q", 0)):
                            src = when_full(dve, "hi", "E", c, w, x)
                            dve.wait_ge(hi_ready.sem, hi_ready.at("E", c, w, x))
                            parts = [(src, QE[:, x, 0, :], QE[:, x, 1, :])] if w == "q" else \
                                    [(src[:, 0:T:st], KE[:, 0, a:a + T // st], KE[:, 1, a:a + T // st])
                                     for (xx, st), a in KCOPY.items() if xx == x]
                            for p, hi, lo in parts:
                                last = dve.scalar_tensor_tensor(rounded(lo), p, c_qkvb[:, n + x:n + x + 1], hi,
                                                                ALU.add, ALU.subtract)
                            freed(last, "hi", "E", c, w, x)

                def attention(s, c):
                    for st in STEPS[s]:
                        g = st[1]
                        r = g % 2
                        if st[0] == "rope":
                            if r == 0:
                                for w, dst in (("k", KC), ("q", QC)):
                                    src = when_full(dve, "hi", s, c, w, g // 2)
                                    dve.wait_ge(hi_ready.sem, hi_ready.at(s, c, w, g // 2))
                                    freed(dve.tensor_tensor(rounded(dst[:, 1, :]), src, dst[:, 0, :], ALU.subtract),
                                          "hi", s, c, w, g // 2)
                            for n, (w, dst) in enumerate((("k", KR), ("q", QR))):
                                a, b = (XN[:, n].rearrange("p (v u) d -> p v (u d)", v=2)[:, v, :] for v in range(2))
                                if ropes.index((c, g, w)) >= 2:
                                    dve.wait_ge(rope_lo.sem, rope_lo.at(*ropes[ropes.index((c, g, w)) - 2]))
                                src = when_full(dve, "rope", c, g, w, "straight")
                                freed(dve.tensor_tensor(a, src, rope_cos[:], ALU.mult), "rope", c, g, w, "straight")
                                src = when_full(dve, "rope", c, g, w, "turned")
                                freed(dve.tensor_tensor(b, src, rope_sin[:], ALU.mult), "rope", c, g, w, "turned")
                            for n, (w, dst) in enumerate((("k", KR), ("q", QR))):
                                a = XN[:, n].rearrange("p (v u) d -> p v (u d)", v=2)[:, 0, :]
                                if g >= 2:
                                    dve.wait_ge(stacked[r], stack_count[s, c, g - 2])
                                dve.wait_ge(rope_sum.sem, rope_sum.at(c, g, w))
                                dve.tensor_copy(rounded(dst[:, r, 0, :]), a).then_inc(rope_hi.sem, 1)
                        elif st[0] == "max":
                            ts, hs, nk = max_jobs(s, g, T)[st[2]]
                            src = when_full(dve, *((s, c) + st))
                            src = src[:, 0:len(ts) * len(hs) * nk].rearrange("p (t h k) -> p t h k", t=len(ts), h=len(hs))
                            dst = MX[:, ts[0]:ts[-1] + 1, 32 * hs[0]:32 * hs[-1] + 1:32]
                            if st[2] == 0 and groups.index((s, c, g)):
                                e = groups[groups.index((s, c, g)) - 1]
                                when_full(dve, e[0], e[1], "shift", e[2])
                            last = dve.tensor_reduce(dst, src, AX_X, ALU.max)
                            freed(last, *((s, c) + st))
                        elif st[0] == "divide":
                            src = when_full(dve, s, c, "divide", g).rearrange("p (t j e) -> p t j e", t=TT, j=4)
                            link(dve.reciprocal(rden[:], src[:, :, :, HD]))
                            dst = ATN[:, :, g * 64:(g + 1) * 64].rearrange("p t (j e) -> p t j e", j=4)
                            freed(dve.tensor_tensor(dst, src[:, :, :, 0:HD],
                                                    rden[:].unsqueeze(3).broadcast_to([P, TT, 4, HD]), ALU.mult),
                                  s, c, "divide", g)
                            read_out(dve, s, c, "divide", g)
                    if s == "E":
                        dve.wait_ge(biased.sem, biased.at("E", c))
                    for b in range(2):
                        src = when_full(dve, s, c, "proj", b).rearrange("p (t d) -> p t d", t=2)
                        acc = (X if s == "B" else XN)[:, c, 2 * b:2 * b + 2, :]
                        last = dve.tensor_tensor(acc, src, acc, ALU.add)
                        freed(last, s, c, "proj", b)

                def per_feature(s, after):
                    both_norms(s, after)
                    for c in seqs:
                        read_out(dve, "s", s, c)
                        for j in range(8):
                            last = dve.tensor_scalar(R[:, j, :], S[:, c, :], c_mw1[:, j:j + 1], c_mb1[:, j:j + 1],
                                                     ALU.mult, ALU.max)
                        link(last)
                        link(dve.tensor_scalar(G[:, c, :], R[:, 0, :], c_mw2[:, 0:1], c_mbias, ALU.mult, ALU.add))
                        for j in range(1, 8):
                            last = dve.scalar_tensor_tensor(G[:, c, :], R[:, j, :], c_mw2[:, j:j + 1], G[:, c, :],
                                                            ALU.mult, ALU.add)
                            if j < 7:
                                link(last)
                        last.then_inc(g_ready.sem, 1)
                        dve.wait_ge(g_ready.sem, g_ready.at(s, c))
                    for c in seqs:
                        dve.wait_ge(biased.sem, biased.at(s, c))
                        for b in range(2):
                            src = when_full(dve, "mout", s, c, b).rearrange("p (t d) -> p t d", t=2)
                            x = X[:, c, 2 * b:2 * b + 2, :]
                            last = dve.tensor_tensor(x, src, x, ALU.add)
                            freed(last, "mout", s, c, b)

                def outs(name, *rest):
                    return lambda c: [(name, *rest, c, b) for b in range(2)]

                dve.wait_ge(x_loaded, 16 * CH)
                coupled("A", lambda c: [])
                both_norms("B", outs("back", "A"))
                for c in seqs:
                    latent(c)
                    attention("B", c)
                coupled("C", lambda c: [("B", c, "proj", b) for b in range(2)])
                per_feature("D", outs("back", "C"))
                both_norms("E", outs("mout", "D"))
                for c in seqs:
                    qkv(c)
                    attention("E", c)
                for c in seqs:
                    statistics("E2", c, XN[:, c], *[("E", c, "proj", b) for b in range(2)])
                for c in seqs:
                    normalize("E2", c, XN[:, c], XN[:, c])
                for c in seqs:
                    dve.wait_ge(biased.sem, biased.at("HB", c))
                    for b in range(2):
                        src = when_full(dve, "down", c, b).rearrange("p (t d) -> p t d", t=2)
                        acc = HB[:, c, 2 * b:2 * b + 2, :]
                        freed(dve.tensor_tensor(acc, src, acc, ALU.add), "down", c, b)
                    statistics("E3", c, HB[:, c], *[("down", c, b) for b in range(2)])
                for c in seqs:
                    normalize("E3", c, HB[:, c], HB[:, c])
                for c in seqs:
                    dve.wait_ge(biased.sem, biased.at("E3", c))
                    link(dve.tensor_tensor(X[:, c], X[:, c], HB[:, c], ALU.add))
                per_feature("F", lambda c: [])

            @block.scalar
            def _(act):
                def copied(s, c, gc=False):
                    for f in range(KT):
                        src = when_full(act, "xt", s, c, f)
                        if gc:
                            last = act.activation(XT[:, c, f, :], src, ACT.Copy, accum_out=means[:, c, f:f + 1])
                        elif s == "E2":
                            last = act.activation(XT[:, c, f, :], src, ACT.Identity, scale=c_gamma[:, f:f + 1],
                                                  bias=c_beta[:, f:f + 1])
                        else:
                            last = act.activation(XT[:, c, f, :], src, ACT.Copy)
                        freed(last, "xt", s, c, f)

                def coupled(s):
                    for c in seqs:
                        copied(s, c, gc=True)
                    for k in range(CYCLES):
                        for c in seqs:
                            for m in range(2):
                                src = when_full(act, "h1", s, k, c, m)
                                freed(act.activation(H1[:, c, m, :], src, ACT.Gelu, bias=c_b1[:, m:m + 1]),
                                      "h1", s, k, c, m)
                            if k == 0:
                                src = when_full(act, "gc", s, 0, c)
                                freed(act.activation(gc_h[:, c, 0:1], src[:, 0:1], ACT.Gelu, bias=c_g1, scale=1.0 / T),
                                      "gc", s, 0, c)
                        for c in seqs:
                            if k == 0:
                                src = when_full(act, "gc", s, 1, c)
                                freed(act.activation(gc_h[:, c, 1:2], src[:, 0:1], ACT.Gelu, bias=c_g2), "gc", s, 1, c)
                            src = when_full(act, "h2", s, k, c)
                            freed(act.activation(H2[:, c, :], src, ACT.Gelu, bias=c_b2), "h2", s, k, c)
                        for c in seqs:
                            if k == 0:
                                src = when_full(act, "gc", s, 2, c)
                                freed(act.activation(gc_h[:, c, 2:3], src[:, 0:1], ACT.Tanh, bias=c_half3, scale=0.5),
                                      "gc", s, 2, c)
                            src = when_full(act, "h3", s, k, c)
                            freed(act.activation(H3[:, c, :], src, ACT.Gelu, bias=c_b3), "h3", s, k, c)
                        for c in seqs:
                            src = when_full(act, "tf", s, k, c)
                            freed(act.activation(TF[:, c, :], src, ACT.Tanh, bias=c_half4, scale=0.5), "tf", s, k, c)

                def latent(c):
                    src = when_full(act, "kv", c)
                    freed(act.activation(XN[:, c, 0, :], src[:, 0:256], ACT.Copy), "kv", c)
                    src = when_full(act, "ql", c)
                    freed(act.activation(QL, src, ACT.Copy), "ql", c)
                    src = when_full(act, "kvt", c)
                    freed(act.activation(KVT[0:64, :], src[0:64, :], ACT.Copy), "kvt", c)
                    for b in range(2):
                        src = when_full(act, "v", "B", c, b).rearrange("p (t h d) -> p t h d", t=2, d=HD)
                        freed(act.activation(VB[:, 2 * b:2 * b + 2, :, 0:HD], src, ACT.Copy), "v", "B", c, b)

                def qkv(c):
                    for x in range(2):
                        for w, n in (("k", 2), ("q", 0)):
                            src = when_full(act, "hi", "E", c, w, x)
                            parts = [(src, QE[:, x, 0, :])] if w == "q" else \
                                    [(src[:, 0:T:st], KE[:, 0, a:a + T // st]) for (xx, st), a in KCOPY.items() if xx == x]
                            for p, hi in parts:
                                last = act.activation(rounded(hi), p, ACT.Identity, bias=c_qkvb[:, n + x:n + x + 1])
                            last.then_inc(hi_ready.sem, 1)
                    src = when_full(act, "v", "E", c, 0)
                    at = 0
                    for st, heads, m in V_PARTS:
                        n, t = len(heads), e_tiles[heads[0]]
                        f0 = e_first[heads[0]]
                        dst = VE[0:m, f0:f0 + n * t, 0:HD].rearrange("p (h t) d -> p t h d", t=t)
                        a = src[0:m, at:at + n * t * HD].rearrange("p (t h d) -> p t h d", t=t, d=HD)
                        last = act.activation(dst, a, ACT.Copy)
                        at += n * t * HD
                    freed(last, "v", "E", c, 0)

                def attention(s, c):
                    _, tiles, _ = attention_shapes(s, T)
                    for st in STEPS[s]:
                        g = st[1]
                        if st[0] == "rope" and g % 2 == 0:
                            if g:
                                act.wait_ge(stacked[1], stack_count[s, c, g - 1])
                                act.wait_ge(stacked[0], stack_count[s, c, g - 2])
                            for w, dst in (("k", KC), ("q", QC)):
                                src = when_full(act, "hi", s, c, w, g // 2)
                                act.activation(rounded(dst[:, 0, :]), src, ACT.Copy).then_inc(hi_ready.sem, 1)
                        elif st[0] == "shift":
                            src = when_full(act, s, c, "shift", g)
                            n = groups.index((s, c, g))
                            if n:
                                act.wait_ge(shift_in, 16 * n)
                            freed(act.activation(rounded(NM), src, ACT.Copy, scale=-1.0), s, c, "shift", g)
                        elif st[0] == "exp":
                            _, _, kt, pair = st
                            when_full(act, s, c, "exp", g, kt, pair)
                            q0 = kt * P if s == "B" else 0
                            b = 2 + 2 * pair
                            last_use(s, c, g, kt)
                            freed(act.activation(PR[:, kt % 2, 2 * pair:2 * pair + 2, q0:T], ps[:, b:b + 2, 0:T - q0],
                                                 ACT.Exp, scale=SCALE[s]), s, c, "exp", g, kt, pair)
                        elif st[0] == "sum" and st[2] == depth(s, g) - 1:
                            src = when_full(act, s, c, "sum", g)
                            n = groups.index((s, c, g))
                            if n:
                                e = groups[n - 1]
                                when_full(act, e[0], e[1], "divide", e[2])
                            freed(act.activation(AO, src, ACT.Copy), s, c, "sum", g)
                    for f in range(KT):
                        src = when_full(act, s, c, "att", f)
                        if s == "B":
                            last = act.activation(ATT[:, f, :], src, ACT.Copy)
                        else:
                            last = act.activation(ATT[:, f, :], src, ACT.Identity, bias=c_qkvb[:, 4 + f:5 + f])
                        freed(last, s, c, "att", f)

                def last_use(s, c, g, kt):
                    before = [e for e in sums[:sums.index((s, c, g, kt))] if e[3] % 2 == kt % 2]
                    if before:
                        e = before[-1]
                        if e in sum_done.events:
                            act.wait_ge(sum_done.sem, sum_done.at(*e))
                        else:
                            when_full(act, e[0], e[1], "sum", e[2])

                def per_feature(s):
                    for c in seqs:
                        copied(s, c)
                        src = when_full(act, "s", s, c)
                        freed(act.activation(S[:, c, :], src, ACT.Identity, bias=c_bin), "s", s, c)

                coupled("A")
                for c in seqs:
                    copied("B", c)
                for c in seqs:
                    latent(c)
                    attention("B", c)
                coupled("C")
                per_feature("D")
                for c in seqs:
                    copied("E", c)
                for c in seqs:
                    qkv(c)
                    attention("E", c)
                for c in seqs:
                    copied("E2", c)
                    for m in range(8):
                        src = when_full(act, "up", c, m)
                        if c:
                            when_full(act, "down", c - 1, 1)
                        freed(act.activation(U[:, m, :], src, ACT.Relu, bias=c_ub[:, m:m + 1]), "up", c, m)
                per_feature("F")

            @block.gpsimd
            def _(pool):
                def power(s, c):
                    pool.wait_ge(var_ready.sem, var_ready.at(s, c))
                    pool.tensor_tensor(rstd[:, c, :], var[:, c, :], neg_half[:], ALU.pow).then_inc(rstd_ready.sem, 1)

                def bcast(v):
                    return v.unsqueeze(1).broadcast_to([P, TT, C])

                psteps = [0]

                def link(ins_):
                    ins_.then_inc(pool_step, 1)
                    psteps[0] += 1
                    pool.wait_ge(pool_step, psteps[0])

                def coupled(s):
                    for c in seqs:
                        power(s, c)
                    for k in range(CYCLES):
                        for c in seqs:
                            pool.wait_ge(coupling_ready.sem, coupling_ready.at(s, k, c))
                            pool.tensor_tensor(MV[:, c, 1, :], TF[:, c, :], XT[:, c, 0, :],
                                               ALU.mult).then_inc(moved_pool.sem, 1)
                            pool.wait_ge(moved_pool.sem, moved_pool.at(s, k, c))
                            pool.wait_ge(first_moved.sem, first_moved.at(s, k, c))
                            pool.tensor_tensor(XT[:, c, 1, :], XT[:, c, 1, :], MV[:, c, 1, :],
                                               ALU.subtract).then_inc(second_moved.sem, 1)

                def per_feature(s):
                    for c in seqs:
                        power(s, c)
                    for c in seqs:
                        pool.wait_ge(xn_ready.sem, xn_ready.at(s, c))
                        pool.tensor_tensor(X[:, c], X[:, c], bcast(bout_d), ALU.add).then_inc(biased.sem, 1)

                coupled("A")
                for c in seqs:
                    power("B", c)
                for c in seqs:
                    power("KV", c)
                    for st in STEPS["B"]:
                        if st[0] == "rope":
                            g = st[1]
                            r = g % 2
                            for n, (w, dst) in enumerate((("k", KR), ("q", QR))):
                                a, b = (XN[:, n].rearrange("p (v u) d -> p v (u d)", v=2)[:, v, :] for v in range(2))
                                for part in ("straight", "turned"):
                                    read_out(pool, "rope", c, g, w, part)
                                pool.tensor_tensor(a, a, b, ALU.add).then_inc(rope_sum.sem, 1)
                                pool.wait_ge(rope_hi.sem, rope_hi.at(c, g, w))
                                pool.tensor_tensor(rounded(dst[:, r, 1, :]), a, dst[:, r, 0, :],
                                                   ALU.subtract).then_inc(rope_lo.sem, 1)
                coupled("C")
                per_feature("D")
                for c in seqs:
                    power("E", c)
                for c in seqs:
                    pool.wait_ge(xn_ready.sem, xn_ready.at("E", c))
                    for f in range(KT):
                        when_full(pool, "xt", "E", c, f)
                    pool.tensor_tensor(XN[:, c], XN[:, c], bcast(bout_e), ALU.add).then_inc(biased.sem, 1)
                for c in seqs:
                    power("E2", c)
                for c in seqs:
                    pool.wait_ge(xn_ready.sem, xn_ready.at("E2", c))
                    link(pool.tensor_tensor(HB[:, c], XN[:, c], bcast(gamma_r), ALU.mult))
                    pool.tensor_tensor(HB[:, c], HB[:, c], bcast(betab2_r), ALU.add).then_inc(biased.sem, 1)
                for c in seqs:
                    power("E3", c)
                for c in seqs:
                    pool.wait_ge(xn_ready.sem, xn_ready.at("E3", c))
                    link(pool.tensor_tensor(HB[:, c], HB[:, c], bcast(gamma_r), ALU.mult))
                    pool.tensor_tensor(HB[:, c], HB[:, c], bcast(beta_r), ALU.add).then_inc(biased.sem, 1)
                per_feature("F")

            @block.sync
            def _(sp):
                for c in seqs:
                    sp.dma_start(X[:, c], x_v[turn, c]).then_inc(x_loaded, 16)

                def raw(ap):
                    return ap.bitcast(F32)

                for s in "BE":
                    keys, tiles, first = attention_shapes(s, T)
                    for c in seqs:
                        for st in STEPS[s]:
                            g = st[1]
                            r = g % 2
                            if st[0] == "stack":
                                for w in "kq":
                                    if s == "B":
                                        sp.wait_ge(rope_lo.sem, rope_lo.at(c, g, w))
                                    read_out(sp, "hi", s, c, w, g // 2)
                                n = groups.index((s, c, g))
                                if n >= 2:
                                    e = groups[n - 2]
                                    when_full(sp, e[0], e[1], "exp", e[2], *last_exp(e[0], e[2]))
                                for j in range(4):
                                    h = 4 * g + j
                                    a = HD * (h % 8)
                                    x = h // 8
                                    if s == "B":
                                        b = RD * j
                                        moves = []
                                        for m in range(2):
                                            moves += [(SQ[32 * m:32 * m + RD, r, j, :], QR[b:b + RD, r, m, :]),
                                                      (SQ[64 + HD * m:64 + HD * m + HD, r, j, :], QC[a:a + HD, m, :]),
                                                      (SK1[32 * m:32 * m + RD, r, j, :], KR[b:b + RD, r, 0, :]),
                                                      (SK1[64 + HD * m:64 + HD * m + HD, r, j, :], KC[a:a + HD, 0, :])]
                                        moves += [(SK2[0:RD, r, j, :], KR[b:b + RD, r, 1, :]),
                                                  (SK2[64:64 + HD, r, j, :], KC[a:a + HD, 1, :])]
                                    else:
                                        k0, n_k = KCOPY[x, STRIDES[h]], keys[h]
                                        d0 = first[h] * P
                                        moves = [(SQ[HD * m:HD * m + HD, r, j, :], QE[a:a + HD, x, m % 2, :]) for m in range(3)]
                                        moves += [(SKE[HD * m:HD * m + HD, d0:d0 + n_k], KE[a:a + HD, m // 2, k0:k0 + n_k])
                                                  for m in range(3)]
                                    for dst, src in moves:
                                        sp.dma_start(raw(dst), src).then_inc(stacked[r], 16)
                            elif st[0] == "shift":
                                read_out(sp, s, c, "shift", g)
                                sp.dma_start(raw(SQ[SHIFT:SHIFT + 1, r, :, :]), NM[0:P:32, :]).then_inc(shift_in, 16)
                for c in seqs:
                    for b in range(2):
                        read_out(sp, "mout", "F", c, b)
                    sp.dma_start(o_v[turn, c], X[:, c]).then_inc(x_stored, 16)
                sp.wait_ge(x_stored, 16 * CH)

          nc.all_engine_barrier(sems_to_clear=range(cleared.num, last_sem.num + 1))


NAMES = ["L0_attn_x", "L0_attn_W_kv", "L0_attn_g_kv", "L0_attn_W_kdec", "L0_attn_W_vdec", "L0_attn_W_q",
         "L0_attn_W_qdec", "L0_attn_W_krope", "L0_attn_W_qrope", "L0_attn_W_o",
         "L0_ffn_cn_w1", "L0_ffn_cn_b1", "L0_ffn_cn_w2", "L0_ffn_cn_b2", "L0_ffn_cn_w3", "L0_ffn_cn_b3",
         "L0_ffn_cn_w4", "L0_ffn_cn_b4", "L0_ffn_gc_w1", "L0_ffn_gc_b1", "L0_ffn_gc_w2", "L0_ffn_gc_b2",
         "L0_ffn_gc_w3", "L0_ffn_gc_b3", "L0_ffn_adaptive_range",
         "L1_attn_Wqkv", "L1_attn_bqkv", "L1_attn_Wout", "L1_attn_bout", "L1_attn_gamma", "L1_attn_beta",
         "L1_attn_W1", "L1_attn_b1", "L1_attn_W2", "L1_attn_b2",
         "L1_ffn_Win", "L1_ffn_bin_", "L1_ffn_W1", "L1_ffn_b1", "L1_ffn_W2", "L1_ffn_b2", "L1_ffn_Wout",
         "L1_ffn_bout"]


def rope_tables(T):
    inv_freq = 1.0 / 10000.0 ** (np.arange(0, RD, 2, dtype=np.float32) / RD)
    angles = np.outer(np.arange(T, dtype=np.float32), inv_freq)
    cos, sin = np.cos(angles).T, np.sin(angles).T
    return (np.ascontiguousarray(np.tile(np.concatenate([cos, cos]), (P // RD, 1)), dtype=np.float32),
            np.ascontiguousarray(np.tile(np.concatenate([-sin, sin]), (P // RD, 1)), dtype=np.float32))


def kernel(**inputs):
    import concourse.bacc as bacc
    from concourse.bass_utils import run_bass_kernel_spmd

    nc = bacc.Bacc("TRN2", target_bir_lowering=False, num_devices=1)
    arrays = {name: np.ascontiguousarray(inputs[name]) for name in NAMES}
    B, T, C = arrays["L0_attn_x"].shape
    arrays["rope_cos"], arrays["rope_sin"] = rope_tables(T)
    ins = {name: nc.dram_tensor(f"in_{name}", a.shape, mybir.dt.from_np(a.dtype), kind="ExternalInput").ap()
           for name, a in arrays.items()}
    out = nc.dram_tensor("out", (B, T, C), F32, kind="ExternalOutput").ap()
    build(nc, ins, out)
    r = run_bass_kernel_spmd(nc, [{f"in_{name}": a for name, a in arrays.items()}], core_ids=[0])
    return r.results[0]["out"]
```

```python
from contextlib import ExitStack

import numpy as np

import concourse.bass as bass
from concourse import mybir

F32 = mybir.dt.float32
F32R = mybir.dt.float32r
BF16 = mybir.dt.bfloat16
ALU = mybir.AluOpType
ACT = mybir.ActivationFunctionType
AX_X = mybir.AxisListType.X

P = 128
CH = 2
CYCLES = 3
HEADS, HD, RD = 16, 16, 32
GROUPS = HEADS // 4
STRIDES = [1, 1, 2, 2, 2, 2, 4, 4, 4, 4, 8, 8, 8, 8, 16, 16]
LN_EPS = 1e-5
RMS_EPS = 1e-6
MASKED = -1.0e30
STAGES = "ABCDEF"


def attention_shapes(stage, T):
    keys = [T] * HEADS if stage == "B" else [T // s for s in STRIDES]
    tiles = [-(-k // P) for k in keys]
    first = [sum(tiles[:h]) for h in range(HEADS)]
    return keys, tiles, first


def max_jobs(stage, g, T):
    keys, _, _ = attention_shapes(stage, T)
    jobs = []
    if stage == "B":
        for t in range(T // P):
            n = P * (t + 1)
            m = min(4, 512 // n)
            m = 1 if m == 3 else m
            jobs += [([t], list(range(j, j + m)), n) for j in range(0, 4, m)]
        return jobs
    for pair in (0, 2):
        n = keys[4 * g + pair]
        if n == 512:
            jobs += [([t], [j], n) for t in range(T // P) for j in (pair, pair + 1)]
        else:
            m = min(T // P, 512 // (2 * n))
            jobs += [(list(range(t, t + m)), [pair, pair + 1], n) for t in range(0, T // P, m)]
    return jobs


def attention_steps(stage, T):
    _, tiles, _ = attention_shapes(stage, T)
    ropes = stage == "B"

    def maxima(g):
        return [("max", g, n) for n in range(len(max_jobs(stage, g, T)))]

    steps = [("content", 0)]
    for g in range(2):
        steps += [("stack", g)] + ([("rope", g), ("place", g)] if ropes else [])
    steps += maxima(0) + [("shift", 0)]
    for g in range(GROUPS):
        exps = [(kt, pair) for kt in range(4) for pair in (0, 1) if kt < tiles[4 * g + 2 * pair]]
        if g:
            steps.append(("divide", g - 1))
            if g + 1 < GROUPS:
                steps += [("stack", g + 1)] + ([("rope", g + 1)] if ropes else [])
        wait = 3 if ropes and g else 0
        ahead = maxima(g + 1) if g + 1 < GROUPS else []
        per = -(-len(ahead) // max(1, len(exps) - wait))
        for n, (kt, pair) in enumerate(exps):
            steps.append(("exp", g, kt, pair))
            if ropes and g and n == 1 and g + 1 < GROUPS:
                steps.append(("place", g + 1))
            if n >= wait:
                steps += ahead[per * (n - wait):per * (n - wait + 1)]
            if n and exps[n - 1][0] != kt:
                steps.append(("sum", g, kt - 1))
        if g + 1 < GROUPS:
            steps.append(("shift", g + 1))
        steps.append(("sum", g, exps[-1][0]))
    steps.append(("divide", GROUPS - 1))
    return steps


def build(nc, ins, out):
    x_in = ins["L0_attn_x"]
    B, T, C = x_in.shape
    TT, KT = T // P, C // P
    assert T == 512 and C == 256 and B % CH == 0
    TURNS = B // CH
    x_v = x_in.rearrange("(i c) (t p) d -> i c p t d", c=CH, p=P)
    o_v = out.rearrange("(i c) (t p) d -> i c p t d", c=CH, p=P)
    _, e_tiles, e_first = attention_shapes("E", T)
    E_SLOTS = sum(e_tiles)
    SCALE = {"B": float(1.0 / np.sqrt(np.float32(HD + RD))), "E": 1.0 / np.sqrt(HD)}
    STEPS = {s: attention_steps(s, T) for s in "BE"}
    KCOPY, width = {}, 0
    for s in sorted(set(STRIDES)):
        KCOPY[s] = width
        width += T // s
    KWIDE = width

    ctx = ExitStack()
    with ctx:
        def sb(name, shape, dt=F32):
            return ctx.enter_context(nc.sbuf_tensor(name, shape, dt))

        def sem(name):
            return ctx.enter_context(nc.semaphore(name))

        cn_w1 = sb("cn_w1", [P, 2, 256])
        cn_w2 = sb("cn_w2", [P, 2, 128])
        cn_w3 = sb("cn_w3", [P, 128])
        cn_w4 = sb("cn_w4", [P, 128])
        gc_w1 = sb("gc_w1", [P, 2, 128])
        gc_w2 = sb("gc_w2", [P, 128])
        gc_w3 = sb("gc_w3", [P, 128])
        cols = sb("cols", [P, 96])
        w_kv = sb("w_kv", [P, 2, 64])
        w_kdec = sb("w_kdec", [P, 256])
        w_vdec = sb("w_vdec", [P, 256])
        w_q = sb("w_q", [P, 2, 128])
        w_qdec = sb("w_qdec", [P, 256])
        w_qrope = sb("w_qrope", [P, 512])
        w_qturn = sb("w_qturn", [P, 512])
        w_krope = sb("w_krope", [P, 2, 512])
        w_kturn = sb("w_kturn", [P, 2, 512])
        w_o = sb("w_o", [P, 2, 256])
        rope_cos = sb("rope_cos", [P, T])
        rope_sin = sb("rope_sin", [P, T])
        ident = sb("ident", [P, P])
        ident_b = sb("ident_b", [P, P], BF16)
        mask_q = sb("mask_q", [P, P], BF16)
        mask_k = sb("mask_k", [P, P], BF16)
        w_qkv = sb("w_qkv", [P, 2, 768])
        w_out = sb("w_out", [P, 2, 256])
        w_up = sb("w_up", [P, 2, 1024])
        w_down = sb("w_down", [P, 8, 256])
        rows = sb("rows", [P, 5, 256])
        bout_e, gamma_r, beta_r, betab2_r, bout_d = (rows[:, n, :] for n in range(5))
        m_in = sb("m_in", [P, 2, 128])
        m_out = sb("m_out", [P, 256])

        used = [0]

        def col(n=1):
            a = used[0]
            used[0] += n
            return cols[:, a:a + n]

        c_b1, c_b2, c_b3, c_b4 = col(2), col(), col(), col()
        c_g1, c_g2, c_g3 = col(), col(), col()
        c_half4, c_half3 = col(), col()
        c_w4, c_gw3, c_range, c_sign = col(), col(), col(), col()
        c_tf, c_gf, c_base = col(), col(), col()
        c_gkv = col()
        c_qkb, c_vb = col(4), col(2)
        c_gamma, c_beta, c_ub = col(2), col(2), col(8)
        c_bin = col()
        c_mw1, c_mb1, c_mw2, c_mprod = col(8), col(8), col(8), col(8)
        c_mb2, c_mbias = col(), col()
        neg_half = sb("neg_half", [P, 4])

        X = sb("X", [P, CH, TT, C])
        XN = sb("XN", [P, CH, TT, C])
        XT = sb("XT", [P, CH, KT, T])
        stats = sb("stats", [P, CH, TT, 6])
        mv = sb("mv", [P, CH, TT, 2])
        var = sb("var", [P, CH, TT])
        rstd = sb("rstd", [P, CH, TT])
        scratch = sb("scratch", [P, 8192])
        H1 = scratch[:, 0:2048].rearrange("p (c m n) -> p c m n", c=CH, m=2)
        H2 = scratch[:, 2048:3072].rearrange("p (c n) -> p c n", c=CH)
        H3 = scratch[:, 3072:4096].rearrange("p (c n) -> p c n", c=CH)
        TF = scratch[:, 4096:5120].rearrange("p (c n) -> p c n", c=CH)
        MV = scratch[:, 5120:7168].rearrange("p (c m n) -> p c m n", c=CH, m=2)
        S = scratch[:, 0:1024].rearrange("p (c n) -> p c n", c=CH)
        R = scratch[:, 1024:5120].rearrange("p (j n) -> p j n", j=8)
        G = scratch[:, 5120:6144].rearrange("p (c n) -> p c n", c=CH)
        split = scratch
        QC = split[:, 0:2048].rearrange("p (x s n) -> p x s n", x=2, s=2)
        KC = split[:, 2048:4096].rearrange("p (x s n) -> p x s n", x=2, s=2)
        AO = scratch[:, 6144:6656]
        NM = scratch[:, 6656:7168]
        ATN = scratch[:, 7168:8192].rearrange("p (t d) -> p t d", t=TT)
        QE = split[:, 0:2048].rearrange("p (x s n) -> p x s n", x=2, s=2)
        KE = split[:, 2048:2048 + 4 * KWIDE].rearrange("p (x s n) -> p x s n", x=2, s=2)
        SQ = sb("SQ", [P, 2, 4, T], F32R)
        SK1 = sb("SK1", [P, 2, 4, T], F32R)
        SK2 = sb("SK2", [P, 2, 4, T], F32R)
        SKE = sb("SKE", [P, E_SLOTS * P], F32R)
        SHIFT = 96
        VB = sb("VB", [P, TT, HEADS, HD + 1])
        VE = sb("VE", [P, E_SLOTS, HD + 1])
        PR = sb("PR", [P, 2, 4, T])
        U = PR[:, :, :, :].rearrange("p a j n -> p (a j) n")
        MX = sb("MX", [P, TT, P])
        rden = sb("rden", [P, 4, 4])
        ATT = sb("ATT", [P, KT, T])
        QL = ATT[:, 0, :]
        KVT = ATT[:, 1, :]
        HB = scratch[:, 6144:8192].rearrange("p (c t d) -> p c t d", c=CH, t=TT)
        means = sb("means", [P, CH, KT])
        gc_h = sb("gc_h", [P, CH, 4])

        ps = ctx.enter_context(nc.psum_tensor("ps", [P, 8, 512], F32))

        loaded, const_pool, const_dve, const_act = sem("loaded"), sem("const_pool"), sem("const_dve"), sem("const_act")
        cleared = sem("x_loaded")
        x_loaded = cleared
        full = [sem(f"bank_full{b}") for b in range(8)]
        free = [sem(f"bank_free{b}") for b in range(8)]

        class Signal:

            def __init__(self, name, events):
                self.sem, self.events = sem(name), list(events)

            def at(self, *event):
                return self.events.index(event if len(event) > 1 else event[0]) + 1

        seqs = range(CH)
        norms = [(s, c) for s in ("A", "B") for c in seqs] + [("KV", c) for c in seqs] + \
                [(s, c) for s in ("C", "D", "E", "E2", "E3", "F") for c in seqs]
        var_ready = Signal("var_ready", norms)
        rstd_ready = Signal("rstd_ready", norms)
        xn_ready = Signal("xn_ready", norms)
        cycles = [(s, k, c) for s in "AC" for k in range(CYCLES) for c in seqs]
        coupling_ready = Signal("coupling_ready", cycles)
        moved_pool = Signal("moved_pool", cycles)
        first_moved = Signal("first_moved", cycles)
        second_moved = Signal("second_moved", cycles)
        hi_ready = Signal("hi_ready", [(s, c, w, x) for s in "BE" for c in seqs for x in range(2) for w in "kq"])
        ropes = [(c, st[1], w) for c in seqs for st in STEPS["B"] if st[0] == "rope" for w in "kq"]
        rope_sum, rope_hi, rope_lo = (Signal(n, ropes) for n in ("rope_sum", "rope_hi", "rope_lo"))
        places = [(c, st[1]) for c in seqs for st in STEPS["B"] if st[0] == "place"]
        placed_act, placed_dve = Signal("placed_act", places), Signal("placed_dve", places)
        groups = [(s, c, g) for s in "BE" for c in seqs for g in range(GROUPS)]
        stacked = [sem(f"stacked{r}") for r in range(2)]
        stack_count, total = {}, [0, 0]
        for s, c, g in groups:
            total[g % 2] += 16 * 2 * (5 if s == "B" else 6)
            stack_count[s, c, g] = total[g % 2]
        shift_in = sem("shift_in")
        sums = [(s, c, *st[1:]) for s in "BE" for c in seqs for st in STEPS[s] if st[0] == "sum"]

        def depth(s, g):
            return max(attention_shapes(s, T)[1][4 * g:4 * g + 4])

        def last_exp(s, g):
            return [st[2:] for st in STEPS[s] if st[0] == "exp" and st[1] == g][-1]

        def rounded(ap):
            return ap.bitcast(F32R)

        sum_done = Signal("sum_done", [e for e in sums if e[3] < depth(e[0], e[2]) - 1])
        biased = Signal("biased", [(s, c) for s in ("D", "E", "HB", "E3", "F") for c in seqs])
        g_ready = Signal("g_ready", [(s, c) for s in "DF" for c in seqs])
        dve_step, pool_step = sem("dve_step"), sem("pool_step")
        x_stored = sem("x_stored")
        last_sem = x_stored
        V_PARTS = [(st, [h for h in range(HEADS) if STRIDES[h] == st], min(P, T // st)) for st in (1, 2, 4, 8, 16)]

        def over_partitions(vec, n):
            return vec.partition_broadcast(P) if n is None else vec.partition_broadcast(n)

        setup = ExitStack()
        with nc.Block() as block:
            loads = []

            def two_tiles(name, dst):
                loads.append((dst, ins[name].rearrange("(k p) n -> p k n", p=P)))

            def column(name, dst, m=None):
                v = ins[name]
                loads.append((dst, v.rearrange("(m p) -> p m", m=m)))

            def by_parity(dst, src):
                for x in range(2):
                    loads.append((dst[:, x * P:(x + 1) * P].rearrange("p (d e) -> p d e", e=HD),
                                  src.rearrange("k (d x e) -> k x d e", x=2, e=HD)[:, x]))

            two_tiles("L0_ffn_cn_w1", cn_w1[:])
            two_tiles("L0_ffn_cn_w2", cn_w2[:])
            two_tiles("L0_ffn_gc_w1", gc_w1[:])
            for h in range(2):
                loads.append((cn_w3[:, 64 * h:64 * h + 64], ins["L0_ffn_cn_w3"]))
                loads.append((gc_w2[:, 64 * h:64 * h + 64], ins["L0_ffn_gc_w2"]))
                loads.append((c_b3[64 * h:64 * h + 64, :], ins["L0_ffn_cn_b3"].rearrange("(p m) -> p m", m=1)))
                loads.append((c_g2[64 * h:64 * h + 64, :], ins["L0_ffn_gc_b2"].rearrange("(p m) -> p m", m=1)))
                loads.append((c_bin[64 * h:64 * h + 64, :], ins["L1_ffn_bin_"].rearrange("(p m) -> p m", m=1)))
                loads.append((c_mw1[64 * h:64 * h + 64, :], ins["L1_ffn_W1"][:, 8 * h:8 * h + 8]))
                loads.append((c_mb1[64 * h:64 * h + 64, :], ins["L1_ffn_b1"][:, 8 * h:8 * h + 8]))
                loads.append((c_mw2[64 * h:64 * h + 64, :], ins["L1_ffn_W2"][:, 8 * h:8 * h + 8]))
                loads.append((m_in[:, :, 64 * h:64 * h + 64], ins["L1_ffn_Win"].rearrange("(k p) n -> p k n", p=P)))
                loads.append((m_out[64 * h:64 * h + 64, :], ins["L1_ffn_Wout"]))
            loads.append((c_mb2[0:64, :], ins["L1_ffn_b2"].rearrange("(p m) -> p m", m=1)))
            loads.append((c_w4[0:64, :], ins["L0_ffn_cn_w4"]))
            loads.append((c_gw3[0:64, :], ins["L0_ffn_gc_w3"]))
            loads.append((c_gkv[0:64, :], ins["L0_attn_g_kv"].rearrange("(p m) -> p m", m=1)))
            column("L0_ffn_cn_b1", c_b1, 2)
            column("L0_ffn_cn_b2", c_b2, 1)
            column("L0_ffn_gc_b1", c_g1, 1)
            loads.append((c_vb, ins["L1_attn_bqkv"][2 * C:3 * C].rearrange("(m p) -> p m", m=2)))
            for w in range(2):
                for d in range(HEADS // 2):
                    v = ins["L1_attn_bqkv"][w * C:(w + 1) * C].rearrange("(d x e) -> d e x", x=2, e=HD)
                    loads.append((c_qkb[HD * d:HD * d + HD, 2 * w:2 * w + 2], v[d]))
            column("L1_attn_gamma", c_gamma, 2)
            column("L1_attn_beta", c_beta, 2)
            column("L1_attn_b1", c_ub, 8)
            loads.append((c_b4, ins["L0_ffn_cn_b4"].partition_broadcast(P)))
            loads.append((c_g3, ins["L0_ffn_gc_b3"].partition_broadcast(P)))
            loads.append((c_range, ins["L0_ffn_adaptive_range"].partition_broadcast(P)))
            two_tiles("L0_attn_W_kv", w_kv[:])
            by_parity(w_kdec[0:64, :], ins["L0_attn_W_kdec"])
            loads.append((w_vdec[0:64, :], ins["L0_attn_W_vdec"]))
            two_tiles("L0_attn_W_q", w_q[:])
            by_parity(w_qdec[:], ins["L0_attn_W_qdec"])
            loads.append((w_qrope[:], ins["L0_attn_W_qrope"]))
            two_tiles("L0_attn_W_krope", w_krope[:])
            two_tiles("L0_attn_W_o", w_o[:])
            loads.append((rope_cos[:], ins["rope_cos"]))
            loads.append((rope_sin[:], ins["rope_sin"]))
            for f in range(KT):
                w = ins["L1_attn_Wqkv"][f * P:(f + 1) * P, :]
                for a in (0, C):
                    by_parity(w_qkv[:, f, a:a + C], w[:, a:a + C])
                loads.append((w_qkv[:, f, 2 * C:3 * C], w[:, 2 * C:3 * C]))
            two_tiles("L1_attn_Wout", w_out[:])
            two_tiles("L1_attn_W1", w_up[:])
            loads.append((w_down[:], ins["L1_attn_W2"].rearrange("(k p) n -> p k n", p=P)))
            loads.append((bout_e, ins["L1_attn_bout"].partition_broadcast(P)))
            loads.append((gamma_r, ins["L1_attn_gamma"].partition_broadcast(P)))
            loads.append((beta_r, ins["L1_attn_beta"].partition_broadcast(P)))
            loads.append((betab2_r, ins["L1_attn_b2"].partition_broadcast(P)))
            loads.append((bout_d, ins["L1_ffn_bout"].partition_broadcast(P)))
            ALL_LOADS = 16 * len(loads)

            @block.sync
            def _(sp):
                for dst, src in loads:
                    sp.dma_start(dst, src, allow_slow_non_contiguous=True).then_inc(loaded, 16)
                sp.wait_ge(loaded, ALL_LOADS)

            @block.gpsimd
            def _(pool):
                for m in (ident, ident_b, mask_q, mask_k):
                    pool.memset(m[:], 0.0).then_inc(const_pool, 1)
                pool.memset(neg_half[:], -0.5).then_inc(const_pool, 1)
                pool.wait_ge(const_pool, 5)
                for m in (ident, ident_b):
                    pool.affine_select(out=m[:], in_=m[:], compare_op=ALU.not_equal, fill=1.0, base=0,
                                       pattern=[[-1, P]], channel_multiplier=1).then_inc(const_pool, 1)
                pool.affine_select(out=mask_q[:], in_=mask_q[:], compare_op=ALU.is_ge, fill=MASKED, base=0,
                                   pattern=[[-1, P]], channel_multiplier=1).then_inc(const_pool, 1)
                pool.affine_select(out=mask_k[:], in_=mask_k[:], compare_op=ALU.is_ge, fill=MASKED, base=0,
                                   pattern=[[1, P]], channel_multiplier=-1).then_inc(const_pool, 1)
                pool.memset(VB[:], 1.0).then_inc(const_pool, 1)
                pool.memset(VE[:], 1.0).then_inc(const_pool, 1)
                pool.memset(MX[:], 0.0).then_inc(const_pool, 1)
                pool.memset(ATT[:], 0.0).then_inc(const_pool, 1)
                pool.wait_ge(const_pool, 13)
                for h in range(HEADS):
                    n = T // STRIDES[h]
                    if n < P and STRIDES[h] != STRIDES[h - 1]:
                        heads = STRIDES.count(STRIDES[h])
                        for q in range(n, P, 32):
                            pool.memset(VE[q:q + 32, e_first[h]:e_first[h] + heads, :], 0.0).then_inc(const_pool, 1)

            @block.vector
            def _(dve):
                n = 0

                def then(ins_):
                    ins_.then_inc(const_dve, 1)
                    nonlocal n
                    n += 1

                for m in (SQ, SK1, SK2):
                    then(dve.memset(m[:].bitcast(F32), 0.0))
                then(dve.memset(SKE[:].bitcast(F32), 0.0))
                then(dve.memset(cn_w4[64:P, :], 0.0))
                then(dve.memset(gc_w3[64:P, :], 0.0))
                then(dve.memset(w_kdec[64:P, :], 0.0))
                then(dve.memset(w_vdec[64:P, :], 0.0))
                then(dve.memset(c_sign[0:64, :], 1.0))
                then(dve.memset(c_sign[64:P, :], -1.0))
                then(dve.memset(c_mb2[64:P, :], 0.0))
                then(dve.memset(cn_w4[0:64, :], 1.0))
                then(dve.memset(gc_w3[0:64, :], 1.0))
                then(dve.memset(ps[:, 6:8, :], 0.0))
                dve.wait_ge(const_dve, n)
                then(dve.memset(SK1[SHIFT:SHIFT + 1, :, :, :].bitcast(F32), 1.0))
                for h in range(HEADS):
                    a = e_first[h] * P
                    then(dve.memset(SKE[SHIFT:SHIFT + 1, a:a + T // STRIDES[h]].bitcast(F32), 1.0))
                dve.wait_ge(loaded, ALL_LOADS)
                then(dve.tensor_scalar(cn_w4[0:64, :], cn_w4[0:64, :], c_w4[0:64, :], None, ALU.mult))
                then(dve.tensor_scalar(gc_w3[0:64, :], gc_w3[0:64, :], c_gw3[0:64, :], None, ALU.mult))
                then(dve.tensor_scalar(c_half4, c_b4, 0.5, None, ALU.mult))
                then(dve.tensor_scalar(c_half3, c_g3, 0.5, None, ALU.mult))
                then(dve.tensor_scalar(c_tf, c_sign, c_range, 0.3, ALU.mult, ALU.mult))
                then(dve.tensor_scalar(c_gf, c_sign, c_range, 0.7, ALU.mult, ALU.mult))
                then(dve.tensor_scalar(c_base, c_sign, 0.1, None, ALU.mult))
                then(dve.tensor_scalar(w_kdec[0:64, :], w_kdec[0:64, :], c_gkv[0:64, :], None, ALU.mult))
                then(dve.tensor_scalar(w_vdec[0:64, :], w_vdec[0:64, :], c_gkv[0:64, :], None, ALU.mult))
                for w, turn in ((w_qrope[:], w_qturn[:]), (w_krope[:, 0, :], w_kturn[:, 0, :]),
                                (w_krope[:, 1, :], w_kturn[:, 1, :])):
                    a = w.rearrange("p (h s d) -> p h s d", s=2, d=RD // 2)
                    b = turn.rearrange("p (h s d) -> p h s d", s=2, d=RD // 2)
                    for s in range(2):
                        then(dve.tensor_copy(b[:, :, s, :], a[:, :, 1 - s, :]))
                then(dve.tensor_tensor(betab2_r, betab2_r, beta_r, ALU.add))
                then(dve.tensor_scalar(bout_d, bout_d, 0.5, None, ALU.mult))
                then(dve.tensor_scalar(m_out[:], m_out[:], 0.5, None, ALU.mult))
                then(dve.tensor_tensor(c_mprod, c_mw2, c_mb1, ALU.mult))
                dve.wait_ge(const_dve, n)
                then(dve.tensor_reduce(c_mbias, c_mprod, AX_X, ALU.add))
                then(dve.tensor_scalar(c_mb1, c_mb1, -1.0, None, ALU.mult))
                dve.wait_ge(const_dve, n)
                then(dve.tensor_tensor(c_mbias, c_mbias, c_mb2, ALU.add))

        J = {}

        def when_full(eng, *key):
            b, n = J[key]
            eng.wait_ge(full[b], n)
            return ps[:, b, :]

        def read_out(eng, *key):
            b, n = J[key]
            eng.wait_ge(free[b], n)

        def freed(ins_, *key):
            ins_.then_inc(free[J[key][0]], 1)

        def stack_free(eng, s, c, g):
            n = groups.index((s, c, g))
            if n >= 2:
                e = groups[n - 2]
                when_full(eng, e[0], e[1], "exp", e[2], *last_exp(e[0], e[2]))

        def rope_parts(w):
            both = XN[:, "kq".index(w)].rearrange("p (v u) d -> p v (u d)", v=2)
            return both[:, 0, :], both[:, 1, :]

        def e_parts(src, w, x):
            if w == "q":
                return [(src, QE[:, x, 0, :], QE[:, x, 1, :], c_qkb[:, x:x + 1])]
            return [(src[:, 0:T:st], KE[:, x, 0, a:a + T // st], KE[:, x, 1, a:a + T // st], c_qkb[:, 2 + x:3 + x])
                    for st, a in KCOPY.items()]

        with nc.Fori(0, TURNS) as turn:
          with nc.Block() as block:

            @block.tensor
            def _(pe):
                count, last_job = [0] * 8, [None] * 8

                def take(bank, *key, width=1):
                    for b in range(bank, bank + width):
                        if last_job[b] is not None and last_job[b] not in [last_job[x] for x in range(bank, b)]:
                            pe.wait_ge(free[last_job[b][0]], last_job[b][1])
                    count[bank] += 1
                    J[key] = (bank, count[bank])
                    for b in range(bank, bank + width):
                        last_job[b] = J[key]
                    return ps[:, bank, :] if width == 1 else ps[:, bank:bank + width, :]

                def mm(dst, lhsT, rhs, start=True, stop=True):
                    return pe.matmul(dst, lhsT, rhs, start=start, stop=stop, skip_group_check=True)

                def transposed(s, c, banks):
                    pe.wait_ge(xn_ready.sem, xn_ready.at(s, c))
                    for f in range(KT):
                        dst = take(banks[f], "xt", s, c, f)
                        for t in range(TT):
                            last = pe.transpose(dst[:, t * P:(t + 1) * P], XN[:, c, t, f * P:(f + 1) * P], ident[:])
                        last.then_inc(full[banks[f]], 1)

                def in_xt(s, c):
                    for f in range(KT):
                        read_out(pe, "xt", s, c, f)

                def product(bank, key, pairs, rows=P, cols_=T):
                    dst = take(bank, *key)
                    for n, (lhsT, rhs) in enumerate(pairs):
                        last = mm(dst[0:rows, 0:cols_], lhsT, rhs, n == 0, n == len(pairs) - 1)
                    last.then_inc(full[bank], 1)

                def coupled(s):
                    for c in seqs:
                        transposed(s, c, (4 * c + 2, 4 * c + 3))
                    for k in range(CYCLES):
                        for c in seqs:
                            if k == 0:
                                in_xt(s, c)
                            else:
                                pe.wait_ge(first_moved.sem, first_moved.at(s, k - 1, c))
                                pe.wait_ge(second_moved.sem, second_moved.at(s, k - 1, c))
                            for m in range(2):
                                product(4 * c + m, ("h1", s, k, c, m),
                                        [(cn_w1[:, f, m * P:(m + 1) * P], XT[:, c, f, :]) for f in range(KT)])
                            if k == 0:
                                product(4 * c + 3, ("gc", s, 0, c),
                                        [(gc_w1[:, f, :], means[:, c, f:f + 1]) for f in range(KT)], cols_=1)
                        for c in seqs:
                            if k == 0:
                                read_out(pe, "gc", s, 0, c)
                                product(4 * c + 3, ("gc", s, 1, c), [(gc_w2[:], gc_h[:, c, 0:1])], cols_=1)
                            for m in range(2):
                                read_out(pe, "h1", s, k, c, m)
                            product(4 * c + 2, ("h2", s, k, c), [(cn_w2[:, f, :], H1[:, c, f, :]) for f in range(KT)])
                        for c in seqs:
                            if k == 0:
                                read_out(pe, "gc", s, 1, c)
                                product(4 * c + 3, ("gc", s, 2, c), [(gc_w3[:], gc_h[:, c, 1:2])], cols_=1)
                            read_out(pe, "h2", s, k, c)
                            product(4 * c, ("h3", s, k, c), [(cn_w3[:], H2[:, c, :])])
                        for c in seqs:
                            read_out(pe, "h3", s, k, c)
                            product(4 * c + 1, ("tf", s, k, c), [(cn_w4[:], H3[:, c, :])])
                    for c in seqs:
                        pe.wait_ge(first_moved.sem, first_moved.at(s, CYCLES - 1, c))
                        pe.wait_ge(second_moved.sem, second_moved.at(s, CYCLES - 1, c))
                        for b in range(2):
                            dst = take(4 * c + 2 + b, "back", s, c, b)
                            for n in range(4):
                                t, f = 2 * b + n // 2, n % 2
                                last = pe.transpose(dst[:, n * P:(n + 1) * P], XT[:, c, f, t * P:(t + 1) * P], ident[:])
                            last.then_inc(full[4 * c + 2 + b], 1)

                def parity(w, x):
                    return w[:, x * P:(x + 1) * P]

                def attention(s, c):
                    keys, tiles, first = attention_shapes(s, T)
                    ring = [0]

                    def side():
                        ring[0] ^= 1
                        return ring[0]

                    def causal(dst, mask, stop=True):
                        return mm(dst, ident_b[:], mask[:], False, stop)

                    for st in STEPS[s]:
                        g = st[1]
                        r = g % 2
                        if st[0] == "content":
                            for x in range(2):
                                for w in "kq":
                                    if s == "B":
                                        pairs = [(parity(w_kdec, x), KVT)] if w == "k" else [(parity(w_qdec, x), QL)]
                                    else:
                                        pairs = [(parity(w_qkv[:, f, C * "qk".index(w):C * "qk".index(w) + C], x),
                                                  XT[:, c, f, :]) for f in range(KT)]
                                    product(2 + 2 * x + "kq".index(w), ("hi", s, c, w, x), pairs)
                        elif st[0] == "rope":
                            for w, (w_r, w_t) in (("k", (w_krope, w_kturn)), ("q", (w_qrope, w_qturn))):
                                for part, wt in (("straight", w_r), ("turned", w_t)):
                                    a = slice(g * P, (g + 1) * P)
                                    pairs = [(wt[:, a], QL)] if w == "q" else \
                                            [(wt[:, f, a], XT[:, c, f, :]) for f in range(KT)]
                                    product(side(), ("rope", c, g, w, part), pairs)
                        elif st[0] == "max":
                            ts, hs, nk = max_jobs(s, g, T)[st[2]]
                            if st[2] == 0:
                                pe.wait_ge(stacked[r], stack_count[s, c, g])
                                if s == "B":
                                    pe.wait_ge(placed_act.sem, placed_act.at(c, g))
                                    pe.wait_ge(placed_dve.sem, placed_dve.at(c, g))
                            b = side()
                            dst = take(b, *((s, c) + st))
                            at = 0
                            for t in ts:
                                for j in hs:
                                    h = 4 * g + j
                                    k1 = SK1[0:SHIFT, r, j, 0:nk] if s == "B" else \
                                        SKE[0:SHIFT, first[h] * P:first[h] * P + nk]
                                    last = mm(dst[:, at:at + nk], SQ[0:SHIFT, r, j, t * P:(t + 1) * P], k1,
                                              True, s == "E")
                                    if s == "B":
                                        last = causal(dst[:, at + t * P:at + nk], mask_q)
                                    at += nk
                            last.then_inc(full[b], 1)
                        elif st[0] == "shift":
                            read_out(pe, s, c, "max", g, len(max_jobs(s, g, T)) - 1)
                            b = side()
                            dst = take(b, s, c, "shift", g)
                            for t in range(TT):
                                last = pe.transpose(dst[:, t * P:(t + 1) * P], MX[:, t, :], ident[:])
                            last.then_inc(full[b], 1)
                        elif st[0] == "exp":
                            _, _, kt, pair = st
                            if (kt, pair) == (0, 0):
                                pe.wait_ge(shift_in, 16 * (groups.index((s, c, g)) + 1))
                            q0 = kt * P if s == "B" else 0
                            b = 2 + 2 * pair
                            both = take(b, s, c, "exp", g, kt, pair, width=2)
                            for n in range(2):
                                j = 2 * pair + n
                                h = 4 * g + j
                                dst = both[:, n, 0:T - q0]
                                q = SQ[0:SHIFT + 1, r, j, q0:T]
                                if s == "B":
                                    mm(dst, SK1[0:SHIFT + 1, r, j, kt * P:(kt + 1) * P], q, True, False)
                                    mm(dst, SK2[0:SHIFT + 1, r, j, kt * P:(kt + 1) * P], q, False, False)
                                    last = causal(dst[:, 0:P], mask_k)
                                else:
                                    a = (first[h] + kt) * P
                                    last = mm(dst, SKE[0:SHIFT + 1, a:a + P], q)
                            last.then_inc(full[b], 1)
                        elif st[0] == "sum":
                            _, _, kt = st
                            for pair in (0, 1):
                                if kt < tiles[4 * g + 2 * pair]:
                                    read_out(pe, s, c, "exp", g, kt, pair)
                            if (g, kt) == (0, 0):
                                for b in range(2 if s == "B" else 1):
                                    read_out(pe, "v", s, c, b)
                            b = 6 + r
                            dst = take(b, s, c, "sum", g) if kt == 0 else ps[:, b, :]
                            q0 = kt * P if s == "B" else 0
                            for j in range(4):
                                h = 4 * g + j
                                if kt < tiles[h]:
                                    v = VB[:, kt, h, :] if s == "B" else VE[:, first[h] + kt, :]
                                    last = mm(dst[32 * j:32 * j + HD + 1, q0:T], v, PR[:, kt % 2, j, q0:T],
                                              kt == 0, kt == tiles[h] - 1)
                            if kt == max(tiles[4 * g:4 * g + 4]) - 1:
                                last.then_inc(full[b], 1)
                            else:
                                last.then_inc(sum_done.sem, 1)
                        elif st[0] == "divide":
                            read_out(pe, s, c, "sum", g)
                            b = side()
                            dst = take(b, s, c, "divide", g)
                            for t in range(TT):
                                last = pe.transpose(dst[:, t * P:(t + 1) * P], AO[:, t * P:(t + 1) * P], ident[:])
                            last.then_inc(full[b], 1)
                    read_out(pe, s, c, "divide", GROUPS - 1)
                    for f in range(KT):
                        dst = take(2 + f, s, c, "att", f)
                        for t in range(TT):
                            last = pe.transpose(dst[:, t * P:(t + 1) * P], ATN[:, t, f * P:(f + 1) * P], ident[:])
                        last.then_inc(full[2 + f], 1)
                    for f in range(KT):
                        read_out(pe, s, c, "att", f)
                    w = w_o if s == "B" else w_out
                    for b in range(2):
                        dst = take(4 + b, s, c, "proj", b)
                        for n in range(2):
                            t = 2 * b + n
                            for f in range(KT):
                                last = mm(dst[:, n * C:(n + 1) * C], ATT[:, f, t * P:(t + 1) * P], w[:, f, :],
                                          f == 0, f == KT - 1)
                        last.then_inc(full[4 + b], 1)

                def latent(c):
                    in_xt("B", c)
                    dst = take(0, "kv", c)
                    for t in range(TT):
                        for f in range(KT):
                            last = mm(dst[:, 64 * t:64 * t + 64], XT[:, c, f, t * P:(t + 1) * P], w_kv[:, f, :],
                                      f == 0, f == KT - 1)
                    last.then_inc(full[0], 1)
                    product(1, ("ql", c), [(w_q[:, f, :], XT[:, c, f, :]) for f in range(KT)])
                    pe.wait_ge(xn_ready.sem, xn_ready.at("KV", c))
                    dst = take(2, "kvt", c)
                    for t in range(TT):
                        last = pe.transpose(dst[0:64, t * P:(t + 1) * P], XN[:, c, 2, 64 * t:64 * t + 64], ident[:])
                    last.then_inc(full[2], 1)
                    read_out(pe, "kvt", c)
                    read_out(pe, "ql", c)
                    for b in range(2):
                        dst = take(2 + b, "v", "B", c, b)
                        for n in range(2):
                            t = 2 * b + n
                            last = mm(dst[:, n * C:(n + 1) * C], KVT[:, t * P:(t + 1) * P], w_vdec[:])
                        last.then_inc(full[2 + b], 1)

                def qkv(c):
                    in_xt("E", c)
                    dst = take(1, "v", "E", c, 0)
                    at = 0
                    for st, heads, m in V_PARTS:
                        for t in range(e_tiles[heads[0]]):
                            for f in range(KT):
                                tok = XT[:, c, f, t * P * st:t * P * st + m * st:st]
                                last = mm(dst[0:m, at:at + HD * len(heads)], tok,
                                          w_qkv[:, f, 512 + HD * heads[0]:512 + HD * (heads[-1] + 1)],
                                          f == 0, f == KT - 1)
                            at += HD * len(heads)
                    last.then_inc(full[1], 1)

                def per_feature(s):
                    for c in seqs:
                        transposed(s, c, (0, 1))
                        in_xt(s, c)
                        product(2 + c, ("s", s, c), [(m_in[:, f, :], XT[:, c, f, :]) for f in range(KT)])
                    for c in seqs:
                        pe.wait_ge(g_ready.sem, g_ready.at(s, c))
                        for b in range(2):
                            dst = take(4 + 2 * c + b, "mout", s, c, b)
                            for n in range(2):
                                t = 2 * b + n
                                last = mm(dst[:, n * C:(n + 1) * C], G[:, c, t * P:(t + 1) * P], m_out[:])
                            last.then_inc(full[4 + 2 * c + b], 1)

                def feed_forward(c):
                    transposed("E2", c, (0, 1))
                    in_xt("E2", c)
                    for m in range(8):
                        product(2 + m % 4, ("up", c, m), [(w_up[:, f, m * P:(m + 1) * P], XT[:, c, f, :]) for f in range(KT)])
                    for b in range(2):
                        dst = take(6 + b, "down", c, b)
                        for n in range(2):
                            t = 2 * b + n
                            for m in range(8):
                                read_out(pe, "up", c, m)
                                last = mm(dst[:, n * C:(n + 1) * C], U[:, m, t * P:(t + 1) * P], w_down[:, m, :],
                                          m == 0, m == 7)
                        last.then_inc(full[6 + b], 1)

                coupled("A")
                for c in seqs:
                    transposed("B", c, (0, 1))
                for c in seqs:
                    latent(c)
                    attention("B", c)
                coupled("C")
                per_feature("D")
                for c in seqs:
                    transposed("E", c, (0, 1))
                for c in seqs:
                    qkv(c)
                    attention("E", c)
                for c in seqs:
                    feed_forward(c)
                per_feature("F")

            @block.vector
            def _(dve):
                steps = [0]

                def link(ins_):
                    ins_.then_inc(dve_step, 1)
                    steps[0] += 1
                    dve.wait_ge(dve_step, steps[0])

                def statistics(s, c, src, *after):
                    for key in after:
                        read_out(dve, *key)
                    for t in range(TT):
                        last = dve.bn_stats(stats[:, c, t, :], src[:, t, :])
                    link(last)
                    for t in range(TT):
                        last = dve.bn_aggr(mv[:, c, t, :], stats[:, c, t, :])
                    link(last)
                    dve.tensor_scalar(var[:, c, :], mv[:, c, :, 1], LN_EPS, None, ALU.add).then_inc(var_ready.sem, 1)

                def normalize(s, c, src, dst):
                    dve.wait_ge(rstd_ready.sem, rstd_ready.at(s, c))
                    for t in range(TT):
                        last = dve.tensor_scalar(dst[:, t, :], src[:, t, :], mv[:, c, t, 0:1], rstd[:, c, t:t + 1],
                                                 ALU.subtract, ALU.mult)
                    last.then_inc(xn_ready.sem, 1)

                def both_norms(s, after):
                    for c in seqs:
                        statistics(s, c, X[:, c], *after(c))
                    for c in seqs:
                        normalize(s, c, X[:, c], XN[:, c])

                def coupled(s, after):
                    both_norms(s, after)
                    for k in range(CYCLES):
                        for c in seqs:
                            if k == 0:
                                read_out(dve, "gc", s, 2, c)
                                link(dve.tensor_scalar(gc_h[:, c, 3:4], gc_h[:, c, 2:3], c_gf, c_base, ALU.mult, ALU.add))
                            read_out(dve, "tf", s, k, c)
                            dve.tensor_scalar(TF[:, c, :], TF[:, c, :], c_tf, gc_h[:, c, 3:4],
                                              ALU.mult, ALU.add).then_inc(coupling_ready.sem, 1)
                            dve.wait_ge(coupling_ready.sem, coupling_ready.at(s, k, c))
                            link(dve.tensor_tensor(MV[:, c, 0, :], TF[:, c, :], XT[:, c, 1, :], ALU.mult))
                            dve.wait_ge(moved_pool.sem, moved_pool.at(s, k, c))
                            dve.tensor_tensor(XT[:, c, 0, :], XT[:, c, 0, :], MV[:, c, 0, :],
                                              ALU.add).then_inc(first_moved.sem, 1)
                    for c in seqs:
                        for b in range(2):
                            src = when_full(dve, "back", s, c, b)
                            x = X[:, c, 2 * b:2 * b + 2, :]
                            last = dve.scalar_tensor_tensor(x, src.rearrange("p (t d) -> p t d", t=2), 0.5, x,
                                                            ALU.mult, ALU.add)
                            freed(last, "back", s, c, b)

                def latent(c):
                    read_out(dve, "kv", c)
                    kv = XN[:, c, 0, :]
                    sq = XN[:, c, 1, :]
                    link(dve.tensor_tensor(sq, kv, kv, ALU.mult))
                    link(dve.tensor_reduce(var[:, c, :], sq.rearrange("p (t d) -> p t d", t=TT), AX_X, ALU.add))
                    dve.tensor_scalar(var[:, c, :], var[:, c, :], 1.0 / 64, RMS_EPS, ALU.mult,
                                      ALU.add).then_inc(var_ready.sem, 1)
                    dve.wait_ge(rstd_ready.sem, rstd_ready.at("KV", c))
                    for t in range(TT):
                        last = dve.tensor_scalar(XN[:, c, 2, 64 * t:64 * t + 64], kv[:, 64 * t:64 * t + 64], rstd[:, c, t:t + 1], None,
                                                 ALU.mult)
                    last.then_inc(xn_ready.sem, 1)
                    dve.wait_ge(xn_ready.sem, xn_ready.at("KV", c))

                def attention(s, c):
                    for st in STEPS[s]:
                        g = st[1]
                        r = g % 2
                        if st[0] == "content":
                            for x in range(2):
                                for w, dst in (("k", KC), ("q", QC)):
                                    src = when_full(dve, "hi", s, c, w, x)
                                    dve.wait_ge(hi_ready.sem, hi_ready.at(s, c, w, x))
                                    if s == "B":
                                        last = dve.tensor_tensor(rounded(dst[:, x, 1, :]), src, dst[:, x, 0, :],
                                                                 ALU.subtract)
                                    else:
                                        for p, hi, lo, bias in e_parts(src, w, x):
                                            last = dve.scalar_tensor_tensor(rounded(lo), p, bias, hi,
                                                                            ALU.add, ALU.subtract)
                                    freed(last, "hi", s, c, w, x)
                        elif st[0] == "rope":
                            n = places.index((c, g))
                            if n:
                                dve.wait_ge(placed_act.sem, placed_act.at(*places[n - 1]))
                                dve.wait_ge(placed_dve.sem, placed_dve.at(*places[n - 1]))
                            for w in "kq":
                                a, b = rope_parts(w)
                                src = when_full(dve, "rope", c, g, w, "straight")
                                freed(dve.tensor_tensor(a, src, rope_cos[:], ALU.mult), "rope", c, g, w, "straight")
                                src = when_full(dve, "rope", c, g, w, "turned")
                                freed(dve.tensor_tensor(b, src, rope_sin[:], ALU.mult), "rope", c, g, w, "turned")
                        elif st[0] == "place":
                            for w in "kq":
                                a, b = rope_parts(w)
                                dve.wait_ge(rope_sum.sem, rope_sum.at(c, g, w))
                                dve.tensor_copy(rounded(b), a).then_inc(rope_hi.sem, 1)
                            stack_free(dve, s, c, g)
                            for w, m in (("q", 1), ("k", 0), ("q", 0)):
                                src = rope_parts(w)[m]
                                if m:
                                    dve.wait_ge(rope_hi.sem, rope_hi.at(c, g, w))
                                else:
                                    dve.wait_ge(rope_lo.sem, rope_lo.at(c, g, w))
                                for j in range(4):
                                    row = 0 if w == "k" or m else RD
                                    last = dve.tensor_copy((SK2 if w == "k" else SQ)[row:row + RD, r, j, :],
                                                           rounded(src[RD * j:RD * j + RD, :]))
                            last.then_inc(placed_dve.sem, 1)
                        elif st[0] == "max":
                            ts, hs, nk = max_jobs(s, g, T)[st[2]]
                            src = when_full(dve, *((s, c) + st))
                            src = src[:, 0:len(ts) * len(hs) * nk].rearrange("p (t h k) -> p t h k", t=len(ts), h=len(hs))
                            dst = MX[:, ts[0]:ts[-1] + 1, 32 * hs[0]:32 * hs[-1] + 1:32]
                            if st[2] == 0 and groups.index((s, c, g)):
                                e = groups[groups.index((s, c, g)) - 1]
                                when_full(dve, e[0], e[1], "shift", e[2])
                            last = dve.tensor_reduce(dst, src, AX_X, ALU.max)
                            freed(last, *((s, c) + st))
                        elif st[0] == "divide":
                            src = when_full(dve, s, c, "divide", g).rearrange("p (t j e) -> p t j e", t=TT, j=4)
                            link(dve.reciprocal(rden[:], src[:, :, :, HD]))
                            dst = ATN[:, :, g * 64:(g + 1) * 64].rearrange("p t (j e) -> p t j e", j=4)
                            freed(dve.tensor_tensor(dst, src[:, :, :, 0:HD],
                                                    rden[:].unsqueeze(3).broadcast_to([P, TT, 4, HD]), ALU.mult),
                                  s, c, "divide", g)
                            read_out(dve, s, c, "divide", g)
                    if s == "E":
                        dve.wait_ge(biased.sem, biased.at("E", c))
                    for b in range(2):
                        src = when_full(dve, s, c, "proj", b).rearrange("p (t d) -> p t d", t=2)
                        acc = (X if s == "B" else XN)[:, c, 2 * b:2 * b + 2, :]
                        last = dve.tensor_tensor(acc, src, acc, ALU.add)
                        freed(last, s, c, "proj", b)

                def per_feature(s, after):
                    both_norms(s, after)
                    for c in seqs:
                        read_out(dve, "s", s, c)
                        for j in range(8):
                            last = dve.tensor_scalar(R[:, j, :], S[:, c, :], c_mw1[:, j:j + 1], c_mb1[:, j:j + 1],
                                                     ALU.mult, ALU.max)
                        link(last)
                        link(dve.tensor_scalar(G[:, c, :], R[:, 0, :], c_mw2[:, 0:1], c_mbias, ALU.mult, ALU.add))
                        for j in range(1, 8):
                            last = dve.scalar_tensor_tensor(G[:, c, :], R[:, j, :], c_mw2[:, j:j + 1], G[:, c, :],
                                                            ALU.mult, ALU.add)
                            if j < 7:
                                link(last)
                        last.then_inc(g_ready.sem, 1)
                        dve.wait_ge(g_ready.sem, g_ready.at(s, c))
                    for c in seqs:
                        dve.wait_ge(biased.sem, biased.at(s, c))
                        for b in range(2):
                            src = when_full(dve, "mout", s, c, b).rearrange("p (t d) -> p t d", t=2)
                            x = X[:, c, 2 * b:2 * b + 2, :]
                            last = dve.tensor_tensor(x, src, x, ALU.add)
                            freed(last, "mout", s, c, b)

                def outs(name, *rest):
                    return lambda c: [(name, *rest, c, b) for b in range(2)]

                dve.wait_ge(x_loaded, 16 * CH)
                coupled("A", lambda c: [])
                both_norms("B", outs("back", "A"))
                for c in seqs:
                    latent(c)
                    attention("B", c)
                coupled("C", lambda c: [("B", c, "proj", b) for b in range(2)])
                per_feature("D", outs("back", "C"))
                both_norms("E", outs("mout", "D"))
                for c in seqs:
                    attention("E", c)
                for c in seqs:
                    statistics("E2", c, XN[:, c], *[("E", c, "proj", b) for b in range(2)])
                for c in seqs:
                    normalize("E2", c, XN[:, c], XN[:, c])
                for c in seqs:
                    dve.wait_ge(biased.sem, biased.at("HB", c))
                    for b in range(2):
                        src = when_full(dve, "down", c, b).rearrange("p (t d) -> p t d", t=2)
                        acc = HB[:, c, 2 * b:2 * b + 2, :]
                        freed(dve.tensor_tensor(acc, src, acc, ALU.add), "down", c, b)
                    statistics("E3", c, HB[:, c], *[("down", c, b) for b in range(2)])
                for c in seqs:
                    normalize("E3", c, HB[:, c], HB[:, c])
                for c in seqs:
                    dve.wait_ge(biased.sem, biased.at("E3", c))
                    link(dve.tensor_tensor(X[:, c], X[:, c], HB[:, c], ALU.add))
                per_feature("F", lambda c: [])

            @block.scalar
            def _(act):
                def copied(s, c, gc=False):
                    for f in range(KT):
                        src = when_full(act, "xt", s, c, f)
                        if gc:
                            last = act.activation(XT[:, c, f, :], src, ACT.Copy, accum_out=means[:, c, f:f + 1])
                        elif s == "E2":
                            last = act.activation(XT[:, c, f, :], src, ACT.Identity, scale=c_gamma[:, f:f + 1],
                                                  bias=c_beta[:, f:f + 1])
                        else:
                            last = act.activation(XT[:, c, f, :], src, ACT.Copy)
                        freed(last, "xt", s, c, f)

                def coupled(s):
                    for c in seqs:
                        copied(s, c, gc=True)
                    for k in range(CYCLES):
                        for c in seqs:
                            for m in range(2):
                                src = when_full(act, "h1", s, k, c, m)
                                freed(act.activation(H1[:, c, m, :], src, ACT.Gelu, bias=c_b1[:, m:m + 1]),
                                      "h1", s, k, c, m)
                            if k == 0:
                                src = when_full(act, "gc", s, 0, c)
                                freed(act.activation(gc_h[:, c, 0:1], src[:, 0:1], ACT.Gelu, bias=c_g1, scale=1.0 / T),
                                      "gc", s, 0, c)
                        for c in seqs:
                            if k == 0:
                                src = when_full(act, "gc", s, 1, c)
                                freed(act.activation(gc_h[:, c, 1:2], src[:, 0:1], ACT.Gelu, bias=c_g2), "gc", s, 1, c)
                            src = when_full(act, "h2", s, k, c)
                            freed(act.activation(H2[:, c, :], src, ACT.Gelu, bias=c_b2), "h2", s, k, c)
                        for c in seqs:
                            if k == 0:
                                src = when_full(act, "gc", s, 2, c)
                                freed(act.activation(gc_h[:, c, 2:3], src[:, 0:1], ACT.Tanh, bias=c_half3, scale=0.5),
                                      "gc", s, 2, c)
                            src = when_full(act, "h3", s, k, c)
                            freed(act.activation(H3[:, c, :], src, ACT.Gelu, bias=c_b3), "h3", s, k, c)
                        for c in seqs:
                            src = when_full(act, "tf", s, k, c)
                            freed(act.activation(TF[:, c, :], src, ACT.Tanh, bias=c_half4, scale=0.5), "tf", s, k, c)

                def latent(c):
                    src = when_full(act, "kv", c)
                    freed(act.activation(XN[:, c, 0, :], src[:, 0:256], ACT.Copy), "kv", c)
                    src = when_full(act, "ql", c)
                    freed(act.activation(QL, src, ACT.Copy), "ql", c)
                    src = when_full(act, "kvt", c)
                    freed(act.activation(KVT[0:64, :], src[0:64, :], ACT.Copy), "kvt", c)
                    for b in range(2):
                        src = when_full(act, "v", "B", c, b).rearrange("p (t h d) -> p t h d", t=2, d=HD)
                        freed(act.activation(VB[:, 2 * b:2 * b + 2, :, 0:HD], src, ACT.Copy), "v", "B", c, b)

                def qkv(c):
                    src = when_full(act, "v", "E", c, 0)
                    at = 0
                    for st, heads, m in V_PARTS:
                        n, t = len(heads), e_tiles[heads[0]]
                        f0 = e_first[heads[0]]
                        dst = VE[0:m, f0:f0 + n * t, 0:HD].rearrange("p (h t) d -> p t h d", t=t)
                        a = src[0:m, at:at + n * t * HD].rearrange("p (t h d) -> p t h d", t=t, d=HD)
                        last = act.activation(dst, a, ACT.Copy)
                        at += n * t * HD
                    freed(last, "v", "E", c, 0)

                def attention(s, c):
                    _, tiles, _ = attention_shapes(s, T)
                    for st in STEPS[s]:
                        g = st[1]
                        r = g % 2
                        if st[0] == "content":
                            if c:
                                for b in range(2):
                                    act.wait_ge(stacked[b], stack_count[s, c - 1, GROUPS - 2 + b])
                            for x in range(2):
                                for w, dst in (("k", KC), ("q", QC)):
                                    src = when_full(act, "hi", s, c, w, x)
                                    if s == "B":
                                        last = act.activation(rounded(dst[:, x, 0, :]), src, ACT.Copy)
                                    else:
                                        for p, hi, _, bias in e_parts(src, w, x):
                                            last = act.activation(rounded(hi), p, ACT.Identity, bias=bias)
                                    last.then_inc(hi_ready.sem, 1)
                        elif st[0] == "place":
                            act.wait_ge(rope_hi.sem, rope_hi.at(c, g, "k"))
                            stack_free(act, s, c, g)
                            for j in range(4):
                                for m in range(2):
                                    last = act.activation(SK1[RD * m:RD * m + RD, r, j, :],
                                                          rounded(rope_parts("k")[1][RD * j:RD * j + RD, :]), ACT.Copy)
                            last.then_inc(placed_act.sem, 1)
                        elif st[0] == "shift":
                            src = when_full(act, s, c, "shift", g)
                            n = groups.index((s, c, g))
                            if n:
                                act.wait_ge(shift_in, 16 * n)
                            freed(act.activation(rounded(NM), src, ACT.Copy, scale=-1.0), s, c, "shift", g)
                        elif st[0] == "exp":
                            _, _, kt, pair = st
                            when_full(act, s, c, "exp", g, kt, pair)
                            q0 = kt * P if s == "B" else 0
                            b = 2 + 2 * pair
                            last_use(s, c, g, kt)
                            freed(act.activation(PR[:, kt % 2, 2 * pair:2 * pair + 2, q0:T], ps[:, b:b + 2, 0:T - q0],
                                                 ACT.Exp, scale=SCALE[s]), s, c, "exp", g, kt, pair)
                        elif st[0] == "sum" and st[2] == depth(s, g) - 1:
                            src = when_full(act, s, c, "sum", g)
                            n = groups.index((s, c, g))
                            if n:
                                e = groups[n - 1]
                                when_full(act, e[0], e[1], "divide", e[2])
                            freed(act.activation(AO, src, ACT.Copy), s, c, "sum", g)
                    for f in range(KT):
                        src = when_full(act, s, c, "att", f)
                        if s == "B":
                            last = act.activation(ATT[:, f, :], src, ACT.Copy)
                        else:
                            last = act.activation(ATT[:, f, :], src, ACT.Identity, bias=c_vb[:, f:f + 1])
                        freed(last, s, c, "att", f)

                def last_use(s, c, g, kt):
                    before = [e for e in sums[:sums.index((s, c, g, kt))] if e[3] % 2 == kt % 2]
                    if before:
                        e = before[-1]
                        if e in sum_done.events:
                            act.wait_ge(sum_done.sem, sum_done.at(*e))
                        else:
                            when_full(act, e[0], e[1], "sum", e[2])

                def per_feature(s):
                    for c in seqs:
                        copied(s, c)
                        src = when_full(act, "s", s, c)
                        freed(act.activation(S[:, c, :], src, ACT.Identity, bias=c_bin), "s", s, c)

                coupled("A")
                for c in seqs:
                    copied("B", c)
                for c in seqs:
                    latent(c)
                    attention("B", c)
                coupled("C")
                per_feature("D")
                for c in seqs:
                    copied("E", c)
                for c in seqs:
                    qkv(c)
                    attention("E", c)
                for c in seqs:
                    copied("E2", c)
                    for m in range(8):
                        src = when_full(act, "up", c, m)
                        if c:
                            when_full(act, "down", c - 1, 1)
                        freed(act.activation(U[:, m, :], src, ACT.Relu, bias=c_ub[:, m:m + 1]), "up", c, m)
                per_feature("F")

            @block.gpsimd
            def _(pool):
                def power(s, c):
                    pool.wait_ge(var_ready.sem, var_ready.at(s, c))
                    pool.tensor_tensor(rstd[:, c, :], var[:, c, :], neg_half[:], ALU.pow).then_inc(rstd_ready.sem, 1)

                def bcast(v):
                    return v.unsqueeze(1).broadcast_to([P, TT, C])

                psteps = [0]

                def link(ins_):
                    ins_.then_inc(pool_step, 1)
                    psteps[0] += 1
                    pool.wait_ge(pool_step, psteps[0])

                def coupled(s):
                    for c in seqs:
                        power(s, c)
                    for k in range(CYCLES):
                        for c in seqs:
                            pool.wait_ge(coupling_ready.sem, coupling_ready.at(s, k, c))
                            pool.tensor_tensor(MV[:, c, 1, :], TF[:, c, :], XT[:, c, 0, :],
                                               ALU.mult).then_inc(moved_pool.sem, 1)
                            pool.wait_ge(moved_pool.sem, moved_pool.at(s, k, c))
                            pool.wait_ge(first_moved.sem, first_moved.at(s, k, c))
                            pool.tensor_tensor(XT[:, c, 1, :], XT[:, c, 1, :], MV[:, c, 1, :],
                                               ALU.subtract).then_inc(second_moved.sem, 1)

                def per_feature(s):
                    for c in seqs:
                        power(s, c)
                    for c in seqs:
                        pool.wait_ge(xn_ready.sem, xn_ready.at(s, c))
                        pool.tensor_tensor(X[:, c], X[:, c], bcast(bout_d), ALU.add).then_inc(biased.sem, 1)

                coupled("A")
                for c in seqs:
                    power("B", c)
                for c in seqs:
                    power("KV", c)
                    for st in STEPS["B"]:
                        if st[0] == "rope":
                            g = st[1]
                            for w in "kq":
                                a, b = rope_parts(w)
                                for part in ("straight", "turned"):
                                    read_out(pool, "rope", c, g, w, part)
                                pool.tensor_tensor(a, a, b, ALU.add).then_inc(rope_sum.sem, 1)
                            for w in "kq":
                                a, b = rope_parts(w)
                                pool.wait_ge(rope_hi.sem, rope_hi.at(c, g, w))
                                pool.tensor_tensor(rounded(a), a, b, ALU.subtract).then_inc(rope_lo.sem, 1)
                coupled("C")
                per_feature("D")
                for c in seqs:
                    power("E", c)
                for c in seqs:
                    pool.wait_ge(xn_ready.sem, xn_ready.at("E", c))
                    for f in range(KT):
                        when_full(pool, "xt", "E", c, f)
                    pool.tensor_tensor(XN[:, c], XN[:, c], bcast(bout_e), ALU.add).then_inc(biased.sem, 1)
                for c in seqs:
                    power("E2", c)
                for c in seqs:
                    pool.wait_ge(xn_ready.sem, xn_ready.at("E2", c))
                    link(pool.tensor_tensor(HB[:, c], XN[:, c], bcast(gamma_r), ALU.mult))
                    pool.tensor_tensor(HB[:, c], HB[:, c], bcast(betab2_r), ALU.add).then_inc(biased.sem, 1)
                for c in seqs:
                    power("E3", c)
                for c in seqs:
                    pool.wait_ge(xn_ready.sem, xn_ready.at("E3", c))
                    link(pool.tensor_tensor(HB[:, c], HB[:, c], bcast(gamma_r), ALU.mult))
                    pool.tensor_tensor(HB[:, c], HB[:, c], bcast(beta_r), ALU.add).then_inc(biased.sem, 1)
                per_feature("F")

            @block.sync
            def _(sp):
                for c in seqs:
                    sp.dma_start(X[:, c], x_v[turn, c]).then_inc(x_loaded, 16)

                def raw(ap):
                    return ap.bitcast(F32)

                for s in "BE":
                    keys, tiles, first = attention_shapes(s, T)
                    for c in seqs:
                        for st in STEPS[s]:
                            g = st[1]
                            r = g % 2
                            if st[0] == "stack":
                                for x in range(2):
                                    for w in "kq":
                                        read_out(sp, "hi", s, c, w, x)
                                stack_free(sp, s, c, g)
                                for j in (0, 2):
                                    h = 4 * g + j
                                    a = HD * (h // 2)
                                    if s == "B":
                                        b = 2 * RD
                                        moves = [(SQ[b + HD * m:b + HD * m + HD, r, j:j + 2, :], QC[a:a + HD, :, m, :])
                                                 for m in range(2)]
                                        moves += [(SK1[b + HD * m:b + HD * m + HD, r, j:j + 2, :], KC[a:a + HD, :, 0, :])
                                                  for m in range(2)]
                                        moves += [(SK2[b:b + HD, r, j:j + 2, :], KC[a:a + HD, :, 1, :])]
                                    else:
                                        k0, n_k = KCOPY[STRIDES[h]], keys[h]
                                        cols_ = SKE[:, first[h] * P:(first[h] + 2 * tiles[h]) * P]
                                        moves = [(SQ[HD * m:HD * m + HD, r, j:j + 2, :], QE[a:a + HD, :, m % 2, :])
                                                 for m in range(3)]
                                        moves += [(cols_[HD * m:HD * m + HD].rearrange("p (x n) -> p x n", x=2)[:, :, 0:n_k],
                                                   KE[a:a + HD, :, m // 2, k0:k0 + n_k]) for m in range(3)]
                                    for dst, src in moves:
                                        sp.dma_start(raw(dst), src).then_inc(stacked[r], 16)
                            elif st[0] == "shift":
                                read_out(sp, s, c, "shift", g)
                                sp.dma_start(raw(SQ[SHIFT:SHIFT + 1, r, :, :]), NM[0:P:32, :]).then_inc(shift_in, 16)
                for c in seqs:
                    for b in range(2):
                        read_out(sp, "mout", "F", c, b)
                    sp.dma_start(o_v[turn, c], X[:, c]).then_inc(x_stored, 16)
                sp.wait_ge(x_stored, 16 * CH)

          nc.all_engine_barrier(sems_to_clear=range(cleared.num, last_sem.num + 1))


NAMES = ["L0_attn_x", "L0_attn_W_kv", "L0_attn_g_kv", "L0_attn_W_kdec", "L0_attn_W_vdec", "L0_attn_W_q",
         "L0_attn_W_qdec", "L0_attn_W_krope", "L0_attn_W_qrope", "L0_attn_W_o",
         "L0_ffn_cn_w1", "L0_ffn_cn_b1", "L0_ffn_cn_w2", "L0_ffn_cn_b2", "L0_ffn_cn_w3", "L0_ffn_cn_b3",
         "L0_ffn_cn_w4", "L0_ffn_cn_b4", "L0_ffn_gc_w1", "L0_ffn_gc_b1", "L0_ffn_gc_w2", "L0_ffn_gc_b2",
         "L0_ffn_gc_w3", "L0_ffn_gc_b3", "L0_ffn_adaptive_range",
         "L1_attn_Wqkv", "L1_attn_bqkv", "L1_attn_Wout", "L1_attn_bout", "L1_attn_gamma", "L1_attn_beta",
         "L1_attn_W1", "L1_attn_b1", "L1_attn_W2", "L1_attn_b2",
         "L1_ffn_Win", "L1_ffn_bin_", "L1_ffn_W1", "L1_ffn_b1", "L1_ffn_W2", "L1_ffn_b2", "L1_ffn_Wout",
         "L1_ffn_bout"]


def rope_tables(T):
    inv_freq = 1.0 / 10000.0 ** (np.arange(0, RD, 2, dtype=np.float32) / RD)
    angles = np.outer(np.arange(T, dtype=np.float32), inv_freq)
    cos, sin = np.cos(angles).T, np.sin(angles).T
    return (np.ascontiguousarray(np.tile(np.concatenate([cos, cos]), (P // RD, 1)), dtype=np.float32),
            np.ascontiguousarray(np.tile(np.concatenate([-sin, sin]), (P // RD, 1)), dtype=np.float32))


def kernel(**inputs):
    import concourse.bacc as bacc
    from concourse.bass_utils import run_bass_kernel_spmd

    nc = bacc.Bacc("TRN2", target_bir_lowering=False, num_devices=1)
    arrays = {name: np.ascontiguousarray(inputs[name]) for name in NAMES}
    B, T, C = arrays["L0_attn_x"].shape
    arrays["rope_cos"], arrays["rope_sin"] = rope_tables(T)
    ins = {name: nc.dram_tensor(f"in_{name}", a.shape, mybir.dt.from_np(a.dtype), kind="ExternalInput").ap()
           for name, a in arrays.items()}
    out = nc.dram_tensor("out", (B, T, C), F32, kind="ExternalOutput").ap()
    build(nc, ins, out)
    r = run_bass_kernel_spmd(nc, [{f"in_{name}": a for name, a in arrays.items()}], core_ids=[0])
    return r.results[0]["out"]
```

```python
from contextlib import ExitStack

import numpy as np

import concourse.bass as bass
from concourse import mybir

F32 = mybir.dt.float32
F32R = mybir.dt.float32r
BF16 = mybir.dt.bfloat16
ALU = mybir.AluOpType
ACT = mybir.ActivationFunctionType
AX_X = mybir.AxisListType.X

P = 128
CH = 2
ORDER = {"B": [(c, g) for c in range(2) for g in range(4)],
         "E": [(0, g) for g in (3, 2, 1, 0)] + [(1, g) for g in range(4)]}
CYCLES = 3
HEADS, HD, RD = 16, 16, 32
GROUPS = HEADS // 4
STRIDES = [1, 1, 2, 2, 2, 2, 4, 4, 4, 4, 8, 8, 8, 8, 16, 16]
HALVES_OVER = [(n + RD // 2) % RD for n in range(RD)]
LN_EPS = 1e-5
RMS_EPS = 1e-6
MASKED = -1.0e30


def attention_shapes(stage, T):
    keys = [T] * HEADS if stage == "B" else [T // s for s in STRIDES]
    tiles = [-(-k // P) for k in keys]
    first = [sum(tiles[:h]) for h in range(HEADS)]
    return keys, tiles, first


def max_jobs(stage, g, T):
    keys, _, _ = attention_shapes(stage, T)
    jobs = []
    if stage == "B":
        for t in range(T // P):
            n = P * (t + 1)
            m = min(4, 512 // n)
            m = 1 if m == 3 else m
            jobs += [([t], list(range(j, j + m)), n) for j in range(0, 4, m)]
        return jobs
    for pair in (0, 2):
        n = keys[4 * g + pair]
        if n == 512:
            jobs += [([t], [j], n) for t in range(T // P) for j in (pair, pair + 1)]
        else:
            m = min(T // P, 512 // (2 * n))
            jobs += [(list(range(t, t + m)), [pair, pair + 1], n) for t in range(0, T // P, m)]
    return jobs


def attention_steps(stage, T):
    order, ropes = ORDER[stage], stage == "B"
    _, tiles, _ = attention_shapes(stage, T)

    def maxima(n):
        return [("max", *order[n], m) for m in range(len(max_jobs(stage, order[n][1], T)))] + [("shift", *order[n])]

    def place(n, half):
        return [("place", *order[n], half)]

    content = [("content", 0, 0), ("content", 0, 1)]
    if ropes:
        steps = [("latent", 0), ("rope", *order[0]), ("kvt", 0), ("split", *order[0])] + content
        steps += place(0, 0) + place(0, 1) + [("stack", *order[0]), ("stack", *order[1]), ("v", 0)]
        steps += [("rope", *order[1]), ("split", *order[1])]
    else:
        steps = content + [("stack", *order[n]) for n in range(4)] + [("v", 0)]
    during = {n: [n + 1] for n in range(7)} if ropes else {0: [2], 1: [3], 3: [4, 5], 4: [6], 5: [7]}
    for n in range(8):
        if not any(n in ahead for ahead in during.values()):
            steps += maxima(n)
    for n, (c, g) in enumerate(order):
        exps = [(kt, pair) for kt in range(4) for pair in (0, 1) if kt < tiles[4 * g + 2 * pair]]
        extra = {i: [] for i in range(len(exps))}
        if ropes and n and n + 1 < len(order):
            steps.append(("stack", *order[n + 1]))
        if n:
            last = order[n - 1]
            extra[0].append(("sum", *last, max(tiles[4 * last[1]:4 * last[1] + 4]) - 1))
            extra[1].append(("divide", *last))
        if ropes and n + 1 < len(order):
            extra[0] += place(n + 1, 0)
            extra[1] += place(n + 1, 1)
        if n == 4:
            extra[0].append(("v", 1))
            extra[3].append(("att", 0))
            extra[4].append(("proj", 0))
        if n == 5 and not ropes:
            extra[0].append(("norm", 0))
        if ropes and n == 1:
            extra[5].append(("latent", 1))
        if ropes and n == 2:
            extra[0].append(("kvt", 1))
            extra[3].append(("content", 1, 0))
            extra[4].append(("content", 1, 1))
        if not ropes and n == 1:
            extra[1].append(("content", 1, 0))
        if not ropes and n == 2:
            extra[0] += [("content", 1, 1)] + [("stack", *order[m]) for m in range(4, 8)]
        for i in range(1, len(exps)):
            if exps[i][0] != exps[i - 1][0]:
                extra[i].append(("sum", c, g, exps[i - 1][0]))
        ahead = [step for m in during.get(n, []) for step in maxima(m)]
        where = range(len(exps))
        if not ropes and n == 3:
            where = range(2, 6)
        if ropes and ahead:
            shift = ahead.pop()
            where = range(2, 5)
        per = -(-len(ahead) // len(where))
        for i, at in enumerate(where):
            extra[at] += ahead[per * i:per * (i + 1)]
        if ropes and n + 2 < len(order):
            extra[4].append(("rope", *order[n + 2]))
            extra[6].append(("split", *order[n + 2]))
        if ropes and ahead:
            extra[5].append(shift)
        for i, (kt, pair) in enumerate(exps):
            steps += [("exp", c, g, kt, pair)] + extra[i]
    c, g = order[-1]
    return steps + [("sum", c, g, max(tiles[4 * g:4 * g + 4]) - 1), ("divide", c, g), ("att", 1), ("proj", 1)]


def build(nc, ins, out):
    x_in = ins["L0_attn_x"]
    B, T, C = x_in.shape
    TT, KT = T // P, C // P
    assert T == 512 and C == 256 and B % CH == 0
    TURNS = B // CH
    x_v = x_in.rearrange("(i c) (t p) d -> i c p t d", c=CH, p=P)
    o_v = out.rearrange("(i c) (t p) d -> i c p t d", c=CH, p=P)
    _, e_tiles, e_first = attention_shapes("E", T)
    E_SLOTS = sum(e_tiles)
    SCALE = {"B": float(1.0 / np.sqrt(np.float32(HD + RD))), "E": 1.0 / np.sqrt(HD)}
    STEPS = {s: attention_steps(s, T) for s in "BE"}
    KCOPY, width = {}, 0
    for s in sorted(set(STRIDES)):
        KCOPY[s] = width
        width += T // s
    KWIDE = width

    ctx = ExitStack()
    with ctx:
        def sb(name, shape, dt=F32):
            return ctx.enter_context(nc.sbuf_tensor(name, shape, dt))

        def sem(name):
            return ctx.enter_context(nc.semaphore(name))

        cn_w1 = sb("cn_w1", [P, 2, 256])
        cn_w2 = sb("cn_w2", [P, 2, 128])
        cn_w3 = sb("cn_w3", [P, 128])
        cn_w4 = sb("cn_w4", [P, 128])
        gc_w1 = sb("gc_w1", [P, 2, 128])
        gc_w2 = sb("gc_w2", [P, 128])
        gc_w3 = sb("gc_w3", [P, 128])
        cols = sb("cols", [P, 96])
        w_kv = sb("w_kv", [P, 2, 64])
        w_kdec = sb("w_kdec", [P, 256])
        w_vdec = sb("w_vdec", [P, 256])
        w_q = sb("w_q", [P, 2, 128])
        w_qdec = sb("w_qdec", [P, 256])
        w_qrope = sb("w_qrope", [P, 512])
        w_krope = sb("w_krope", [P, 2, 512])
        w_o = sb("w_o", [P, 2, 256])
        rope_cos = sb("rope_cos", [P, T])
        rope_sin = sb("rope_sin", [P, T])
        ident = sb("ident", [P, P])
        ident_b = sb("ident_b", [P, P], BF16)
        mask_q = sb("mask_q", [P, P], BF16)
        mask_k = sb("mask_k", [P, P], BF16)
        w_qkv = sb("w_qkv", [P, 2, 768])
        w_out = sb("w_out", [P, 2, 256])
        w_up = sb("w_up", [P, 2, 1024])
        w_down = sb("w_down", [P, 8, 256])
        rows = sb("rows", [P, 5, 256])
        bout_e, gamma_r, beta_r, betab2_r, bout_d = (rows[:, n, :] for n in range(5))
        m_in = sb("m_in", [P, 2, 128])
        m_out = sb("m_out", [P, 256])

        used = [0]

        def col(n=1):
            a = used[0]
            used[0] += n
            return cols[:, a:a + n]

        c_b1, c_b2, c_b3, c_b4 = col(2), col(), col(), col()
        c_g1, c_g2, c_g3 = col(), col(), col()
        c_half4, c_half3 = col(), col()
        c_w4, c_gw3, c_range, c_sign = col(), col(), col(), col()
        c_tf, c_gf, c_base = col(), col(), col()
        c_gkv = col()
        c_qkb, c_vb = col(4), col(2)
        c_gamma, c_beta, c_ub = col(2), col(2), col(8)
        c_bin = col()
        c_mw1, c_mb1, c_mw2 = col(8), col(8), col(8)
        c_mb2 = col()
        neg_half = sb("neg_half", [P, 4])

        X = sb("X", [P, CH, TT, C])
        XN = sb("XN", [P, CH, TT, C])
        XT = sb("XT", [P, CH, KT, T])
        stats = sb("stats", [P, CH, TT, 6])
        mv = sb("mv", [P, CH, TT, 2])
        var = sb("var", [P, CH, TT])
        rstd = sb("rstd", [P, CH, TT])
        scratch = sb("scratch", [P, 8192])
        H1 = scratch[:, 0:2048].rearrange("p (c m n) -> p c m n", c=CH, m=2)
        H2 = scratch[:, 2048:3072].rearrange("p (c n) -> p c n", c=CH)
        H3 = scratch[:, 3072:4096].rearrange("p (c n) -> p c n", c=CH)
        TF = scratch[:, 4096:5120].rearrange("p (c n) -> p c n", c=CH)
        ZT = scratch[:, 5120:7168].rearrange("p (c m n) -> p c m n", c=CH, m=2)
        WT = scratch[:, 7168:8192].rearrange("p (c n) -> p c n", c=CH)
        S = scratch[:, 0:1024].rearrange("p (c n) -> p c n", c=CH)
        G = scratch[:, 5120:6144].rearrange("p (c n) -> p c n", c=CH)
        QC = scratch[:, 0:2048].rearrange("p (x s n) -> p x s n", x=2, s=2)
        KC = scratch[:, 2048:4096].rearrange("p (x s n) -> p x s n", x=2, s=2)
        LT = scratch[:, 4096:4864].rearrange("p (m n) -> p m n", m=3)
        AO = scratch[:, 6144:6656]
        NM = scratch[:, 6656:7168]
        ATN = scratch[:, 7168:8192].rearrange("p (t d) -> p t d", t=TT)
        QE = scratch[:, 0:2048].rearrange("p (x s n) -> p x s n", x=2, s=2)
        KE = scratch[:, 2048:2048 + 4 * KWIDE].rearrange("p (x s n) -> p x s n", x=2, s=2)
        STACK = sb("STACK", [P, 6, 4, T], F32R)
        SQ, SK1, SK2 = (STACK[:, 2 * n:2 * n + 2] for n in range(3))
        SKE0 = sb("SKE", [P, E_SLOTS * P], F32R)
        SKE = [SKE0[:], SK2.rearrange("p r j n -> p (r j n)")[:, 0:E_SLOTS * P]]
        E_ROWS = (0, HD, 2 * RD)
        SHIFT = 96
        VB = sb("VB", [P, TT, HEADS, HD + 1])
        VE = sb("VE", [P, E_SLOTS, HD + 1])
        PR = sb("PR", [P, 2, 4, T])
        U = PR[:, :, :, :].rearrange("p a j n -> p (a j) n")
        R = [scratch[:, 1024:5120].rearrange("p (j n) -> p j n", j=8), U]
        MX = sb("MX", [P, TT, P])
        rden = sb("rden", [P, 4, 4])
        ATT = sb("ATT", [P, KT, T])
        QL, KVT = scratch[:, 4864:5376], scratch[:, 5376:5888]
        HB = scratch[:, 6144:8192].rearrange("p (c t d) -> p c t d", c=CH, t=TT)
        means = sb("means", [P, CH, KT])
        gc_h = sb("gc_h", [P, CH, 4])

        ps = ctx.enter_context(nc.psum_tensor("ps", [P, 8, 512], F32))

        loaded, const_pool, const_dve = sem("loaded"), sem("const_pool"), sem("const_dve")
        cleared = sem("x_loaded")
        x_loaded = cleared
        full = [sem(f"bank_full{b}") for b in range(8)]
        free = [sem(f"bank_free{b}") for b in range(8)]

        class Signal:

            def __init__(self, name, events):
                self.sem, self.events = sem(name), list(events)

            def at(self, *event):
                return self.events.index(event if len(event) > 1 else event[0]) + 1

        seqs = range(CH)
        norms = [(s, c) for s in ("A", "B") for c in seqs] + [("KV", c) for c in seqs] + \
                [(s, c) for s in ("C", "D", "E", "E2") for c in seqs] + [(s, c) for c in seqs for s in ("E3", "F")]
        var_ready = Signal("var_ready", norms)
        rstd_ready = Signal("rstd_ready", norms)
        xn_ready = Signal("xn_ready", [e for e in norms if e[0] != "E3"])
        cycles = [(s, k, c, v) for s in "AC" for k in range(CYCLES) for c in seqs for v in range(2)]
        first_moved = Signal("first_moved", cycles)
        second_moved = Signal("second_moved", cycles)
        contents = [(s, c, w, x) for s in "BE" for c in seqs for x in range(2) for w in "kq"]
        hi_ready = Signal("hi_ready", contents)
        ropes = [st[1:] for st in STEPS["B"] if st[0] == "rope"]
        halves = [(*e, w) for e in ropes for w in "kq"]
        rope_sines, rope_turned = Signal("rope_sines", halves), Signal("rope_turned", halves)
        rope_sum, rope_hi, rope_lo = (Signal(n, halves) for n in ("rope_sum", "rope_hi", "rope_lo"))
        places = [st[1:] for st in STEPS["B"] if st[0] == "place"]
        placed_act, placed_dve = Signal("placed_act", places), Signal("placed_dve", places)
        groups = [(s, c, g) for s in "BE" for c, g in ORDER[s]]
        SLOTS = {"B": 2, "E": 4}

        def slot(s, c, g):
            return ORDER[s].index((c, g)) % SLOTS[s]

        stacked = [sem(f"stacked{r}") for r in range(4)]
        stack_count, total = {}, [0] * 4
        for e in groups:
            total[slot(*e)] += 16 * 2 * (5 if e[0] == "B" else 6)
            stack_count[e] = total[slot(*e)]
        ones_back = sem("ones_back")
        shift_in = sem("shift_in")
        sums = [(s, *st[1:]) for s in "BE" for st in STEPS[s] if st[0] == "sum"]

        def depth(s, g):
            return max(attention_shapes(s, T)[1][4 * g:4 * g + 4])

        def last_exp(s, c, g):
            return [(s, c, "exp", g, *st[3:]) for st in STEPS[s] if st[0] == "exp" and st[1:3] == (c, g)][-1]

        def tile_of(s, c, g, kt):
            return sums.index((s, c, g, kt)) % 2

        def rounded(ap):
            return ap.bitcast(F32R)

        sum_done = Signal("sum_done", [e for e in sums if e[3] < depth(e[0], e[2]) - 1])
        biased = Signal("biased", [(s, c) for s in ("D", "E", "beta", "HB", "F") for c in seqs])
        inner_ready = Signal("inner_ready", [(s, c, j) for s in "DF" for c in seqs for j in range(8)])
        g_ready = Signal("g_ready", [(s, c) for s in "DF" for c in seqs])
        dve_step, pool_step = sem("dve_step"), sem("pool_step")
        x_stored = sem("x_stored")
        last_sem = x_stored
        V_PARTS = [(st, [h for h in range(HEADS) if STRIDES[h] == st], min(P, T // st)) for st in (1, 2, 4, 8, 16)]

        with nc.Block() as block:
            loads = []

            def two_tiles(name, dst):
                loads.append((dst, ins[name].rearrange("(k p) n -> p k n", p=P)))

            def column(name, dst, m=None):
                v = ins[name]
                loads.append((dst, v.rearrange("(m p) -> p m", m=m)))

            def by_parity(dst, src):
                for x in range(2):
                    loads.append((dst[:, x * P:(x + 1) * P].rearrange("p (d e) -> p d e", e=HD),
                                  src.rearrange("k (d x e) -> k x d e", x=2, e=HD)[:, x]))

            two_tiles("L0_ffn_cn_w1", cn_w1[:])
            two_tiles("L0_ffn_cn_w2", cn_w2[:])
            two_tiles("L0_ffn_gc_w1", gc_w1[:])
            for h in range(2):
                loads.append((cn_w3[:, 64 * h:64 * h + 64], ins["L0_ffn_cn_w3"]))
                loads.append((gc_w2[:, 64 * h:64 * h + 64], ins["L0_ffn_gc_w2"]))
                loads.append((c_b3[64 * h:64 * h + 64, :], ins["L0_ffn_cn_b3"].rearrange("(p m) -> p m", m=1)))
                loads.append((c_g2[64 * h:64 * h + 64, :], ins["L0_ffn_gc_b2"].rearrange("(p m) -> p m", m=1)))
                loads.append((c_bin[64 * h:64 * h + 64, :], ins["L1_ffn_bin_"].rearrange("(p m) -> p m", m=1)))
                loads.append((c_mw1[64 * h:64 * h + 64, :], ins["L1_ffn_W1"][:, 8 * h:8 * h + 8]))
                loads.append((c_mb1[64 * h:64 * h + 64, :], ins["L1_ffn_b1"][:, 8 * h:8 * h + 8]))
                loads.append((c_mw2[64 * h:64 * h + 64, :], ins["L1_ffn_W2"][:, 8 * h:8 * h + 8]))
                loads.append((m_in[:, :, 64 * h:64 * h + 64], ins["L1_ffn_Win"].rearrange("(k p) n -> p k n", p=P)))
                loads.append((m_out[64 * h:64 * h + 64, :], ins["L1_ffn_Wout"]))
            loads.append((c_mb2[0:64, :], ins["L1_ffn_b2"].rearrange("(p m) -> p m", m=1)))
            loads.append((c_w4[0:64, :], ins["L0_ffn_cn_w4"]))
            loads.append((c_gw3[0:64, :], ins["L0_ffn_gc_w3"]))
            loads.append((c_gkv[0:64, :], ins["L0_attn_g_kv"].rearrange("(p m) -> p m", m=1)))
            column("L0_ffn_cn_b1", c_b1, 2)
            column("L0_ffn_cn_b2", c_b2, 1)
            column("L0_ffn_gc_b1", c_g1, 1)
            loads.append((c_vb, ins["L1_attn_bqkv"][2 * C:3 * C].rearrange("(m p) -> p m", m=2)))
            for w in range(2):
                for d in range(HEADS // 2):
                    v = ins["L1_attn_bqkv"][w * C:(w + 1) * C].rearrange("(d x e) -> d e x", x=2, e=HD)
                    loads.append((c_qkb[HD * d:HD * d + HD, 2 * w:2 * w + 2], v[d]))
            column("L1_attn_gamma", c_gamma, 2)
            column("L1_attn_beta", c_beta, 2)
            column("L1_attn_b1", c_ub, 8)
            loads.append((c_b4, ins["L0_ffn_cn_b4"].partition_broadcast(P)))
            loads.append((c_g3, ins["L0_ffn_gc_b3"].partition_broadcast(P)))
            loads.append((c_range, ins["L0_ffn_adaptive_range"].partition_broadcast(P)))
            two_tiles("L0_attn_W_kv", w_kv[:])
            by_parity(w_kdec[0:64, :], ins["L0_attn_W_kdec"])
            loads.append((w_vdec[0:64, :], ins["L0_attn_W_vdec"]))
            two_tiles("L0_attn_W_q", w_q[:])
            by_parity(w_qdec[:], ins["L0_attn_W_qdec"])
            loads.append((w_qrope[:], ins["L0_attn_W_qrope"]))
            two_tiles("L0_attn_W_krope", w_krope[:])
            two_tiles("L0_attn_W_o", w_o[:])
            loads.append((rope_cos[:], ins["rope_cos"]))
            loads.append((rope_sin[:], ins["rope_sin"]))
            for f in range(KT):
                w = ins["L1_attn_Wqkv"][f * P:(f + 1) * P, :]
                for a in (0, C):
                    by_parity(w_qkv[:, f, a:a + C], w[:, a:a + C])
                loads.append((w_qkv[:, f, 2 * C:3 * C], w[:, 2 * C:3 * C]))
            two_tiles("L1_attn_Wout", w_out[:])
            two_tiles("L1_attn_W1", w_up[:])
            loads.append((w_down[:], ins["L1_attn_W2"].rearrange("(k p) n -> p k n", p=P)))
            loads.append((bout_e, ins["L1_attn_bout"].partition_broadcast(P)))
            loads.append((gamma_r, ins["L1_attn_gamma"].partition_broadcast(P)))
            loads.append((beta_r, ins["L1_attn_beta"].partition_broadcast(P)))
            loads.append((betab2_r, ins["L1_attn_b2"].partition_broadcast(P)))
            loads.append((bout_d, ins["L1_ffn_bout"].partition_broadcast(P)))
            ALL_LOADS = 16 * len(loads)

            @block.sync
            def _(sp):
                for dst, src in loads:
                    sp.dma_start(dst, src, allow_slow_non_contiguous=True).then_inc(loaded, 16)
                sp.wait_ge(loaded, ALL_LOADS)

            @block.gpsimd
            def _(pool):
                for m in (ident, ident_b, mask_q, mask_k):
                    pool.memset(m[:], 0.0).then_inc(const_pool, 1)
                pool.memset(neg_half[:], -0.5).then_inc(const_pool, 1)
                pool.wait_ge(const_pool, 5)
                for m in (ident, ident_b):
                    pool.affine_select(out=m[:], in_=m[:], compare_op=ALU.not_equal, fill=1.0, base=0,
                                       pattern=[[-1, P]], channel_multiplier=1).then_inc(const_pool, 1)
                pool.affine_select(out=mask_q[:], in_=mask_q[:], compare_op=ALU.is_ge, fill=MASKED, base=0,
                                   pattern=[[-1, P]], channel_multiplier=1).then_inc(const_pool, 1)
                pool.affine_select(out=mask_k[:], in_=mask_k[:], compare_op=ALU.is_ge, fill=MASKED, base=0,
                                   pattern=[[1, P]], channel_multiplier=-1).then_inc(const_pool, 1)
                pool.memset(VB[:], 1.0).then_inc(const_pool, 1)
                pool.memset(VE[:], 1.0).then_inc(const_pool, 1)
                pool.memset(MX[:], 0.0).then_inc(const_pool, 1)
                pool.memset(PR[:], 0.0).then_inc(const_pool, 1)
                pool.wait_ge(const_pool, 13)
                for h in range(HEADS):
                    n = T // STRIDES[h]
                    if n < P and STRIDES[h] != STRIDES[h - 1]:
                        heads = STRIDES.count(STRIDES[h])
                        for q in range(n, P, 32):
                            pool.memset(VE[q:q + 32, e_first[h]:e_first[h] + heads, :], 0.0).then_inc(const_pool, 1)

            @block.vector
            def _(dve):
                n = 0

                def then(ins_):
                    ins_.then_inc(const_dve, 1)
                    nonlocal n
                    n += 1

                then(dve.memset(STACK[:].bitcast(F32), 0.0))
                then(dve.memset(SKE0[:].bitcast(F32), 0.0))
                then(dve.memset(cn_w4[64:P, :], 0.0))
                then(dve.memset(gc_w3[64:P, :], 0.0))
                then(dve.memset(w_kdec[64:P, :], 0.0))
                then(dve.memset(w_vdec[64:P, :], 0.0))
                then(dve.memset(c_sign[0:64, :], 1.0))
                then(dve.memset(c_sign[64:P, :], -1.0))
                then(dve.memset(c_mb2[64:P, :], 0.0))
                then(dve.memset(cn_w4[0:64, :], 1.0))
                then(dve.memset(gc_w3[0:64, :], 1.0))
                then(dve.memset(ps[:, 6:8, :], 0.0))
                dve.wait_ge(const_dve, n)
                for m in (SK1, SK2):
                    then(dve.memset(m[SHIFT:SHIFT + 1].bitcast(F32), 1.0))
                then(dve.memset(SKE0[SHIFT:SHIFT + 1, :].bitcast(F32), 1.0))
                dve.wait_ge(loaded, ALL_LOADS)
                then(dve.tensor_scalar(cn_w4[0:64, :], cn_w4[0:64, :], c_w4[0:64, :], None, ALU.mult))
                then(dve.tensor_scalar(gc_w3[0:64, :], gc_w3[0:64, :], c_gw3[0:64, :], None, ALU.mult))
                then(dve.tensor_scalar(c_half4, c_b4, 0.5, None, ALU.mult))
                then(dve.tensor_scalar(c_half3, c_g3, 0.5, None, ALU.mult))
                then(dve.tensor_scalar(c_tf, c_sign, c_range, 0.3, ALU.mult, ALU.mult))
                then(dve.tensor_scalar(c_gf, c_sign, c_range, 0.7, ALU.mult, ALU.mult))
                then(dve.tensor_scalar(c_base, c_sign, 0.1, None, ALU.mult))
                then(dve.tensor_scalar(w_kdec[0:64, :], w_kdec[0:64, :], c_gkv[0:64, :], None, ALU.mult))
                then(dve.tensor_scalar(w_vdec[0:64, :], w_vdec[0:64, :], c_gkv[0:64, :], None, ALU.mult))
                then(dve.tensor_tensor(betab2_r, betab2_r, beta_r, ALU.add))
                then(dve.tensor_scalar(bout_d, bout_d, 0.5, None, ALU.mult))
                then(dve.tensor_scalar(m_out[:], m_out[:], 0.5, None, ALU.mult))

        J = {}

        def when_full(eng, *key):
            b, n = J[key]
            eng.wait_ge(full[b], n)
            return ps[:, b, :]

        def read_out(eng, *key):
            b, n = J[key]
            eng.wait_ge(free[b], n)

        def freed(ins_, *key):
            ins_.then_inc(free[J[key][0]], 1)

        def stack_free(eng, s, c, g):
            n = ORDER[s].index((c, g)) - SLOTS[s]
            if n >= 0:
                when_full(eng, *last_exp(s, *ORDER[s][n]))

        def rope_parts(w):
            both = XN[:, "kq".index(w)].rearrange("p (v u) d -> p v (u d)", v=2)
            return both[:, 0, :], both[:, 1, :]

        def e_parts(src, w, x):
            if w == "q":
                return [(src, QE[:, x, 0, :], QE[:, x, 1, :], c_qkb[:, x:x + 1])]
            return [(src[:, 0:T:st], KE[:, x, 0, a:a + T // st], KE[:, x, 1, a:a + T // st], c_qkb[:, 2 + x:3 + x])
                    for st, a in KCOPY.items()]

        with nc.Fori(0, TURNS) as turn:
            with nc.Block() as block:

                @block.tensor
                def _(pe):
                    count, last_job = [0] * 8, [None] * 8

                    def take(bank, *key, width=1):
                        for b in range(bank, bank + width):
                            if last_job[b] is not None and last_job[b] not in [last_job[x] for x in range(bank, b)]:
                                pe.wait_ge(free[last_job[b][0]], last_job[b][1])
                        count[bank] += 1
                        J[key] = (bank, count[bank])
                        for b in range(bank, bank + width):
                            last_job[b] = J[key]
                        return ps[:, bank, :] if width == 1 else ps[:, bank:bank + width, :]

                    def mm(dst, lhsT, rhs, start=True, stop=True):
                        return pe.matmul(dst, lhsT, rhs, start=start, stop=stop, skip_group_check=True)

                    def transposed(s, c, banks):
                        pe.wait_ge(xn_ready.sem, xn_ready.at(s, c))
                        for f in range(KT):
                            dst = take(banks[f], "xt", s, c, f)
                            for t in range(TT):
                                last = pe.transpose(dst[:, t * P:(t + 1) * P], XN[:, c, t, f * P:(f + 1) * P], ident[:])
                            last.then_inc(full[banks[f]], 1)

                    def in_xt(s, c):
                        for f in range(KT):
                            read_out(pe, "xt", s, c, f)

                    def product(bank, key, pairs, rows=P, cols_=T):
                        dst = take(bank, *key)
                        for n, (lhsT, rhs) in enumerate(pairs):
                            last = mm(dst[0:rows, 0:cols_], lhsT, rhs, n == 0, n == len(pairs) - 1)
                        last.then_inc(full[bank], 1)

                    def coupled(s):
                        for c in seqs:
                            transposed(s, c, (4 * c + 2, 4 * c + 3))
                        for k in range(CYCLES):
                            for c in seqs:
                                for v, f in [(v, f) for v in range(2) for f in range(KT)]:
                                    tok = slice(v * T // 2, (v + 1) * T // 2)
                                    if k == 0:
                                        read_out(pe, "xt", s, c, f)
                                    else:
                                        moved = (first_moved, second_moved)[f]
                                        pe.wait_ge(moved.sem, moved.at(s, k - 1, c, v))
                                    for m in range(2):
                                        dst = take(4 * c + m, "h1", s, k, c, m) if (v, f) == (0, 0) else \
                                            ps[:, 4 * c + m, :]
                                        last = mm(dst[:, tok], cn_w1[:, f, m * P:(m + 1) * P], XT[:, c, f, tok],
                                                  f == 0, f == KT - 1)
                                        if (v, f) == (1, KT - 1):
                                            last.then_inc(full[4 * c + m], 1)
                                if k == 0:
                                    product(4 * c + 3, ("gc", s, 0, c),
                                            [(gc_w1[:, f, :], means[:, c, f:f + 1]) for f in range(KT)], cols_=1)
                            for c in seqs:
                                if k == 0:
                                    read_out(pe, "gc", s, 0, c)
                                    product(4 * c + 3, ("gc", s, 1, c), [(gc_w2[:], gc_h[:, c, 0:1])], cols_=1)
                                for m in range(2):
                                    read_out(pe, "h1", s, k, c, m)
                                product(4 * c + 2, ("h2", s, k, c), [(cn_w2[:, f, :], H1[:, c, f, :]) for f in range(KT)])
                            for c in seqs:
                                if k == 0:
                                    read_out(pe, "gc", s, 1, c)
                                    product(4 * c + 3, ("gc", s, 2, c), [(gc_w3[:], gc_h[:, c, 1:2])], cols_=1)
                                read_out(pe, "h2", s, k, c)
                                product(4 * c, ("h3", s, k, c), [(cn_w3[:], H2[:, c, :])])
                            for c in seqs:
                                read_out(pe, "h3", s, k, c)
                                product(4 * c + 1, ("tf", s, k, c), [(cn_w4[:], H3[:, c, :])])
                        for c in seqs:
                            pe.wait_ge(first_moved.sem, first_moved.at(s, CYCLES - 1, c, 1))
                            pe.wait_ge(second_moved.sem, second_moved.at(s, CYCLES - 1, c, 1))
                            for b in range(2):
                                dst = take(4 * c + 2 + b, "back", s, c, b)
                                for n in range(4):
                                    t, f = 2 * b + n // 2, n % 2
                                    last = pe.transpose(dst[:, n * P:(n + 1) * P], XT[:, c, f, t * P:(t + 1) * P], ident[:])
                                last.then_inc(full[4 * c + 2 + b], 1)

                    def parity(w, x):
                        return w[:, x * P:(x + 1) * P]

                    ring = [0]

                    def side():
                        ring[0] = (ring[0] + 1) % 3
                        return (0, 1, 7)[ring[0]]

                    def causal(dst, mask):
                        return mm(dst, ident_b[:], mask[:], False, True)

                    def latent(c):
                        in_xt("B", c)
                        b = side()
                        dst = take(b, "kv", c)
                        for t in range(TT):
                            for f in range(KT):
                                last = mm(dst[:, 64 * t:64 * t + 64], XT[:, c, f, t * P:(t + 1) * P], w_kv[:, f, :],
                                          f == 0, f == KT - 1)
                        last.then_inc(full[b], 1)
                        product(side(), ("ql", c), [(w_q[:, f, :], XT[:, c, f, :]) for f in range(KT)])

                    def latent_turned(c):
                        pe.wait_ge(xn_ready.sem, xn_ready.at("KV", c))
                        b = side()
                        dst = take(b, "kvt", c)
                        for t in range(TT):
                            last = pe.transpose(dst[0:64, t * P:(t + 1) * P], LT[:, 2, 64 * t:64 * t + 64], ident[:])
                        last.then_inc(full[b], 1)

                    def content(s, c, x):
                        if s == "E":
                            in_xt("E", c)
                        else:
                            read_out(pe, "kvt", c)
                            read_out(pe, "ql", c)
                        for w in "kq":
                            if s == "B":
                                pairs = [(parity(w_kdec, x), KVT)] if w == "k" else [(parity(w_qdec, x), QL)]
                            else:
                                pairs = [(parity(w_qkv[:, f, C * "qk".index(w):C * "qk".index(w) + C], x),
                                          XT[:, c, f, :]) for f in range(KT)]
                            product(side(), ("hi", s, c, w, x), pairs)

                    def values(s, c):
                        if s == "B":
                            for n in range(2):
                                b = side()
                                dst = take(b, "v", s, c, n)
                                for m in range(2):
                                    t = 2 * n + m
                                    last = mm(dst[:, m * C:(m + 1) * C], KVT[:, t * P:(t + 1) * P], w_vdec[:])
                                last.then_inc(full[b], 1)
                            return
                        b = side()
                        dst = take(b, "v", s, c, 0)
                        at = 0
                        for st, heads, m in V_PARTS:
                            for t in range(e_tiles[heads[0]]):
                                for f in range(KT):
                                    tok = XT[:, c, f, t * P * st:t * P * st + m * st:st]
                                    last = mm(dst[0:m, at:at + HD * len(heads)], tok,
                                              w_qkv[:, f, 512 + HD * heads[0]:512 + HD * (heads[-1] + 1)],
                                              f == 0, f == KT - 1)
                                at += HD * len(heads)
                        last.then_inc(full[b], 1)

                    def maxima(s, c, g, m):
                        _, _, first = attention_shapes(s, T)
                        r = slot(s, c, g)
                        ts, hs, nk = max_jobs(s, g, T)[m]
                        if m == 0:
                            pe.wait_ge(stacked[r], stack_count[s, c, g])
                            if s == "B":
                                pe.wait_ge(placed_act.sem, placed_act.at(c, g, 1))
                                pe.wait_ge(placed_dve.sem, placed_dve.at(c, g, 1))
                        b = side()
                        dst = take(b, s, c, "max", g, m)
                        at = 0
                        for t in ts:
                            for j in hs:
                                a = first[4 * g + j] * P
                                k1 = SK1[0:SHIFT, r, j, 0:nk] if s == "B" else SKE[c][0:SHIFT, a:a + nk]
                                last = mm(dst[:, at:at + nk], STACK[0:SHIFT, r, j, t * P:(t + 1) * P], k1, True, s == "E")
                                if s == "B":
                                    last = causal(dst[:, at + t * P:at + nk], mask_q)
                                at += nk
                        last.then_inc(full[b], 1)

                    def exponents(s, c, g, kt, pair):
                        keys, _, first = attention_shapes(s, T)
                        r = slot(s, c, g)
                        if (kt, pair) == (0, 0):
                            pe.wait_ge(shift_in, 16 * (groups.index((s, c, g)) + 1))
                        q0 = kt * P if s == "B" else 0
                        b = 2 + 2 * pair
                        both = take(b, s, c, "exp", g, kt, pair, width=2)
                        for n in range(2):
                            j = 2 * pair + n
                            h = 4 * g + j
                            q = STACK[:, r, j, q0:T]
                            if s == "B":
                                dst = both[:, n, 0:T - q0]
                                mm(dst, SK1[0:SHIFT + 1, r, j, kt * P:(kt + 1) * P], q[0:SHIFT + 1], True, False)
                                mm(dst, SK2[0:SHIFT, r, j, kt * P:(kt + 1) * P], q[0:SHIFT], False, False)
                                last = causal(dst[:, 0:P], mask_k)
                            else:
                                a, m = (first[h] + kt) * P, min(P, keys[h])
                                last = mm(both[0:m, n, 0:T], SKE[c][0:SHIFT + 1, a:a + m], q[0:SHIFT + 1])
                        last.then_inc(full[b], 1)

                    def add_up(s, c, g, kt):
                        _, tiles, first = attention_shapes(s, T)
                        for pair in (0, 1):
                            if kt < tiles[4 * g + 2 * pair]:
                                read_out(pe, s, c, "exp", g, kt, pair)
                        for b in range(2 if s == "B" else 1):
                            read_out(pe, "v", s, c, b)
                        b = 6
                        dst = take(b, s, c, "sum", g) if kt == 0 else ps[:, b, :]
                        q0 = kt * P if s == "B" else 0
                        for j in range(4):
                            h = 4 * g + j
                            if kt < tiles[h]:
                                v = VB[:, kt, h, :] if s == "B" else VE[:, first[h] + kt, :]
                                last = mm(dst[32 * j:32 * j + HD + 1, q0:T], v, PR[:, tile_of(s, c, g, kt), j, q0:T],
                                          kt == 0, kt == tiles[h] - 1)
                        if kt == depth(s, g) - 1:
                            last.then_inc(full[b], 1)
                        else:
                            last.then_inc(sum_done.sem, 1)

                    def turned(b, key, src):
                        dst = take(b, *key)
                        for t in range(TT):
                            last = pe.transpose(dst[:, t * P:(t + 1) * P], src(t), ident[:])
                        last.then_inc(full[b], 1)

                    def attention(s):
                        for name, c, *rest in STEPS[s]:
                            if name == "latent":
                                latent(c)
                            elif name == "kvt":
                                latent_turned(c)
                            elif name == "content":
                                content(s, c, *rest)
                            elif name == "v":
                                values(s, c)
                            elif name == "rope":
                                g, = rest
                                a = slice(g * P, (g + 1) * P)
                                product(side(), ("rope", c, g, "k"),
                                        [(w_krope[:, f, a], XT[:, c, f, :]) for f in range(KT)])
                                read_out(pe, "ql", c)
                                product(side(), ("rope", c, g, "q"), [(w_qrope[:, a], QL)])
                            elif name == "max":
                                maxima(s, c, *rest)
                            elif name == "shift":
                                g, = rest
                                read_out(pe, s, c, "max", g, len(max_jobs(s, g, T)) - 1)
                                turned(side(), (s, c, "shift", g), lambda t: MX[:, t, :])
                            elif name == "exp":
                                exponents(s, c, *rest)
                            elif name == "sum":
                                add_up(s, c, *rest)
                            elif name == "divide":
                                g, = rest
                                read_out(pe, s, c, "sum", g)
                                turned(side(), (s, c, "divide", g), lambda t: AO[:, t * P:(t + 1) * P])
                            elif name == "att":
                                read_out(pe, s, c, "divide", [g for cc, g in ORDER[s] if cc == c][-1])
                                for f in range(KT):
                                    turned(side(), (s, c, "att", f), lambda t: ATN[:, t, f * P:(f + 1) * P])
                            elif name == "proj":
                                for f in range(KT):
                                    read_out(pe, s, c, "att", f)
                                w = w_o if s == "B" else w_out
                                for n in range(2):
                                    b = side()
                                    dst = take(b, s, c, "proj", n)
                                    for m in range(2):
                                        t = 2 * n + m
                                        for f in range(KT):
                                            last = mm(dst[:, m * C:(m + 1) * C], ATT[:, f, t * P:(t + 1) * P], w[:, f, :],
                                                      f == 0, f == KT - 1)
                                    last.then_inc(full[b], 1)

                    def features_in(s, c):
                        transposed(s, c, (0, 1))
                        in_xt(s, c)
                        product(2 + c, ("s", s, c), [(m_in[:, f, :], XT[:, c, f, :]) for f in range(KT)])

                    def features_out(s, c):
                        pe.wait_ge(g_ready.sem, g_ready.at(s, c))
                        for b in range(2):
                            dst = take(4 + 2 * c + b, "mout", s, c, b)
                            for n in range(2):
                                t = 2 * b + n
                                last = mm(dst[:, n * C:(n + 1) * C], G[:, c, t * P:(t + 1) * P], m_out[:])
                            last.then_inc(full[4 + 2 * c + b], 1)

                    def up(c):
                        transposed("E2", c, (0, 1))
                        in_xt("E2", c)
                        for m in range(8):
                            product(2 + m % 4, ("up", c, m), [(w_up[:, f, m * P:(m + 1) * P], XT[:, c, f, :]) for f in range(KT)])

                    def down(c):
                        for b in range(2):
                            dst = take(6 + b, "down", c, b)
                            for n in range(2):
                                t = 2 * b + n
                                for m in range(8):
                                    read_out(pe, "up", c, m)
                                    last = mm(dst[:, n * C:(n + 1) * C], U[:, m, t * P:(t + 1) * P], w_down[:, m, :],
                                              m == 0, m == 7)
                            last.then_inc(full[6 + b], 1)

                    coupled("A")
                    for c in seqs:
                        transposed("B", c, (0, 1))
                    attention("B")
                    coupled("C")
                    for c in seqs:
                        features_in("D", c)
                    for c in seqs:
                        features_out("D", c)
                    for c in seqs:
                        transposed("E", c, (0, 1))
                    attention("E")
                    up(0)
                    down(0)
                    up(1)
                    features_in("F", 0)
                    down(1)
                    features_out("F", 0)
                    features_in("F", 1)
                    features_out("F", 1)

                @block.vector
                def _(dve):
                    steps = [0]

                    def link(ins_):
                        ins_.then_inc(dve_step, 1)
                        steps[0] += 1
                        dve.wait_ge(dve_step, steps[0])

                    def statistics(s, c, src, *after):
                        for key in after:
                            read_out(dve, *key)
                        for t in range(TT):
                            last = dve.bn_stats(stats[:, c, t, :], src[:, t, :])
                        link(last)
                        averaged(s, c)

                    def averaged(s, c):
                        for t in range(TT):
                            last = dve.bn_aggr(mv[:, c, t, :], stats[:, c, t, :])
                        link(last)
                        dve.tensor_scalar(var[:, c, :], mv[:, c, :, 1], LN_EPS, None, ALU.add).then_inc(var_ready.sem, 1)

                    def normalize(s, c, src, dst):
                        dve.wait_ge(rstd_ready.sem, rstd_ready.at(s, c))
                        for t in range(TT):
                            last = dve.tensor_scalar(dst[:, t, :], src[:, t, :], mv[:, c, t, 0:1], rstd[:, c, t:t + 1],
                                                     ALU.subtract, ALU.mult)
                        last.then_inc(xn_ready.sem, 1)

                    def both_norms(s, before=None):
                        for c in seqs:
                            if before:
                                before(c)
                            if c:
                                normalize(s, 0, X[:, 0], XN[:, 0])
                            if (s, c) != ("C", 0):
                                statistics(s, c, X[:, c])
                        normalize(s, 1, X[:, 1], XN[:, 1])

                    def coupled(s):
                        for k in range(CYCLES):
                            for c in seqs:
                                if k == 0:
                                    read_out(dve, "gc", s, 2, c)
                                    link(dve.tensor_scalar(gc_h[:, c, 3:4], gc_h[:, c, 2:3], c_gf, c_base, ALU.mult, ALU.add))
                                if k:
                                    for ready in (first_moved, second_moved):
                                        dve.wait_ge(ready.sem, ready.at(s, k - 1, c, 1))
                                else:
                                    for f in range(KT):
                                        read_out(dve, "xt", s, c, f)
                                dve.scalar_tensor_tensor(ZT[:, c, 0, :], XT[:, c, 1, :], gc_h[:, c, 3:4], XT[:, c, 0, :],
                                                         ALU.mult, ALU.add)
                                link(dve.scalar_tensor_tensor(ZT[:, c, 1, :], XT[:, c, 0, :], gc_h[:, c, 3:4],
                                                              XT[:, c, 1, :], ALU.mult, ALU.subtract))
                            for c in seqs:
                                read_out(dve, "tf", s, k, c)
                                for v in range(2):
                                    tok = slice(v * T // 2, (v + 1) * T // 2)
                                    dve.scalar_tensor_tensor(WT[:, c, tok], TF[:, c, tok], c_tf, XT[:, c, 0, tok],
                                                             ALU.mult, ALU.mult)
                                    link(dve.scalar_tensor_tensor(TF[:, c, tok], TF[:, c, tok], c_tf,
                                                                  XT[:, c, 1, tok], ALU.mult, ALU.mult))
                                    dve.tensor_tensor(XT[:, c, 0, tok], ZT[:, c, 0, tok], TF[:, c, tok],
                                                      ALU.add).then_inc(first_moved.sem, 1)
                                    dve.scalar_tensor_tensor(XT[:, c, 1, tok], ZT[:, c, 1, tok], -1.0, WT[:, c, tok],
                                                             ALU.mult, ALU.subtract).then_inc(second_moved.sem, 1)

                    def came_back(s):
                        def add(c):
                            for b in range(2):
                                src = when_full(dve, "back", s, c, b)
                                x = X[:, c, 2 * b:2 * b + 2, :]
                                last = dve.scalar_tensor_tensor(x, src.rearrange("p (t d) -> p t d", t=2), 0.5, x,
                                                                ALU.mult, ALU.add)
                                freed(last, "back", s, c, b)
                            for b in range(2):
                                read_out(dve, "back", s, c, b)
                        return add

                    def latent(c):
                        read_out(dve, "kv", c)
                        kv, sq = LT[:, 0, :], LT[:, 1, :]
                        link(dve.tensor_tensor(sq, kv, kv, ALU.mult))
                        link(dve.tensor_reduce(var[:, c, :], sq.rearrange("p (t d) -> p t d", t=TT), AX_X, ALU.add))
                        dve.tensor_scalar(var[:, c, :], var[:, c, :], 1.0 / 64, RMS_EPS, ALU.mult,
                                          ALU.add).then_inc(var_ready.sem, 1)
                        dve.wait_ge(rstd_ready.sem, rstd_ready.at("KV", c))
                        for t in range(TT):
                            last = dve.tensor_scalar(LT[:, 2, 64 * t:64 * t + 64], kv[:, 64 * t:64 * t + 64], rstd[:, c, t:t + 1], None,
                                                     ALU.mult)
                        last.then_inc(xn_ready.sem, 1)
                        dve.wait_ge(xn_ready.sem, xn_ready.at("KV", c))

                    def second_parts(s, c, x):
                        for w, dst in (("k", KC), ("q", QC)):
                            src = when_full(dve, "hi", s, c, w, x)
                            dve.wait_ge(hi_ready.sem, hi_ready.at(s, c, w, x))
                            if s == "B":
                                last = dve.tensor_tensor(rounded(dst[:, x, 1, :]), src, dst[:, x, 0, :], ALU.subtract)
                            else:
                                for p, hi, lo, bias in e_parts(src, w, x):
                                    last = dve.scalar_tensor_tensor(rounded(lo), p, bias, hi, ALU.add, ALU.subtract)
                            freed(last, "hi", s, c, w, x)

                    def rotate(c, g):
                        n = ropes.index((c, g))
                        if n:
                            dve.wait_ge(placed_act.sem, placed_act.at(*places[2 * n - 1]))
                            dve.wait_ge(placed_dve.sem, placed_dve.at(*places[2 * n - 1]))
                        for w in "kq":
                            a, b = rope_parts(w)
                            src = when_full(dve, "rope", c, g, w)
                            dve.tensor_tensor(b, src, rope_sin[:], ALU.mult).then_inc(rope_sines.sem, 1)
                            freed(dve.tensor_tensor(a, src, rope_cos[:], ALU.mult), "rope", c, g, w)
                            dve.wait_ge(rope_sines.sem, rope_sines.at(c, g, w))
                            dve.stream_shuffle(out=b, in_=b, mask=HALVES_OVER).then_inc(rope_turned.sem, 1)

                    def split(c, g):
                        for w in "kq":
                            a, b = rope_parts(w)
                            dve.wait_ge(rope_sum.sem, rope_sum.at(c, g, w))
                            dve.tensor_copy(rounded(b), a).then_inc(rope_hi.sem, 1)

                    def place(c, g, half):
                        stack_free(dve, "B", c, g)
                        for w, m, dst, row in (("k", 1, SK1, RD), ("q", 1, SQ, 0), ("k", 0, SK2, 0), ("q", 0, SQ, RD)):
                            ready = (rope_lo, rope_hi)[m]
                            dve.wait_ge(ready.sem, ready.at(c, g, w))
                            for j in range(2 * half, 2 * half + 2):
                                last = dve.tensor_copy(dst[row:row + RD, slot("B", c, g), j, :],
                                                       rounded(rope_parts(w)[m][RD * j:RD * j + RD, :]))
                        last.then_inc(placed_dve.sem, 1)

                    def row_maxima(s, c, g, m):
                        ts, hs, nk = max_jobs(s, g, T)[m]
                        src = when_full(dve, s, c, "max", g, m)
                        src = src[:, 0:len(ts) * len(hs) * nk].rearrange("p (t h k) -> p t h k", t=len(ts), h=len(hs))
                        dst = MX[:, ts[0]:ts[-1] + 1, 32 * hs[0]:32 * hs[-1] + 1:32]
                        n = groups.index((s, c, g))
                        if m == 0 and n:
                            e = groups[n - 1]
                            when_full(dve, e[0], e[1], "shift", e[2])
                        freed(dve.tensor_reduce(dst, src, AX_X, ALU.max), s, c, "max", g, m)

                    def divided(s, c, g):
                        src = when_full(dve, s, c, "divide", g).rearrange("p (t j e) -> p t j e", t=TT, j=4)
                        link(dve.reciprocal(rden[:], src[:, :, :, HD]))
                        if c:
                            when_full(dve, s, c - 1, "att", KT - 1)
                        dst = ATN[:, :, g * 64:(g + 1) * 64].rearrange("p t (j e) -> p t j e", j=4)
                        freed(dve.tensor_tensor(dst, src[:, :, :, 0:HD],
                                                rden[:].unsqueeze(3).broadcast_to([P, TT, 4, HD]), ALU.mult),
                              s, c, "divide", g)
                        read_out(dve, s, c, "divide", g)

                    def projected(s, c):
                        if s == "E":
                            dve.wait_ge(biased.sem, biased.at("E", c))
                        for b in range(2):
                            src = when_full(dve, s, c, "proj", b).rearrange("p (t d) -> p t d", t=2)
                            acc = (X if s == "B" else XN)[:, c, 2 * b:2 * b + 2, :]
                            last = dve.tensor_tensor(acc, src, acc, ALU.add)
                            freed(last, s, c, "proj", b)
                        if s == "E":
                            statistics("E2", c, XN[:, c], *[(s, c, "proj", b) for b in range(2)])
                        elif c == 0:
                            statistics("C", c, X[:, c], *[(s, c, "proj", b) for b in range(2)])

                    def attention(s):
                        for name, c, *rest in STEPS[s]:
                            if name == "latent":
                                latent(c)
                            elif name == "content":
                                second_parts(s, c, *rest)
                            elif name == "rope":
                                rotate(c, *rest)
                            elif name == "split":
                                split(c, *rest)
                            elif name == "place":
                                place(c, *rest)
                            elif name == "max":
                                row_maxima(s, c, *rest)
                            elif name == "divide":
                                divided(s, c, *rest)
                            elif name == "proj":
                                projected(s, c)
                            elif name == "norm":
                                normalize("E2", c, XN[:, c], XN[:, c])

                    def inner_sum(s, c):
                        dve.wait_ge(inner_ready.sem, inner_ready.at(s, c, 0))
                        link(dve.tensor_scalar(G[:, c, :], R[c][:, 0, :], c_mw2[:, 0:1], c_mb2, ALU.mult, ALU.add))
                        for j in range(1, 8):
                            dve.wait_ge(inner_ready.sem, inner_ready.at(s, c, j))
                            last = dve.scalar_tensor_tensor(G[:, c, :], R[c][:, j, :], c_mw2[:, j:j + 1], G[:, c, :],
                                                            ALU.mult, ALU.add)
                            if j < 7:
                                link(last)
                        last.then_inc(g_ready.sem, 1)
                        dve.wait_ge(g_ready.sem, g_ready.at(s, c))

                    def features_added(s):
                        def add(c):
                            dve.wait_ge(biased.sem, biased.at(s, c))
                            for b in range(2):
                                src = when_full(dve, "mout", s, c, b).rearrange("p (t d) -> p t d", t=2)
                                x = X[:, c, 2 * b:2 * b + 2, :]
                                freed(dve.tensor_tensor(x, src, x, ALU.add), "mout", s, c, b)
                            for b in range(2):
                                read_out(dve, "mout", s, c, b)
                        return add

                    def feed_forward_end(c):
                        dve.wait_ge(biased.sem, biased.at("HB", c))
                        for b in range(2):
                            src = when_full(dve, "down", c, b).rearrange("p (t d) -> p t d", t=2)
                            acc = HB[:, c, 2 * b:2 * b + 2, :]
                            freed(dve.tensor_tensor(acc, src, acc, ALU.add), "down", c, b)
                            read_out(dve, "down", c, b)
                            for t in (2 * b, 2 * b + 1):
                                last = dve.bn_stats(stats[:, c, t, :], HB[:, c, t, :])
                        link(last)
                        averaged("E3", c)
                        for t in range(TT):
                            last = dve.scalar_tensor_tensor(HB[:, c, t, :], HB[:, c, t, :], mv[:, c, t, 0:1], gamma_r,
                                                            ALU.subtract, ALU.mult)
                        link(last)
                        dve.wait_ge(rstd_ready.sem, rstd_ready.at("E3", c))
                        for t in range(TT):
                            last = dve.scalar_tensor_tensor(X[:, c, t, :], HB[:, c, t, :], rstd[:, c, t:t + 1], X[:, c, t, :],
                                                            ALU.mult, ALU.add)
                        link(last)
                        statistics("F", c, X[:, c])
                        normalize("F", c, X[:, c], XN[:, c])

                    dve.wait_ge(x_loaded, 16 * CH)
                    both_norms("A")
                    coupled("A")
                    both_norms("B", came_back("A"))
                    attention("B")
                    both_norms("C", lambda c: [read_out(dve, "B", c, "proj", b) for b in range(2)])
                    coupled("C")
                    both_norms("D", came_back("C"))
                    for c in seqs:
                        inner_sum("D", c)
                    both_norms("E", features_added("D"))
                    attention("E")
                    normalize("E2", 1, XN[:, 1], XN[:, 1])
                    for c in seqs:
                        dve.wait_ge(biased.sem, biased.at("beta", c))
                    feed_forward_end(0)
                    inner_sum("F", 0)
                    feed_forward_end(1)
                    inner_sum("F", 1)
                    for c in seqs:
                        features_added("F")(c)

                @block.scalar
                def _(act):
                    def copied(s, c, gc=False):
                        for f in range(KT):
                            src = when_full(act, "xt", s, c, f)
                            if gc:
                                last = act.activation(XT[:, c, f, :], src, ACT.Copy, accum_out=means[:, c, f:f + 1])
                            elif s == "E2":
                                last = act.activation(XT[:, c, f, :], src, ACT.Identity, scale=c_gamma[:, f:f + 1],
                                                      bias=c_beta[:, f:f + 1])
                            else:
                                last = act.activation(XT[:, c, f, :], src, ACT.Copy)
                            freed(last, "xt", s, c, f)

                    def coupled(s):
                        for c in seqs:
                            copied(s, c, gc=True)
                        for k in range(CYCLES):
                            for c in seqs:
                                for m in range(2):
                                    src = when_full(act, "h1", s, k, c, m)
                                    freed(act.activation(H1[:, c, m, :], src, ACT.Gelu, bias=c_b1[:, m:m + 1]),
                                          "h1", s, k, c, m)
                                if k == 0:
                                    src = when_full(act, "gc", s, 0, c)
                                    freed(act.activation(gc_h[:, c, 0:1], src[:, 0:1], ACT.Gelu, bias=c_g1, scale=1.0 / T),
                                          "gc", s, 0, c)
                            for c in seqs:
                                if k == 0:
                                    src = when_full(act, "gc", s, 1, c)
                                    freed(act.activation(gc_h[:, c, 1:2], src[:, 0:1], ACT.Gelu, bias=c_g2), "gc", s, 1, c)
                                src = when_full(act, "h2", s, k, c)
                                freed(act.activation(H2[:, c, :], src, ACT.Gelu, bias=c_b2), "h2", s, k, c)
                            for c in seqs:
                                if k == 0:
                                    src = when_full(act, "gc", s, 2, c)
                                    freed(act.activation(gc_h[:, c, 2:3], src[:, 0:1], ACT.Tanh, bias=c_half3, scale=0.5),
                                          "gc", s, 2, c)
                                src = when_full(act, "h3", s, k, c)
                                freed(act.activation(H3[:, c, :], src, ACT.Gelu, bias=c_b3), "h3", s, k, c)
                            for c in seqs:
                                src = when_full(act, "tf", s, k, c)
                                freed(act.activation(TF[:, c, :], src, ACT.Tanh, bias=c_half4, scale=0.5), "tf", s, k, c)

                    def first_parts(s, c, x):
                        if c and x == 0:
                            for r in range(SLOTS[s]):
                                last = [e for e in groups if e[:2] == (s, c - 1) and slot(*e) == r][-1]
                                act.wait_ge(stacked[r], stack_count[last])
                        for w, dst in (("k", KC), ("q", QC)):
                            src = when_full(act, "hi", s, c, w, x)
                            if s == "B":
                                last = act.activation(rounded(dst[:, x, 0, :]), src, ACT.Copy)
                            else:
                                for p, hi, _, bias in e_parts(src, w, x):
                                    last = act.activation(rounded(hi), p, ACT.Identity, bias=bias)
                            last.then_inc(hi_ready.sem, 1)

                    def values(s, c):
                        if s == "B":
                            for b in range(2):
                                src = when_full(act, "v", s, c, b).rearrange("p (t h d) -> p t h d", t=2, d=HD)
                                freed(act.activation(VB[:, 2 * b:2 * b + 2, :, 0:HD], src, ACT.Copy), "v", s, c, b)
                            return
                        src = when_full(act, "v", s, c, 0)
                        at = 0
                        for st, heads, m in V_PARTS:
                            n, t = len(heads), e_tiles[heads[0]]
                            f0 = e_first[heads[0]]
                            dst = VE[0:m, f0:f0 + n * t, 0:HD].rearrange("p (h t) d -> p t h d", t=t)
                            a = src[0:m, at:at + n * t * HD].rearrange("p (t h d) -> p t h d", t=t, d=HD)
                            last = act.activation(dst, a, ACT.Copy)
                            at += n * t * HD
                        freed(last, "v", s, c, 0)

                    def place(c, g, half):
                        stack_free(act, "B", c, g)
                        act.wait_ge(rope_hi.sem, rope_hi.at(c, g, "k"))
                        for j in range(2 * half, 2 * half + 2):
                            last = act.activation(SK1[0:RD, slot("B", c, g), j, :],
                                                  rounded(rope_parts("k")[1][RD * j:RD * j + RD, :]), ACT.Copy)
                        last.then_inc(placed_act.sem, 1)

                    def exponents(s, c, g, kt, pair):
                        when_full(act, s, c, "exp", g, kt, pair)
                        q0, m = (kt * P, P) if s == "B" else (0, min(P, attention_shapes(s, T)[0][4 * g + 2 * pair]))
                        n = sums.index((s, c, g, kt)) - 2
                        if n >= 0:
                            e = sums[n]
                            if e in sum_done.events:
                                act.wait_ge(sum_done.sem, sum_done.at(*e))
                            else:
                                when_full(act, e[0], e[1], "sum", e[2])
                        b = 2 + 2 * pair
                        freed(act.activation(PR[0:m, tile_of(s, c, g, kt), 2 * pair:2 * pair + 2, q0:T],
                                             ps[0:m, b:b + 2, 0:T - q0], ACT.Exp, scale=SCALE[s]),
                              s, c, "exp", g, kt, pair)

                    def attention(s):
                        for name, c, *rest in STEPS[s]:
                            if name == "latent":
                                src = when_full(act, "kv", c)
                                freed(act.activation(LT[:, 0, :], src[:, 0:256], ACT.Copy), "kv", c)
                                if c:
                                    when_full(act, "rope", c - 1, GROUPS - 1, "q")
                                src = when_full(act, "ql", c)
                                freed(act.activation(QL, src, ACT.Copy), "ql", c)
                            elif name == "kvt":
                                src = when_full(act, "kvt", c)
                                freed(act.activation(KVT[0:64, :], src[0:64, :], ACT.Copy), "kvt", c)
                            elif name == "content":
                                first_parts(s, c, *rest)
                            elif name == "v":
                                values(s, c)
                            elif name == "place":
                                place(c, *rest)
                            elif name == "shift":
                                g, = rest
                                src = when_full(act, s, c, "shift", g)
                                n = groups.index((s, c, g))
                                if n:
                                    act.wait_ge(shift_in, 16 * n)
                                freed(act.activation(rounded(NM), src, ACT.Copy, scale=-1.0), s, c, "shift", g)
                                read_out(act, s, c, "shift", g)
                                act.dma_start(STACK[SHIFT:SHIFT + 1, slot(s, c, g), :, :].bitcast(F32),
                                              NM[0:P:32, :]).then_inc(shift_in, 16)
                            elif name == "exp":
                                exponents(s, c, *rest)
                            elif name == "sum" and rest[1] == depth(s, rest[0]) - 1:
                                src = when_full(act, s, c, "sum", rest[0])
                                n = groups.index((s, c, rest[0]))
                                if n:
                                    e = groups[n - 1]
                                    when_full(act, e[0], e[1], "divide", e[2])
                                freed(act.activation(AO, src, ACT.Copy), s, c, "sum", rest[0])
                            elif name == "att":
                                if c:
                                    when_full(act, s, c - 1, "proj", 1)
                                for f in range(KT):
                                    src = when_full(act, s, c, "att", f)
                                    if s == "B":
                                        last = act.activation(ATT[:, f, :], src, ACT.Copy)
                                    else:
                                        last = act.activation(ATT[:, f, :], src, ACT.Identity, bias=c_vb[:, f:f + 1])
                                    freed(last, s, c, "att", f)

                    def features_in(s, c):
                        copied(s, c)
                        src = when_full(act, "s", s, c)
                        freed(act.activation(S[:, c, :], src, ACT.Identity, bias=c_bin), "s", s, c)

                    def inner(s, c):
                        read_out(act, "s", s, c)
                        for j in range(8):
                            act.activation(R[c][:, j, :], S[:, c, :], ACT.Relu, scale=c_mw1[:, j:j + 1],
                                           bias=c_mb1[:, j:j + 1]).then_inc(inner_ready.sem, 1)

                    def up(c):
                        copied("E2", c)
                        for m in range(8):
                            src = when_full(act, "up", c, m)
                            if c:
                                when_full(act, "down", c - 1, 1)
                            freed(act.activation(U[:, m, :], src, ACT.Relu, bias=c_ub[:, m:m + 1]), "up", c, m)

                    coupled("A")
                    for c in seqs:
                        copied("B", c)
                    attention("B")
                    coupled("C")
                    for c in seqs:
                        features_in("D", c)
                    for c in seqs:
                        inner("D", c)
                    for c in seqs:
                        copied("E", c)
                    attention("E")
                    for c in seqs:
                        up(c)
                        if c == 0:
                            continue
                        features_in("F", 0)
                        inner("F", 0)
                    features_in("F", 1)
                    inner("F", 1)

                @block.gpsimd
                def _(pool):
                    def power(s, c):
                        pool.wait_ge(var_ready.sem, var_ready.at(s, c))
                        pool.tensor_tensor(rstd[:, c, :], var[:, c, :], neg_half[:], ALU.pow).then_inc(rstd_ready.sem, 1)

                    def bcast(v):
                        return v.unsqueeze(1).broadcast_to([P, TT, C])

                    psteps = [0]

                    def link(ins_):
                        ins_.then_inc(pool_step, 1)
                        psteps[0] += 1
                        pool.wait_ge(pool_step, psteps[0])

                    def output_bias(s, c):
                        pool.wait_ge(xn_ready.sem, xn_ready.at(s, c))
                        pool.tensor_tensor(X[:, c], X[:, c], bcast(bout_d), ALU.add).then_inc(biased.sem, 1)

                    for s in "AB":
                        for c in seqs:
                            power(s, c)
                    for name, c, *rest in STEPS["B"]:
                        if name == "latent":
                            power("KV", c)
                        elif name == "rope":
                            g, = rest
                            for w in "kq":
                                a, b = rope_parts(w)
                                read_out(pool, "rope", c, g, w)
                                pool.wait_ge(rope_turned.sem, rope_turned.at(c, g, w))
                                pool.tensor_tensor(a, a, b, ALU.add).then_inc(rope_sum.sem, 1)
                        elif name == "split":
                            for w in "kq":
                                a, b = rope_parts(w)
                                pool.wait_ge(rope_hi.sem, rope_hi.at(c, *rest, w))
                                pool.tensor_tensor(rounded(a), a, b, ALU.subtract).then_inc(rope_lo.sem, 1)
                    for s in "CD":
                        for c in seqs:
                            power(s, c)
                    for c in seqs:
                        output_bias("D", c)
                    for c in seqs:
                        power("E", c)
                    for c in seqs:
                        pool.wait_ge(xn_ready.sem, xn_ready.at("E", c))
                        for f in range(KT):
                            when_full(pool, "xt", "E", c, f)
                        pool.tensor_tensor(XN[:, c], XN[:, c], bcast(bout_e), ALU.add).then_inc(biased.sem, 1)
                    for c in seqs:
                        pool.tensor_tensor(X[:, c], X[:, c], bcast(beta_r), ALU.add).then_inc(biased.sem, 1)
                    power("E2", 0)
                    when_full(pool, *last_exp("E", *ORDER["E"][-1]))
                    pool.wait_ge(biased.sem, biased.at("beta", CH - 1))
                    pool.memset(SK1[SHIFT:SHIFT + 1].bitcast(F32), 1.0).then_inc(ones_back, 1)
                    pool.wait_ge(ones_back, 1)
                    when_full(pool, "E", 1, "att", KT - 1)
                    for c in seqs:
                        if c:
                            power("E2", c)
                        pool.wait_ge(xn_ready.sem, xn_ready.at("E2", c))
                        link(pool.tensor_tensor(HB[:, c], XN[:, c], bcast(gamma_r), ALU.mult))
                        pool.tensor_tensor(HB[:, c], HB[:, c], bcast(betab2_r), ALU.add).then_inc(biased.sem, 1)
                    for c in seqs:
                        power("E3", c)
                        power("F", c)
                        output_bias("F", c)

                @block.sync
                def _(sp):
                    for c in seqs:
                        sp.dma_start(X[:, c], x_v[turn, c]).then_inc(x_loaded, 16)

                    def raw(ap):
                        return ap.bitcast(F32)

                    def stack(s, c, g):
                        keys, tiles, first = attention_shapes(s, T)
                        r = slot(s, c, g)
                        for x in range(2):
                            for w in "kq":
                                read_out(sp, "hi", s, c, w, x)
                        stack_free(sp, s, c, g)
                        for j in (0, 2):
                            h = 4 * g + j
                            a = HD * (h // 2)
                            if s == "B":
                                b = 2 * RD
                                moves = [(SQ[b + HD * m:b + HD * m + HD, r, j:j + 2, :], QC[a:a + HD, :, m, :])
                                         for m in range(2)]
                                moves += [(SK1[b + HD * m:b + HD * m + HD, r, j:j + 2, :], KC[a:a + HD, :, 0, :])
                                          for m in range(2)]
                                moves += [(SK2[b:b + HD, r, j:j + 2, :], KC[a:a + HD, :, 1, :])]
                            else:
                                k0, n_k = KCOPY[STRIDES[h]], keys[h]
                                stacks = SKE[c][:, first[h] * P:(first[h] + 2 * tiles[h]) * P]
                                moves = []
                                for m, row in enumerate(E_ROWS):
                                    moves += [(STACK[row:row + HD, r, j:j + 2, :], QE[a:a + HD, :, m % 2, :]),
                                              (stacks[row:row + HD].rearrange("p (x n) -> p x n", x=2)[:, :, 0:n_k],
                                               KE[a:a + HD, :, m // 2, k0:k0 + n_k])]
                            for dst, src in moves:
                                sp.dma_start(raw(dst), src).then_inc(stacked[r], 16)

                    for s in "BE":
                        for name, c, *rest in STEPS[s]:
                            if name == "stack":
                                stack(s, c, *rest)
                    for c in seqs:
                        for b in range(2):
                            read_out(sp, "mout", "F", c, b)
                        sp.dma_start(o_v[turn, c], X[:, c]).then_inc(x_stored, 16)
                    sp.wait_ge(x_stored, 16 * CH)

            nc.all_engine_barrier(sems_to_clear=range(cleared.num, last_sem.num + 1))


NAMES = ["L0_attn_x", "L0_attn_W_kv", "L0_attn_g_kv", "L0_attn_W_kdec", "L0_attn_W_vdec", "L0_attn_W_q",
         "L0_attn_W_qdec", "L0_attn_W_krope", "L0_attn_W_qrope", "L0_attn_W_o",
         "L0_ffn_cn_w1", "L0_ffn_cn_b1", "L0_ffn_cn_w2", "L0_ffn_cn_b2", "L0_ffn_cn_w3", "L0_ffn_cn_b3",
         "L0_ffn_cn_w4", "L0_ffn_cn_b4", "L0_ffn_gc_w1", "L0_ffn_gc_b1", "L0_ffn_gc_w2", "L0_ffn_gc_b2",
         "L0_ffn_gc_w3", "L0_ffn_gc_b3", "L0_ffn_adaptive_range",
         "L1_attn_Wqkv", "L1_attn_bqkv", "L1_attn_Wout", "L1_attn_bout", "L1_attn_gamma", "L1_attn_beta",
         "L1_attn_W1", "L1_attn_b1", "L1_attn_W2", "L1_attn_b2",
         "L1_ffn_Win", "L1_ffn_bin_", "L1_ffn_W1", "L1_ffn_b1", "L1_ffn_W2", "L1_ffn_b2", "L1_ffn_Wout",
         "L1_ffn_bout"]


def rope_tables(T):
    inv_freq = 1.0 / 10000.0 ** (np.arange(0, RD, 2, dtype=np.float32) / RD)
    angles = np.outer(np.arange(T, dtype=np.float32), inv_freq)
    cos, sin = np.cos(angles).T, np.sin(angles).T
    return (np.ascontiguousarray(np.tile(np.concatenate([cos, cos]), (P // RD, 1)), dtype=np.float32),
            np.ascontiguousarray(np.tile(np.concatenate([sin, -sin]), (P // RD, 1)), dtype=np.float32))


def kernel(**inputs):
    import concourse.bacc as bacc
    from concourse.bass_utils import run_bass_kernel_spmd

    nc = bacc.Bacc("TRN2", target_bir_lowering=False, num_devices=1)
    arrays = {name: np.ascontiguousarray(inputs[name]) for name in NAMES}
    B, T, C = arrays["L0_attn_x"].shape
    arrays["rope_cos"], arrays["rope_sin"] = rope_tables(T)
    ins = {name: nc.dram_tensor(f"in_{name}", a.shape, mybir.dt.from_np(a.dtype), kind="ExternalInput").ap()
           for name, a in arrays.items()}
    out = nc.dram_tensor("out", (B, T, C), F32, kind="ExternalOutput").ap()
    build(nc, ins, out)
    r = run_bass_kernel_spmd(nc, [{f"in_{name}": a for name, a in arrays.items()}], core_ids=[0])
    return r.results[0]["out"]
```
